# Optimizing a Trainium2 kernel written in Bass

```python
import numpy as np
import jax
import jax.numpy as jnp

def _softmax(x, axis=-1):
    return jax.nn.softmax(x, axis=axis)

def _gelu(x):
    return jax.nn.gelu(x, approximate=True)

def _silu(x):
    return jax.nn.silu(x)

def _sigmoid(x):
    return jax.nn.sigmoid(x)

def _layernorm(x, axis=-1, eps=1e-05):
    m = jnp.mean(x, axis=axis, keepdims=True)
    v = jnp.var(x, axis=axis, keepdims=True)
    return (x - m) / jnp.sqrt(v + eps)

def _scatter_add(tgt, idx, src, axis=0):
    return tgt.at[idx].add(src)

def _segment_sum(src, seg, n):
    return jax.ops.segment_sum(src, seg, n)
kernel_name = 'mk_vit_tower_d2_tok_img1024_r4_0065df'

def setup_inputs(seed: int=0):
    np.random.seed(seed)
    _w = jnp.asarray

    def _rec_inputs():
        import jax
        import jax.numpy as jnp
        _rk = jax.random.key(seed)
        x = -0.00016672 + 0.999947 * jax.random.normal(jax.random.fold_in(_rk, 1), (32, 3, 96, 96), jnp.float32)
        return x
    x = _rec_inputs()

    def _L0_tok_setup():
        import jax, jax.numpy as jnp
        import numpy as np
        PATCH = 16

        def _patchify(x, p):
            B, C, H, W = x.shape
            nh, nw = (H // p, W // p)
            x = x.reshape(B, C, nh, p, nw, p)
            x = x.transpose(0, 2, 4, 1, 3, 5)
            return x.reshape(B, nh * nw, C * p * p)
        key = jax.random.key(seed)
        k1, k2, k3, k4, k5 = jax.random.split(key, 5)
        B, C, H = (64, 3, 96)
        d_model = 256
        p = PATCH
        num_patches = (H // p) ** 2
        in_dim = p * p * C
        x = jax.random.normal(k1, (B, C, H, H), dtype=jnp.float32)
        bound = 1.0 / np.sqrt(in_dim)
        W = jax.random.uniform(k2, (d_model, in_dim), dtype=jnp.float32, minval=-bound, maxval=bound)
        b = jax.random.uniform(k3, (d_model,), dtype=jnp.float32, minval=-bound, maxval=bound)
        cls_token = jax.random.normal(k4, (1, 1, d_model), dtype=jnp.float32)
        pos_enc = jax.random.normal(k5, (1, num_patches + 1, d_model), dtype=jnp.float32)
        return {'x': x, 'W': W, 'b': b, 'cls_token': cls_token, 'pos_enc': pos_enc}
    _L0_tok_all = _L0_tok_setup()
    _L0_tok_in = {k: v for k, v in _L0_tok_all.items() if k in ('W', 'b', 'cls_token', 'pos_enc')}
    del _L0_tok_all

    def _L0_attn_setup():
        import jax, jax.numpy as jnp
        import numpy as np
        D_MODEL = 256
        N_HEADS = 16
        D_K = D_MODEL // N_HEADS
        THETA = 10000.0
        BATCH = 1
        SEQ = 1024

        def _rope(x, pos, inv_freq):
            angles = pos[:, None].astype(jnp.float32) * inv_freq
            cos = jnp.repeat(jnp.cos(angles), 2, axis=-1)
            sin = jnp.repeat(jnp.sin(angles), 2, axis=-1)
            x_rot = jnp.stack([-x[..., 1::2], x[..., 0::2]], axis=-1).reshape(x.shape)
            return x * cos + x_rot * sin
        key = jax.random.key(seed)
        ks = jax.random.split(key, 5)
        std = (2.0 / (D_MODEL + D_MODEL)) ** 0.5
        mk = lambda k: jax.random.truncated_normal(k, -3.0, 3.0, (D_MODEL, D_MODEL), jnp.float32) * std
        return {'x': jax.random.normal(ks[0], (BATCH, SEQ, D_MODEL), jnp.float32), 'Wq': mk(ks[1]), 'Wk': mk(ks[2]), 'Wv': mk(ks[3]), 'Wo': mk(ks[4])}
    _L0_attn_all = _L0_attn_setup()
    _L0_attn_in = {k: v for k, v in _L0_attn_all.items() if k in ('Wq', 'Wk', 'Wv', 'Wo')}
    del _L0_attn_all

    def _L0_ffn_setup():
        import jax, jax.numpy as jnp
        import numpy as np
        D_MODEL = 256
        D_FF = 512
        N_EXPERTS = 8
        TOP_K = 2
        CLAMP = 10000.0
        ROUTER_EPS = 1e-08
        LN_EPS = 1e-05

        def _layernorm(x, g, b):
            mu = jnp.mean(x, axis=-1, keepdims=True)
            var = jnp.mean(jnp.square(x - mu), axis=-1, keepdims=True)
            return (x - mu) * jax.lax.rsqrt(var + LN_EPS) * g + b
        key = jax.random.key(seed)
        k1, k2, k3, k4 = jax.random.split(key, 4)
        B, S = (8, 256)
        x = jax.random.normal(k1, (B, S, D_MODEL), dtype=jnp.float32)
        ln_gamma = jnp.ones((D_MODEL,), jnp.float32)
        ln_beta = jnp.zeros((D_MODEL,), jnp.float32)
        bound = 0.02 * float(np.sqrt(3.0))
        router_w = jax.random.uniform(k2, (N_EXPERTS, D_MODEL), jnp.float32, -bound, bound)
        gate_up_w = jax.random.normal(k3, (N_EXPERTS, 2 * D_FF, D_MODEL), jnp.float32) * (1.0 / np.sqrt(D_MODEL))
        down_w = jax.random.normal(k4, (N_EXPERTS, D_MODEL, D_FF), jnp.float32) * (1.0 / np.sqrt(D_FF))
        return {'x': x, 'ln_gamma': ln_gamma, 'ln_beta': ln_beta, 'router_w': router_w, 'gate_up_w': gate_up_w, 'down_w': down_w}
    _L0_ffn_all = _L0_ffn_setup()
    _L0_ffn_in = {k: v for k, v in _L0_ffn_all.items() if k in ('ln_gamma', 'ln_beta', 'router_w', 'gate_up_w', 'down_w')}
    del _L0_ffn_all

    def _L1_attn_setup():
        import jax, jax.numpy as jnp
        import numpy as np
        D_MODEL = 256
        N_HEADS = 16
        HEAD_DIM = D_MODEL // N_HEADS
        WINDOW = 128
        ROPE_BASE = 10000.0

        def _rope_cos_sin(T, dim, dtype):
            inv_freq = 1.0 / ROPE_BASE ** (jnp.arange(0, dim, 2, dtype=jnp.float32) / dim)
            freqs = jnp.arange(T, dtype=jnp.float32)[:, None] * inv_freq[None, :]
            emb = jnp.concatenate([freqs, freqs], axis=-1)
            return (jnp.cos(emb).astype(dtype), jnp.sin(emb).astype(dtype))

        def _rotate_half(x):
            h = x.shape[-1] // 2
            return jnp.concatenate([-x[..., h:], x[..., :h]], axis=-1)

        def _apply_rotary(x, cos, sin):
            c = cos[None, :, None, :]
            s = sin[None, :, None, :]
            return x * c + _rotate_half(x) * s
        key = jax.random.key(seed)
        ks = jax.random.split(key, 6)
        B, T = (2, 512)
        query = jax.random.normal(ks[0], (B, T, D_MODEL), dtype=jnp.float32)
        scale = 1.0 / np.sqrt(D_MODEL)
        Wq = jax.random.normal(ks[1], (D_MODEL, D_MODEL), dtype=jnp.float32) * scale
        Wk = jax.random.normal(ks[2], (D_MODEL, D_MODEL), dtype=jnp.float32) * scale
        Wv = jax.random.normal(ks[3], (D_MODEL, D_MODEL), dtype=jnp.float32) * scale
        Wo = jax.random.normal(ks[4], (D_MODEL, D_MODEL), dtype=jnp.float32) * scale
        bo = jax.random.normal(ks[5], (D_MODEL,), dtype=jnp.float32) * 0.01
        return {'query': query, 'Wq': Wq, 'Wk': Wk, 'Wv': Wv, 'Wo': Wo, 'bo': bo}
    _L1_attn_all = _L1_attn_setup()
    _L1_attn_in = {k: v for k, v in _L1_attn_all.items() if k in ('Wq', 'Wk', 'Wv', 'Wo', 'bo')}
    del _L1_attn_all

    def _L1_ffn_setup():
        import jax, jax.numpy as jnp
        import numpy as np
        from jax import lax
        H = 256
        E = 8
        E_MLP = E - 4
        TOP_K = 2
        I = 128
        KC = 4
        SHARED_SCALE = 1.0
        key = jax.random.key(seed)
        ks = jax.random.split(key, 8)
        B, S = (4, 1024)
        s_h = 1.0 / np.sqrt(H)
        s_i = 1.0 / np.sqrt(I)
        return {'hidden_states': jax.random.normal(ks[0], (B, S, H), dtype=jnp.float32), 'Wr': jax.random.normal(ks[1], (H, E), dtype=jnp.float32) * s_h, 'router_bias': jnp.zeros((E,), dtype=jnp.float32), 'Wg': jax.random.normal(ks[2], (E_MLP, H, I), dtype=jnp.float32) * s_h, 'Wu': jax.random.normal(ks[3], (E_MLP, H, I), dtype=jnp.float32) * s_h, 'Wd': jax.random.normal(ks[4], (E_MLP, I, H), dtype=jnp.float32) * s_i, 'conv_w': jax.random.normal(ks[5], (KC, 1, H), dtype=jnp.float32) * (1.0 / np.sqrt(KC)), 'conv_b': jnp.zeros((H,), dtype=jnp.float32)}
    _L1_ffn_all = _L1_ffn_setup()
    _L1_ffn_in = {k: v for k, v in _L1_ffn_all.items() if k in ('Wr', 'router_bias', 'Wg', 'Wu', 'Wd', 'conv_w', 'conv_b')}
    del _L1_ffn_all
    return {'x': x, 'L0_tok_W': _L0_tok_in['W'], 'L0_tok_b': _L0_tok_in['b'], 'L0_tok_cls_token': _L0_tok_in['cls_token'], 'L0_tok_pos_enc': _L0_tok_in['pos_enc'], 'L0_attn_Wq': _L0_attn_in['Wq'], 'L0_attn_Wk': _L0_attn_in['Wk'], 'L0_attn_Wv': _L0_attn_in['Wv'], 'L0_attn_Wo': _L0_attn_in['Wo'], 'L0_ffn_ln_gamma': _L0_ffn_in['ln_gamma'], 'L0_ffn_ln_beta': _L0_ffn_in['ln_beta'], 'L0_ffn_router_w': _L0_ffn_in['router_w'], 'L0_ffn_gate_up_w': _L0_ffn_in['gate_up_w'], 'L0_ffn_down_w': _L0_ffn_in['down_w'], 'L1_attn_Wq': _L1_attn_in['Wq'], 'L1_attn_Wk': _L1_attn_in['Wk'], 'L1_attn_Wv': _L1_attn_in['Wv'], 'L1_attn_Wo': _L1_attn_in['Wo'], 'L1_attn_bo': _L1_attn_in['bo'], 'L1_ffn_Wr': _L1_ffn_in['Wr'], 'L1_ffn_router_bias': _L1_ffn_in['router_bias'], 'L1_ffn_Wg': _L1_ffn_in['Wg'], 'L1_ffn_Wu': _L1_ffn_in['Wu'], 'L1_ffn_Wd': _L1_ffn_in['Wd'], 'L1_ffn_conv_w': _L1_ffn_in['conv_w'], 'L1_ffn_conv_b': _L1_ffn_in['conv_b']}

def reference(x, L0_tok_W, L0_tok_b, L0_tok_cls_token, L0_tok_pos_enc, L0_attn_Wq, L0_attn_Wk, L0_attn_Wv, L0_attn_Wo, L0_ffn_ln_gamma, L0_ffn_ln_beta, L0_ffn_router_w, L0_ffn_gate_up_w, L0_ffn_down_w, L1_attn_Wq, L1_attn_Wk, L1_attn_Wv, L1_attn_Wo, L1_attn_bo, L1_ffn_Wr, L1_ffn_router_bias, L1_ffn_Wg, L1_ffn_Wu, L1_ffn_Wd, L1_ffn_conv_w, L1_ffn_conv_b):
    import jax
    import jax.numpy as jnp

    def _L0_tok_ref(x, W, b, cls_token, pos_enc):
        import jax, jax.numpy as jnp
        import numpy as np
        PATCH = 16

        def _patchify(x, p):
            B, C, H, W = x.shape
            nh, nw = (H // p, W // p)
            x = x.reshape(B, C, nh, p, nw, p)
            x = x.transpose(0, 2, 4, 1, 3, 5)
            return x.reshape(B, nh * nw, C * p * p)
        B = x.shape[0]
        patches = _patchify(x, PATCH)
        proj = jnp.einsum('bnf,df->bnd', patches, W) + b
        cls = jnp.broadcast_to(cls_token, (B, 1, cls_token.shape[-1]))
        out = jnp.concatenate([cls, proj], axis=1) + pos_enc
        return out

    def _L0_attn_ref(x, Wq, Wk, Wv, Wo):
        import jax, jax.numpy as jnp
        import numpy as np
        D_MODEL = 256
        N_HEADS = 16
        D_K = D_MODEL // N_HEADS
        THETA = 10000.0
        BATCH = 1
        SEQ = 1024

        def _rope(x, pos, inv_freq):
            angles = pos[:, None].astype(jnp.float32) * inv_freq
            cos = jnp.repeat(jnp.cos(angles), 2, axis=-1)
            sin = jnp.repeat(jnp.sin(angles), 2, axis=-1)
            x_rot = jnp.stack([-x[..., 1::2], x[..., 0::2]], axis=-1).reshape(x.shape)
            return x * cos + x_rot * sin
        b, s, _ = x.shape
        h, dk = (N_HEADS, D_K)
        proj = lambda W: jnp.einsum('bsi,oi->bso', x, W).reshape(b, s, h, dk).transpose(0, 2, 1, 3)
        q = proj(Wq)
        k = proj(Wk)
        v = proj(Wv)
        pos = jnp.arange(s)
        inv_freq = 1.0 / THETA ** (jnp.arange(0, dk, 2, dtype=jnp.float32) / dk)
        q = _rope(q, pos, inv_freq)
        k = _rope(k, pos, inv_freq)
        scores = jnp.einsum('bhqd,bhkd->bhqk', q, k) / jnp.sqrt(jnp.asarray(dk, jnp.float32))
        causal_mask = jnp.arange(s)[None, :] > jnp.arange(s)[:, None]
        scores = jnp.where(causal_mask, -jnp.inf, scores)
        weights = jax.nn.softmax(scores, axis=-1)
        out = jnp.einsum('bhqk,bhkd->bhqd', weights, v)
        out = out.transpose(0, 2, 1, 3).reshape(b, s, h * dk)
        return jnp.einsum('bsi,oi->bso', out, Wo)

    def _L0_ffn_ref(x, ln_gamma, ln_beta, router_w, gate_up_w, down_w):
        import jax, jax.numpy as jnp
        import numpy as np
        D_MODEL = 256
        D_FF = 512
        N_EXPERTS = 8
        TOP_K = 2
        CLAMP = 10000.0
        ROUTER_EPS = 1e-08
        LN_EPS = 1e-05

        def _layernorm(x, g, b):
            mu = jnp.mean(x, axis=-1, keepdims=True)
            var = jnp.mean(jnp.square(x - mu), axis=-1, keepdims=True)
            return (x - mu) * jax.lax.rsqrt(var + LN_EPS) * g + b
        B, S, D = x.shape
        xn = _layernorm(x, ln_gamma, ln_beta)
        xf = xn.reshape(-1, D)
        N = xf.shape[0]
        logits = jnp.clip(xf @ router_w.T, -CLAMP, CLAMP)
        m = jnp.max(logits, axis=-1, keepdims=True)
        e = jnp.exp(logits - m)
        probs = e / (jnp.sum(e, axis=-1, keepdims=True) + ROUTER_EPS)
        probs = jnp.clip(probs, ROUTER_EPS, 1.0)
        topk_p, topk_i = jax.lax.top_k(probs, TOP_K)
        dense_gate = jnp.zeros((N, N_EXPERTS), probs.dtype).at[jnp.arange(N)[:, None], topk_i].add(topk_p)
        out = jnp.zeros_like(xf)
        for eid in range(N_EXPERTS):
            xe = xf * dense_gate[:, eid:eid + 1]
            gu = xe @ gate_up_w[eid].T
            gate, up = jnp.split(gu, 2, axis=-1)
            hidden = jax.nn.silu(gate) * up
            out = out + hidden @ down_w[eid].T
        return x + out.reshape(B, S, D)

    def _L1_attn_ref(query, Wq, Wk, Wv, Wo, bo):
        import jax, jax.numpy as jnp
        import numpy as np
        D_MODEL = 256
        N_HEADS = 16
        HEAD_DIM = D_MODEL // N_HEADS
        WINDOW = 128
        ROPE_BASE = 10000.0

        def _rope_cos_sin(T, dim, dtype):
            inv_freq = 1.0 / ROPE_BASE ** (jnp.arange(0, dim, 2, dtype=jnp.float32) / dim)
            freqs = jnp.arange(T, dtype=jnp.float32)[:, None] * inv_freq[None, :]
            emb = jnp.concatenate([freqs, freqs], axis=-1)
            return (jnp.cos(emb).astype(dtype), jnp.sin(emb).astype(dtype))

        def _rotate_half(x):
            h = x.shape[-1] // 2
            return jnp.concatenate([-x[..., h:], x[..., :h]], axis=-1)

        def _apply_rotary(x, cos, sin):
            c = cos[None, :, None, :]
            s = sin[None, :, None, :]
            return x * c + _rotate_half(x) * s
        B, T, D = query.shape
        H, Dh = (N_HEADS, HEAD_DIM)
        sm_scale = Dh ** (-0.5)
        q = (query @ Wq.T).reshape(B, T, H, Dh)
        k = (query @ Wk.T).reshape(B, T, H, Dh)
        v = (query @ Wv.T).reshape(B, T, H, Dh)
        cos, sin = _rope_cos_sin(T, Dh, query.dtype)
        q = _apply_rotary(q, cos, sin)
        k = _apply_rotary(k, cos, sin)
        q = q.transpose(0, 2, 1, 3)
        k = k.transpose(0, 2, 1, 3)
        v = v.transpose(0, 2, 1, 3)
        scores = jnp.einsum('bhqd,bhkd->bhqk', q, k) * sm_scale
        i = jnp.arange(T)[:, None]
        j = jnp.arange(T)[None, :]
        mask = (j > i) | (j < i - (WINDOW - 1))
        scores = jnp.where(mask[None, None], jnp.float32(-jnp.inf), scores)
        attn = jax.nn.softmax(scores, axis=-1)
        out = jnp.einsum('bhqk,bhkd->bhqd', attn, v)
        out = out.transpose(0, 2, 1, 3).reshape(B, T, D)
        return out @ Wo.T + bo

    def _L1_ffn_ref(hidden_states, Wr, router_bias, Wg, Wu, Wd, conv_w, conv_b):
        import jax, jax.numpy as jnp
        import numpy as np
        from jax import lax
        H = 256
        E = 8
        E_MLP = E - 4
        TOP_K = 2
        I = 128
        KC = 4
        SHARED_SCALE = 1.0
        B, S, Hd = hidden_states.shape
        T = B * S
        x = hidden_states.reshape(T, Hd)
        scores = jax.nn.sigmoid(x @ Wr)
        _, idx = lax.top_k(scores + router_bias, TOP_K)
        w = jnp.take_along_axis(scores, idx, axis=-1)
        w = w / (jnp.sum(w, axis=-1, keepdims=True) + 1e-09)
        cw = jnp.zeros((T, E), dtype=x.dtype).at[jnp.arange(T)[:, None], idx].add(w)
        g = jnp.einsum('th,ehi->tei', x, Wg)
        u = jnp.einsum('th,ehi->tei', x, Wu)
        hid = jax.nn.silu(g) * u
        mlp_out = jnp.einsum('tei,eih->teh', hid, Wd)
        routed = jnp.einsum('te,teh->th', cw[:, :E_MLP], mlp_out)
        routed = routed + cw[:, E_MLP:E_MLP + 1] * x
        routed = routed + cw[:, E_MLP + 2:E_MLP + 3] * x
        routed = routed + cw[:, E_MLP + 3:E_MLP + 4] * jax.nn.relu(x)
        routed = routed.reshape(B, S, Hd)
        shared = lax.conv_general_dilated(hidden_states, conv_w, window_strides=(1,), padding=[(KC - 1, 0)], dimension_numbers=('NHC', 'HIO', 'NHC'), feature_group_count=Hd) + conv_b
        return routed + SHARED_SCALE * shared
    h = _L0_tok_ref(x, L0_tok_W, L0_tok_b, L0_tok_cls_token, L0_tok_pos_enc)
    h = h + _L0_attn_ref(_layernorm(h, axis=-1), L0_attn_Wq, L0_attn_Wk, L0_attn_Wv, L0_attn_Wo)
    h = h + _L0_ffn_ref(_layernorm(h, axis=-1), L0_ffn_ln_gamma, L0_ffn_ln_beta, L0_ffn_router_w, L0_ffn_gate_up_w, L0_ffn_down_w)
    h = h + _L1_attn_ref(_layernorm(h, axis=-1), L1_attn_Wq, L1_attn_Wk, L1_attn_Wv, L1_attn_Wo, L1_attn_bo)
    h = h + _L1_ffn_ref(_layernorm(h, axis=-1), L1_ffn_Wr, L1_ffn_router_bias, L1_ffn_Wg, L1_ffn_Wu, L1_ffn_Wd, L1_ffn_conv_w, L1_ffn_conv_b)
    return h

_drawn_inputs = setup_inputs


def setup_inputs(seed=0):
    import zlib

    import numpy as np

    out = dict(_drawn_inputs(seed))
    spreads = {'L0_ffn_ln_gamma': (1.0, 0.6),
     'L0_ffn_ln_beta': (0.0, 0.8),
     'L1_ffn_router_bias': (0.0, 0.8),
     'L1_ffn_conv_b': (0.0, 2.0)}
    factors = {'L0_ffn_router_w': 3.587,
     'L0_ffn_gate_up_w': 3.742,
     'L0_ffn_down_w': 3.292,
     'L1_attn_bo': 44.68,
     'L1_attn_Wq': 6.318,
     'L1_attn_Wk': 6.279,
     'L1_attn_Wv': 3.675,
     'L1_attn_Wo': 3.622,
     'L1_ffn_Wr': 4.557,
     'L1_ffn_Wg': 6.485,
     'L1_ffn_Wu': 6.164,
     'L1_ffn_Wd': 6.089,
     'L1_ffn_conv_w': 4.631}
    for name, (base, spread) in spreads.items():
        noise = np.random.default_rng([zlib.crc32(name.encode()), seed]).standard_normal(out[name].shape)
        drawn = base * np.exp(spread * noise) if base else spread * noise
        out[name] = jnp.asarray(drawn.astype(out[name].dtype))
    for name, factor in factors.items():
        out[name] = (out[name] * factor).astype(out[name].dtype)
    return out
```

```python
import concourse.bass as bass
from concourse import mybir
from contextlib import ExitStack

B, IMG, CH, PATCH = 32, 96, 3, 16
SIDE = IMG // PATCH
Q = SIDE * SIDE + 1
D, H, DK = 256, 16, 16
G = 3
W = G * Q
NT = -(-B // G)
NF = CH * PATCH * PATCH // 128
E = 8
FF = 512
SLOT = 128
NS = (2 * NT * W + E * (SLOT - 1)) // SLOT
MAXT = -(-NT * W // SLOT)
E1, I1 = 4, 128
KC = 4
BANK = 512
HH = H // 2
VW = G * (DK + 1)
HALF = 64
SR = HALF + Q
SC = HH * W
SCR = max(SC, H * VW)
SCALE = DK ** -0.5
EPS = 1e-5
NEG = -3.0e38


def build(nc, patches, tok_w, rows, ident, rope, headmask, imgmask, causal, selq, tri, cumtri,
          thresholds, iota, wqkv, wo, router, router_bias, gate_up, down, gate_up1, down1, conv,
          out, stop="all"):
    fp32, bf16 = mybir.dt.float32, mybir.dt.bfloat16
    u32, i32 = mybir.dt.uint32, mybir.dt.int32
    ALU, ACT, AX = mybir.AluOpType, mybir.ActivationFunctionType, mybir.AxisListType
    ds = bass.ds
    ctx = ExitStack()

    def sb(name, shape, dt=fp32):
        return ctx.enter_context(nc.sbuf_tensor(name, shape, dt))

    def sem(name):
        return ctx.enter_context(nc.semaphore(name))

    both_layers = {}

    def shared(name):
        if name not in both_layers:
            both_layers[name] = sem(name)
        return both_layers[name]

    def later(t, depth):
        return not isinstance(t, int) or t >= depth

    def carry():
        nc.vector.memset(spare[:, :], 0.0)

    def exists(t, n):
        return not isinstance(t, int) or t < n

    def over(eng, n, body, unroll=2, head=2, tail=0):
        for t in range(head):
            body(t, t % unroll, t // unroll)
        trips = (n - tail - head) // unroll
        if trips > 0:
            with eng.Fori(0, trips) as i:
                for u in range(unroll):
                    body(i * unroll + (head + u), (head + u) % unroll, i + (head + u) // unroll)
        else:
            trips = 0
        for t in range(head + trips * unroll, n):
            body(t, t % unroll, t // unroll)

    with ctx:
        w_gu = sb("w_gu", [128, E, 2 * 2 * FF])
        w_dn = sb("w_dn", [128, E, 4 * D])
        tokw = w_gu[:, 6, 0:NF * D]
        patch = [w_gu[:, 7, s * NF * W:(s + 1) * NF * W] for s in range(3)]
        h = sb("h", [W, NT * D])
        scr = sb("scr", [W, NT * SCR])
        v_all = sb("v_all", [W, NT * D])
        wqkv_sb = sb("wqkv_sb", [128, 2, 3 * D])
        wo_sb = sb("wo_sb", [128, 2, D])
        router_sb = sb("router_sb", [128, 2, 2, E])
        rows_sb = sb("rows_sb", [W, 5, D])
        ident_sb = sb("ident_sb", [128, 128])
        rope_sb = sb("rope_sb", [W, 2, DK])
        headmask_sb = sb("headmask_sb", [128, HH])
        imgmask_sb = sb("imgmask_sb", [W, G])
        causal_f = sb("causal_f", [Q, HH * Q])
        selq_f = sb("selq_f", [Q, 128])
        causal_sb = sb("causal_sb", [Q, HH * Q], bf16)
        selq_sb = sb("selq_sb", [Q, 128], bf16)
        tri_sb = sb("tri_sb", [W, W])
        cumtri_sb = sb("cumtri_sb", [128, E * E])
        thr_sb = sb("thr_sb", [128, MAXT])
        iota_sb = sb("iota_sb", [128, NS])
        rbias_sb = sb("rbias_sb", [W, E])
        conv_sb = sb("conv_sb", [128, 2, KC + 1])
        ones = sb("ones", [W, 128])
        halfneg = sb("halfneg", [W, 1])
        epsv = sb("epsv", [W, 1])
        spare = sb("spare", [W, 1])
        stats = [sb(f"stats{s}", [W, 6]) for s in range(2)]
        mv = [sb(f"mv{s}", [W, 2]) for s in range(2)]
        veps = [sb(f"veps{s}", [W, 1]) for s in range(2)]
        rstd = [sb(f"rstd{s}", [W, 1]) for s in range(2)]
        stats2 = [sb(f"stats2{s}", [W, 6]) for s in range(2)]
        mv2 = [sb(f"mv2{s}", [W, 2]) for s in range(2)]
        veps2 = [sb(f"veps2{s}", [W, 1]) for s in range(2)]
        rstd2 = [sb(f"rstd2{s}", [W, 1]) for s in range(2)]
        logits = sb("logits", [W, NT, E])
        cw = sb("cw", [W, NT, E])
        skipw = sb("skipw", [W, NT])
        pos_u = [sb(f"pos_u{c}", [W, NT], u32) for c in range(2)]
        tile_expert = sb("tile_expert", [1, NS], i32)
        work = sb("work", [128, 6500])

        def area(first=0):
            at = [first]

            def take(rows_, cols):
                a = work[0:rows_, at[0]:at[0] + cols]
                at[0] += cols
                assert at[0] <= 6500, at
                return a
            return take

        psum = ctx.enter_context(nc.psum_tensor("psum", [128, 8 * BANK], fp32))
        bank = [psum[:, i * BANK:(i + 1) * BANK] for i in range(8)]

        consts_in = sem("consts_in")
        patch_in = [sem(f"patch_in{s}") for s in range(3)]
        tokw_in = sem("tokw_in")
        attw_in = [sem(f"attw_in{n}") for n in range(2)]
        experts_in = sem("experts_in")
        experts67_in = sem("experts67_in")
        ffn1_in = sem("ffn1_in")
        tables = sem("tables")
        pool_tables = sem("pool_tables")
        tok_done = sem("tok_done")
        h_tok = sem("h_tok")
        zeroed = sem("zeroed")
        out_sent = sem("out_sent")

        xs_d = nc.dram_tensor("sorted_rows", (NS * SLOT, D), fp32, kind="Internal").ap()
        ys_d = nc.dram_tensor("sorted_outputs", (NS * SLOT, D), fp32, kind="Internal").ap()

        block = ctx.enter_context(nc.Block())
        progs = {"sync": [], "gpsimd": [], "scalar": [], "vector": [], "tensor": []}

        def part(engine):
            def add(f):
                progs[engine].append(f)
            return add

        hs = lambda t: h[:, ds(t * D, D)]
        V, P, A, T = nc.vector, nc.gpsimd, nc.scalar, nc.tensor

        CONSTS = [(rows_sb[:, :, :], rows), (ident_sb[:, :], ident), (rope_sb[:, :, :], rope),
                  (headmask_sb[:, :], headmask), (imgmask_sb[:, :], imgmask), (causal_f[:, :], causal),
                  (selq_f[:, :], selq), (tri_sb[:, :], tri), (cumtri_sb[:, :], cumtri),
                  (thr_sb[:, :], thresholds), (iota_sb[:, :], iota), (router_sb[:, :, :, :], router),
                  (rbias_sb[:, :], router_bias), (conv_sb[:, :, :], conv)]

        @part("sync")
        def _(sp):
            sp.dma_start(tokw, tok_w).then_inc(tokw_in, 16)

            def load(t, s, k):
                if later(t, 3):
                    sp.wait_ge(tok_done, t - 2)
                sp.dma_start(patch[s], patches[ds(t, 1), :, :].rearrange("a p n -> (a p) n")).then_inc(patch_in[s], 16)
            for t in range(3):
                load(t, t, 0)
            for dst, src in CONSTS:
                sp.dma_start(dst, src).then_inc(consts_in, 16)
            sp.dma_start(wqkv_sb[:, :, :], wqkv[0]).then_inc(attw_in[0], 16)
            sp.dma_start(wo_sb[:, :, :], wo[0]).then_inc(attw_in[0], 16)
            with sp.Fori(0, (NT - 3) // 3) as i:
                for u in range(3):
                    load(i * 3 + (3 + u), u, i + 1)
            for t in range(3 + (NT - 3) // 3 * 3, NT):
                load(t, t % 3, t // 3)
            for e in range(6):
                sp.dma_start(w_gu[:, e, :], gate_up[e]).then_inc(experts_in, 16)
                sp.dma_start(w_dn[:, e, :], down[e]).then_inc(experts_in, 16)
            sp.wait_ge(tok_done, NT)
            for e in range(6, E):
                sp.dma_start(w_gu[:, e, :], gate_up[e]).then_inc(experts67_in, 16)
                sp.dma_start(w_dn[:, e, :], down[e]).then_inc(experts67_in, 16)

        zero = work[:, 0:2 * D]

        @part("gpsimd")
        def _(pool):
            P.memset(ones[:, :], 1.0).then_inc(pool_tables, 1)
            P.memset(halfneg[:, :], -0.5).then_inc(pool_tables, 1)
            P.memset(epsv[:, :], EPS).then_inc(pool_tables, 1)
            P.memset(zero, 0.0).then_inc(pool_tables, 1)
            pool.wait_ge(pool_tables, 4)
            for n in range(NS):
                pool.dma_start(xs_d[n * SLOT:(n + 1) * SLOT, :], zero[:, 0:D]).then_inc(zeroed, 16)
            pool.wait_ge(zeroed, 16 * NS)

        @part("vector")
        def _(dve):
            dve.wait_ge(consts_in, 16 * len(CONSTS))
            V.tensor_copy(causal_sb[:, :], causal_f[:, :]).then_inc(tables, 1)
            V.tensor_copy(selq_sb[:, :], selq_f[:, :]).then_inc(tables, 1)
            V.tensor_tensor(rows_sb[:, 0, :], rows_sb[:, 0, :], rows_sb[:, 1, :], ALU.add).then_inc(tables, 1)
            dve.wait_ge(tables, 3)

            def add_pos(t, s, k):
                dve.wait_ge(tok_done, t + 1)
                V.tensor_tensor(hs(t), bank[s][0:W, 0:D], rows_sb[:, 0, :], ALU.add).then_inc(h_tok, 1)
            over(dve, NT, add_pos, unroll=3, head=3)

        @part("tensor")
        def _(pe):
            pe.wait_ge(tokw_in, 16)

            def product(t, s, k):
                pe.wait_ge(patch_in[s], 16 * k + 16)
                if later(t, 3):
                    pe.wait_ge(h_tok, t - 2)
                for c in range(NF):
                    mm = T.matmul(bank[s][0:W, 0:D], patch[s][:, c * W:(c + 1) * W],
                                  tokw[:, c * D:(c + 1) * D], start=c == 0, stop=c == NF - 1)
                mm.then_inc(tok_done, 1)
            over(pe, NT, product, unroll=3, head=3)

        def attention(L, h_in, h_out, free_before):
            base = L * NT
            take = area()
            xn = [take(W, D) for _ in range(2)]
            xnT = [take(128, 2 * W) for _ in range(2)]
            qkf = [take(W, 2 * D) for _ in range(2)]
            cosd = [take(W, 2 * D) for _ in range(2)]
            sind = [take(W, 2 * D) for _ in range(2)]
            st, ag, ve, rs, xd, td, xe_, qkd, vd, qke, vev, cosn, sinn, roped = (
                shared(x) for x in ("a_stats", "a_aggr", "a_veps", "a_rstd", "a_xn", "a_transposed",
                                "a_xnT", "a_qk", "a_v", "a_qk_copied", "a_v_copied", "a_cos",
                                "a_sin", "a_roped"))
            tb, qkb, vb = bank[0:2], bank[2:4], bank[4:6]
            scq = lambda t: scr[:, ds(t * SCR, 2 * D)]

            @part("vector")
            def _(dve):
                free_before(dve)

                def stat(t, s):
                    dve.wait_ge(h_in, t + 1)
                    V.bn_stats(stats[s][:, :], hs(t)).then_inc(st, 1)
                    if later(t, 2):
                        dve.wait_ge(rs, base + t - 1)
                    dve.wait_ge(st, base + t + 1)
                    carry()
                    V.bn_aggr(mv[s][:, :], stats[s][:, :]).then_inc(ag, 1)

                def norm(t, s):
                    dve.wait_ge(rs, base + t + 1)
                    dve.wait_ge(ag, base + t + 1)
                    if later(t, 2):
                        dve.wait_ge(td, base + t - 1)
                    V.tensor_scalar(xn[s], hs(t), mv[s][:, 0:1], rstd[s][:, :],
                                    ALU.subtract, ALU.mult).then_inc(xd, 1)

                def rotate(t, s):
                    dve.wait_ge(sinn, base + t + 1)
                    dve.wait_ge(cosn, base + t + 1)
                    V.tensor_tensor(scq(t), cosd[s], sind[s], ALU.add).then_inc(roped, 1)

                stat(0, 0)
                stat(1, 1)
                norm(0, 0)
                norm(1, 1)
                stat(2, 0)

                def body(t, s, k):
                    if exists(t + 2, NT):
                        norm(t + 2, s)
                    if exists(t + 3, NT):
                        stat(t + 3, 1 - s)
                    dve.wait_ge(qke, base + t + 1)
                    if later(t, 2):
                        dve.wait_ge(roped, base + t - 1)
                    V.tensor_tensor(cosd[s].rearrange("p (h d) -> p h d", d=DK),
                                    qkf[s].rearrange("p (h d) -> p h d", d=DK),
                                    rope_sb[:, 0, :].unsqueeze(1).broadcast_to([W, 2 * H, DK]),
                                    ALU.mult).then_inc(cosn, 1)
                    if later(t, 1):
                        rotate(t - 1, 1 - s)
                over(dve, NT, body, head=2, tail=3)
                rotate(NT - 1, (NT - 1) % 2)

            @part("gpsimd")
            def _(pool):
                free_before(pool)

                def root(t, s):
                    pool.wait_ge(ag, base + t + 1)
                    P.tensor_tensor(veps[s][:, :], mv[s][:, 1:2], epsv[:, :], ALU.add).then_inc(ve, 1)
                    pool.wait_ge(ve, base + t + 1)
                    if later(t, 2):
                        pool.wait_ge(xd, base + t - 1)
                    P.tensor_tensor(rstd[s][:, :], veps[s][:, :], halfneg[:, :], ALU.pow).then_inc(rs, 1)
                root(0, 0)
                root(1, 1)
                root(2, 0)

                def body(t, s, k):
                    if exists(t + 3, NT):
                        root(t + 3, 1 - s)
                    pool.wait_ge(qke, base + t + 1)
                    if later(t, 2):
                        pool.wait_ge(roped, base + t - 1)
                    x = qkf[s].rearrange("p (h a d) -> p h a d", a=2, d=DK // 2)
                    o = sind[s].rearrange("p (h a d) -> p h a d", a=2, d=DK // 2)
                    sn = rope_sb[:, 1, :].rearrange("p (a d) -> p a d", a=2)
                    for a in range(2):
                        ins = P.tensor_tensor(o[:, :, a, :], x[:, :, 1 - a, :],
                                              sn[:, a, :].unsqueeze(1).broadcast_to([W, 2 * H, DK // 2]),
                                              ALU.mult)
                    ins.then_inc(sinn, 1)
                over(pool, NT, body, head=2, tail=3)

            @part("scalar")
            def _(act):
                free_before(act)

                def turn(t, s):
                    act.wait_ge(td, base + t + 1)
                    if later(t, 2):
                        act.wait_ge(vd, base + t - 1)
                    A.activation(xnT[s], tb[s][:, 0:2 * W], ACT.Copy).then_inc(xe_, 1)
                turn(0, 0)

                def body(t, s, k):
                    if exists(t + 1, NT):
                        turn(t + 1, 1 - s)
                    act.wait_ge(qkd, base + t + 1)
                    if later(t, 2):
                        act.wait_ge(cosn, base + t - 1)
                        act.wait_ge(sinn, base + t - 1)
                    A.activation(qkf[s], qkb[s][0:W, 0:2 * D], ACT.Copy).then_inc(qke, 1)
                    act.wait_ge(vd, base + t + 1)
                    A.activation(v_all[:, ds(t * D, D)], vb[s][0:W, 0:D], ACT.Copy).then_inc(vev, 1)
                over(act, NT, body, head=2, tail=1)

            @part("tensor")
            def _(pe):
                free_before(pe)
                pe.wait_ge(attw_in[L], 32)
                pe.wait_ge(tables, 3)

                def turn(t, s):
                    pe.wait_ge(xd, base + t + 1)
                    if later(t, 2):
                        pe.wait_ge(xe_, base + t - 1)
                    for c in range(2):
                        mm = T.transpose(tb[s][:, c * W:(c + 1) * W], xn[s][:, c * 128:(c + 1) * 128],
                                         ident_sb[0:W, 0:W])
                    mm.then_inc(td, 1)
                turn(0, 0)

                def body(t, s, k):
                    if exists(t + 1, NT):
                        turn(t + 1, 1 - s)
                    pe.wait_ge(xe_, base + t + 1)
                    if later(t, 2):
                        pe.wait_ge(qke, base + t - 1)
                        pe.wait_ge(vev, base + t - 1)
                    for o, b_, w_, sm in ((0, qkb, 2 * D, qkd), (2 * D, vb, D, vd)):
                        for c in range(2):
                            mm = T.matmul(b_[s][0:W, 0:w_], xnT[s][:, c * W:(c + 1) * W],
                                          wqkv_sb[:, c, o:o + w_], start=c == 0, stop=c == 1)
                        mm.then_inc(sm, 1)
                over(pe, NT, body, head=2, tail=1)

            take = area()
            qks = [take(W, 2 * D) for _ in range(2)]
            qkT = [take(128, 4 * W) for _ in range(2)]
            kblk = [take(128, 2 * HH * W) for _ in range(2)]
            mx = [take(SR, G * HH) for _ in range(2)]
            cp, tr, tre, bl0, bl1, scd, mxd, sbd = (
                shared(x) for x in ("b_qk", "b_transposed", "b_qkT", "b_block0", "b_block1",
                                    "b_scores", "b_max", "b_sub"))
            tbb = bank[0:2]
            sbank = lambda s, b: bank[2 + G * s + b]
            s4 = lambda s: psum[0:SR, (2 + G * s) * BANK:(2 + G * s + G) * BANK].rearrange(
                "p (b n) -> p b n", b=G)[:, :, 0:HH * Q].rearrange("p b (h k) -> p b h k", h=HH)

            def a_over(eng):
                eng.wait_ge(roped, base + NT)
                eng.wait_ge(vev, base + NT)

            @part("scalar")
            def _(act):
                a_over(act)

                def fix(t, s):
                    if later(t, 2):
                        act.wait_ge(tr, base + t - 1)
                    A.activation(qks[s], scq(t), ACT.Copy).then_inc(cp, 1)
                fix(0, 0)
                fix(1, 1)

                def turn(t, s):
                    act.wait_ge(tr, base + t + 1)
                    if later(t, 2):
                        act.wait_ge(scd, base + t - 1)
                    A.activation(qkT[s], tbb[s][:, 0:4 * W], ACT.Copy).then_inc(tre, 1)
                turn(0, 0)

                def body(t, s, k):
                    if exists(t + 2, NT):
                        fix(t + 2, s)
                    if exists(t + 1, NT):
                        turn(t + 1, 1 - s)
                over(act, NT, body, head=2, tail=2)

            def spread(eng, t, s, f, done):
                eng.wait_ge(tre, base + t + 1)
                if later(t, 2):
                    eng.wait_ge(scd, base + t - 1)
                b4 = kblk[s][:, f * HH * W:(f + 1) * HH * W].rearrange("p (b h q) -> p b h q", b=G, h=HH)
                k3 = qkT[s][:, (2 + f) * W:(3 + f) * W].rearrange("p (b q) -> p b q", b=G)
                for b in range(G):
                    ins = eng.tensor_tensor(
                        b4[:, b, :, :], k3[:, b, :].unsqueeze(1).broadcast_to([128, HH, Q]),
                        headmask_sb[:, :].unsqueeze(2).broadcast_to([128, HH, Q]), ALU.mult)
                ins.then_inc(done, 1)

            @part("gpsimd")
            def _(pool):
                a_over(pool)
                over(pool, NT, lambda t, s, k: spread(pool, t, s, 1, bl1), head=2)

            @part("vector")
            def _(dve):
                a_over(dve)
                spread(dve, 0, 0, 0, bl0)

                def body(t, s, k):
                    if exists(t + 1, NT):
                        spread(dve, t + 1, 1 - s, 0, bl0)
                    dve.wait_ge(scd, base + t + 1)
                    V.tensor_reduce(mx[s], s4(s), AX.X, ALU.max).then_inc(mxd, 1)
                    dve.wait_ge(mxd, base + t + 1)
                    m3 = mx[s].rearrange("p (b h) -> p b h", b=G)
                    o4 = scr[0:SR, ds(t * SCR, SC)].rearrange("p (h b k) -> p b h k", h=HH, b=G)
                    for b in range(G):
                        ins = V.tensor_tensor(o4[:, b, :, :], s4(s)[:, b, :, :],
                                              m3[:, b, :].unsqueeze(2).broadcast_to([SR, HH, Q]), ALU.subtract)
                    ins.then_inc(sbd, 1)
                over(dve, NT, body, head=2, tail=1)

            @part("tensor")
            def _(pe):
                a_over(pe)

                def turn(t, s):
                    pe.wait_ge(cp, base + t + 1)
                    if later(t, 2):
                        pe.wait_ge(tre, base + t - 1)
                    for c in range(4):
                        mm = T.transpose(tbb[s][:, c * W:(c + 1) * W], qks[s][:, c * 128:(c + 1) * 128],
                                         ident_sb[0:W, 0:W])
                    mm.then_inc(tr, 1)
                turn(0, 0)

                def body(t, s, k):
                    if exists(t + 1, NT):
                        turn(t + 1, 1 - s)
                    if later(t, 2):
                        pe.wait_ge(sbd, base + t - 1)
                    for b in range(G):
                        T.matmul(sbank(s, b)[:, 0:HH * Q], selq_sb[:, :], causal_sb[:, :],
                                 start=True, stop=False, skip_group_check=True)
                    for f, blocks in ((0, bl0), (1, bl1)):
                        pe.wait_ge(blocks, base + t + 1)
                        for b in range(G):
                            k0 = (f * G + b) * HH * Q
                            mm = T.matmul(sbank(s, b)[f * HALF:f * HALF + Q, 0:HH * Q],
                                          qkT[s][:, f * W + b * Q:f * W + (b + 1) * Q],
                                          kblk[s][:, k0:k0 + HH * Q],
                                          start=False, stop=f == 1, skip_group_check=True)
                    mm.then_inc(scd, 1)
                over(pe, NT, body, head=2, tail=1)

            take = area()
            pr = [take(SR, SC) for _ in range(2)]
            prT = [take(W, HH * 128) for _ in range(2)]
            vblk = [take(W, H * VW) for _ in range(2)]
            ex, pt, pte0, pte1, vb_, pv0, pv1, oe0, oe1, vone = (
                shared(x) for x in ("c_exp", "c_transposed", "c_prT0", "c_prT1", "c_vblock", "c_out0",
                                "c_out1", "c_out0_copied", "c_out1_copied", "c_ones"))
            pte, pvd, oed = (pte0, pte1), (pv0, pv1), (oe0, oe1)
            tpb = lambda s, f: bank[2 * s + f]
            ob = lambda s, f: bank[4 + 2 * s + f]

            def b_over(eng):
                eng.wait_ge(sbd, base + NT)

            def copy_prT(eng, fn, t, s, f):
                eng.wait_ge(pt, base + t + 1)
                if later(t, 2):
                    eng.wait_ge(pv1, base + t - 1)
                n3 = lambda a: a.rearrange("p (h q) -> p h q", q=128)[:, :, 0:SR]
                fn(n3(prT[s][:, f * 512:(f + 1) * 512]), n3(tpb(s, f)[0:W, :])).then_inc(pte[f], 1)

            def copy_out(eng, fn, t, s, f):
                eng.wait_ge(pvd[f], base + t + 1)
                fn(scr[0:Q, ds(t * SCR + f * HH * VW, HH * VW)], ob(s, f)[0:Q, 0:HH * VW]).then_inc(oed[f], 1)

            act_copy = lambda o, i: A.activation(o, i, ACT.Copy)
            dve_copy = lambda o, i: V.tensor_copy(o, i)

            @part("scalar")
            def _(act):
                b_over(act)

                def expo(t, s):
                    if later(t, 2):
                        act.wait_ge(pt, base + t - 1)
                    A.activation(pr[s], scr[0:SR, ds(t * SCR, SC)], ACT.Exp, scale=SCALE).then_inc(ex, 1)
                expo(0, 0)
                expo(1, 1)
                copy_prT(act, act_copy, 0, 0, 0)

                def body(t, s, k):
                    if exists(t + 2, NT):
                        expo(t + 2, s)
                    if exists(t + 1, NT):
                        copy_prT(act, act_copy, t + 1, 1 - s, 0)
                    copy_out(act, act_copy, t, s, 0)
                over(act, NT, body, head=2, tail=2)

            @part("vector")
            def _(dve):
                b_over(dve)
                copy_prT(dve, dve_copy, 0, 0, 1)

                def body(t, s, k):
                    if exists(t + 1, NT):
                        copy_prT(dve, dve_copy, t + 1, 1 - s, 1)
                    dve.wait_ge(ex, base + t + 1)
                    copy_out(dve, dve_copy, t, s, 1)
                over(dve, NT, body, head=2, tail=1)

            @part("gpsimd")
            def _(pool):
                b_over(pool)
                v4 = lambda s: vblk[s].rearrange("p (h b d) -> p h b d", h=H, b=G)
                for s in range(2):
                    for b in range(G):
                        ins = P.tensor_scalar(v4(s)[:, :, b, DK], ones[:, 0:H], imgmask_sb[:, b:b + 1],
                                              None, ALU.mult)
                ins.then_inc(vone, 1)

                def body(t, s, k):
                    if later(t, 2):
                        pool.wait_ge(pv1, base + t - 1)
                    for b in range(G):
                        ins = P.tensor_tensor(v4(s)[:, :, b, 0:DK],
                                              v_all[:, ds(t * D, D)].rearrange("p (h d) -> p h d", d=DK),
                                              imgmask_sb[:, b:b + 1].unsqueeze(2).broadcast_to([W, H, DK]),
                                              ALU.mult)
                    ins.then_inc(vb_, 1)
                over(pool, NT, body, head=2)

            @part("tensor")
            def _(pe):
                b_over(pe)

                def turn(t, s):
                    pe.wait_ge(ex, base + t + 1)
                    if later(t, 2):
                        pe.wait_ge(pte0, base + t - 1)
                        pe.wait_ge(pte1, base + t - 1)
                    for j in range(HH):
                        mm = T.transpose(tpb(s, j // 4)[0:W, (j % 4) * 128:(j % 4) * 128 + SR],
                                         pr[s][:, j * W:(j + 1) * W], ident_sb[0:SR, 0:SR])
                    mm.then_inc(pt, 1)
                turn(0, 0)
                pe.wait_ge(vone, L + 1)

                def body(t, s, k):
                    if exists(t + 1, NT):
                        turn(t + 1, 1 - s)
                    pe.wait_ge(vb_, base + t + 1)
                    pe.wait_ge(pte0, base + t + 1)
                    pe.wait_ge(pte1, base + t + 1)
                    for f in range(2):
                        if later(t, 2):
                            pe.wait_ge(oed[f], base + t - 1)
                        for hd in range(HH):
                            p0 = hd * 128 + f * HALF
                            v0 = (f * HH + hd) * VW
                            mm = T.matmul(ob(s, f)[0:Q, hd * VW:(hd + 1) * VW], prT[s][:, p0:p0 + Q],
                                          vblk[s][:, v0:v0 + VW], start=True, stop=True)
                        mm.then_inc(pvd[f], 1)
                over(pe, NT, body, head=2, tail=1)

            take = area()
            rc = [take(Q, H * G) for _ in range(2)]
            on = [take(W, G * D) for _ in range(2)]
            oT = [take(128, 2 * W) for _ in range(2)]
            clr, rcd, ond, ot, ote, wod, bod = (
                shared(x) for x in ("d_clear", "d_recip", "d_scaled", "d_transposed", "d_outT", "d_proj", "d_bias"))
            otb, wob = bank[0:2], bank[2:4]

            def c_over(eng):
                eng.wait_ge(oe0, base + NT)
                eng.wait_ge(oe1, base + NT)

            @part("gpsimd")
            def _(pool):
                c_over(pool)
                if L == 1:
                    over(pool, NT, lambda t, s, k: P.tensor_tensor(
                        hs(t), hs(t), rows_sb[:, 4, :], ALU.add).then_inc(bod, 1), head=2)

            @part("vector")
            def _(dve):
                c_over(dve)
                for s in range(2):
                    V.memset(on[s], 0.0).then_inc(clr, 1)
                dve.wait_ge(clr, 2 * L + 2)

                def scale(t, s):
                    o4 = scr[0:Q, ds(t * SCR, H * VW)].rearrange("p (n d) -> p n d", d=DK + 1)
                    if later(t, 2):
                        dve.wait_ge(ond, base + t - 1)
                    V.reciprocal(rc[s], o4[:, :, DK]).then_inc(rcd, 1)
                    dve.wait_ge(rcd, base + t + 1)
                    if later(t, 2):
                        dve.wait_ge(ot, base + t - 1)
                    nb = on[s][0:Q, :].rearrange("p (b h d) -> p b h d", b=G, d=DK)
                    ob_ = o4.rearrange("p (h b) d -> p b h d", b=G)
                    rb = rc[s].rearrange("p (h b) -> p b h", b=G)
                    for b in range(G):
                        ins = V.tensor_tensor(nb[:, b, :, :], ob_[:, b, :, 0:DK],
                                              rb[:, b, :].unsqueeze(2).broadcast_to([Q, H, DK]), ALU.mult)
                    ins.then_inc(ond, 1)
                scale(0, 0)
                scale(1, 1)

                def body(t, s, k):
                    if exists(t + 2, NT):
                        scale(t + 2, s)
                    dve.wait_ge(wod, base + t + 1)
                    if L == 1:
                        dve.wait_ge(bod, t + 1)
                    V.tensor_tensor(hs(t), hs(t), wob[s][0:W, 0:D], ALU.add).then_inc(h_out, 1)
                over(dve, NT, body, head=2, tail=2)

            @part("scalar")
            def _(act):
                c_over(act)

                def body(t, s, k):
                    act.wait_ge(ot, base + t + 1)
                    if later(t, 2):
                        act.wait_ge(wod, base + t - 1)
                    A.activation(oT[s], otb[s][:, 0:2 * W], ACT.Copy).then_inc(ote, 1)
                over(act, NT, body, head=2)

            @part("tensor")
            def _(pe):
                c_over(pe)

                def turn(t, s):
                    pe.wait_ge(ond, base + t + 1)
                    if later(t, 2):
                        pe.wait_ge(ote, base + t - 1)
                    for f in range(2):
                        for b in range(G):
                            o = f * W + b * Q
                            mm = T.transpose(otb[s][:, o:o + W],
                                             on[s][:, b * D + f * 128:b * D + (f + 1) * 128],
                                             ident_sb[0:W, 0:W])
                    mm.then_inc(ot, 1)
                turn(0, 0)

                def body(t, s, k):
                    if exists(t + 1, NT):
                        turn(t + 1, 1 - s)
                    pe.wait_ge(ote, base + t + 1)
                    if later(t, 2):
                        pe.wait_ge(h_out, t - 1)
                    for f in range(2):
                        mm = T.matmul(wob[s][0:W, 0:D], oT[s][:, f * W:(f + 1) * W], wo_sb[:, f, :],
                                      start=f == 0, stop=f == 1)
                    mm.then_inc(wod, 1)
                over(pe, NT, body, head=2, tail=1)

        def store(ready):
            @part("sync")
            def _(sp):
                sp.wait_ge(ready, NT)
                sp.wait_ge(experts_in, 16 * 12)
                sp.wait_ge(experts67_in, 64)
                sp.wait_ge(attw_in[0], 32)
                if stop not in ("tok", "attn0"):
                    sp.wait_ge(attw_in[1], 32)
                    sp.wait_ge(ffn1_in, 32)
                for t in range(NT):
                    r = min(W, B * Q - t * W)
                    sp.dma_start(out[t * W:t * W + r, :], h[0:r, t * D:(t + 1) * D]).then_inc(out_sent, 16)
                sp.wait_ge(out_sent, 16 * NT)

        def finish():
            @block.sync
            def _(sp):
                for f in progs["sync"]:
                    f(sp)

            @block.gpsimd
            def _(pool):
                for f in progs["gpsimd"]:
                    f(pool)

            @block.scalar
            def _(act):
                for f in progs["scalar"]:
                    f(act)

            @block.vector
            def _(dve):
                for f in progs["vector"]:
                    f(dve)

            @block.tensor
            def _(pe):
                for f in progs["tensor"]:
                    f(pe)

        if stop == "tok":
            store(h_tok)
            return finish()

        def tok_over(eng):
            eng.wait_ge(tok_done, NT)
            eng.wait_ge(h_tok, NT)
            eng.wait_ge(zeroed, 16 * NS)

        h_att0 = sem("h_att0")
        attention(0, h_tok, h_att0, tok_over)
        if stop == "attn0":
            store(h_att0)
            return finish()

        def route(L, h_in, n_over):
            base = L * NT
            take = area(2600)
            x1 = [take(W, D) for _ in range(2)]
            xg = [take(W, D) for _ in range(2)]
            tmp = [take(W, D) for _ in range(2)]
            xT = [take(128, 2 * W) for _ in range(2)]
            st, ag, ve, rs, n1, st2, ag2, ve2, rs2, f0, f1, hx, kept, td, te, lg, lge = (
                shared(x) for x in ("r_stats", "r_aggr", "r_veps", "r_rstd", "r_norm", "r_stats2",
                                    "r_aggr2", "r_veps2", "r_rstd2", "r_gamma", "r_rows", "r_added",
                                    "r_kept", "r_transposed", "r_rowsT", "r_logits",
                                    "r_logits_copied"))
            tb, lb = bank[4:6], bank[6:8]
            xo = xg if L == 1 else x1
            rows_ready = n1 if L == 1 else f1
            fbase = 0 if L == 0 else base

            @part("vector")
            def _(dve):
                def stat(t, s):
                    dve.wait_ge(h_in, t + 1)
                    V.bn_stats(stats[s][:, :], hs(t)).then_inc(st, 1)
                    if later(t, 2):
                        dve.wait_ge(rs, base + t - 1)
                    dve.wait_ge(st, base + t + 1)
                    carry()
                    V.bn_aggr(mv[s][:, :], stats[s][:, :]).then_inc(ag, 1)

                def norm(t, s):
                    dve.wait_ge(rs, base + t + 1)
                    if later(t, 2):
                        if L == 0:
                            dve.wait_ge(hx, t - 1)
                        else:
                            dve.wait_ge(td, base + t - 1)
                            dve.wait_ge(kept, base + t - 1)
                    V.tensor_scalar(xo[s], hs(t), mv[s][:, 0:1], rstd[s][:, :],
                                    ALU.subtract, ALU.mult).then_inc(n1, 1)
                    if L == 0:
                        dve.wait_ge(n1, t + 1)
                        V.bn_stats(stats2[s][:, :], x1[s]).then_inc(st2, 1)
                        if later(t, 2):
                            dve.wait_ge(rs2, t - 1)
                        dve.wait_ge(st2, t + 1)
                        carry()
                        V.bn_aggr(mv2[s][:, :], stats2[s][:, :]).then_inc(ag2, 1)

                def affine(t, s):
                    dve.wait_ge(rs2, t + 1)
                    V.scalar_tensor_tensor(tmp[s], x1[s], mv2[s][:, 0:1], rows_sb[:, 2, :],
                                           ALU.subtract, ALU.mult).then_inc(f0, 1)
                    dve.wait_ge(f0, t + 1)
                    if later(t, 2):
                        dve.wait_ge(td, t - 1)
                        dve.wait_ge(kept, t - 1)
                    V.scalar_tensor_tensor(xg[s], tmp[s], rstd2[s][:, :], rows_sb[:, 3, :],
                                           ALU.mult, ALU.add).then_inc(f1, 1)
                stat(0, 0)
                stat(1, 1)
                norm(0, 0)
                norm(1, 1)
                stat(2, 0)

                def body(t, s, k):
                    if L == 0:
                        affine(t, s)
                    if exists(t + 2, NT):
                        norm(t + 2, s)
                    if exists(t + 3, NT):
                        stat(t + 3, 1 - s)
                over(dve, NT, body, head=2, tail=3)

            @part("gpsimd")
            def _(pool):
                def root(t, s, m, v, r, agg, vsem, rsem, used):
                    pool.wait_ge(agg, t + 1)
                    P.tensor_tensor(v[s][:, :], m[s][:, 1:2], epsv[:, :], ALU.add).then_inc(vsem, 1)
                    pool.wait_ge(vsem, t + 1)
                    if used is not None and later(t, 2):
                        pool.wait_ge(used, t - 1)
                    P.tensor_tensor(r[s][:, :], v[s][:, :], halfneg[:, :], ALU.pow).then_inc(rsem, 1)

                def root1(t, s):
                    pool.wait_ge(ag, base + t + 1)
                    P.tensor_tensor(veps[s][:, :], mv[s][:, 1:2], epsv[:, :], ALU.add).then_inc(ve, 1)
                    pool.wait_ge(ve, base + t + 1)
                    if later(t, 2):
                        pool.wait_ge(n1, base + t - 1)
                    P.tensor_tensor(rstd[s][:, :], veps[s][:, :], halfneg[:, :], ALU.pow).then_inc(rs, 1)

                def root2(t, s):
                    root(t, s, mv2, veps2, rstd2, ag2, ve2, rs2, f1)
                root1(0, 0)
                root1(1, 1)
                if L == 0:
                    root2(0, 0)
                    root2(1, 1)
                root1(2, 0)

                def body(t, s, k):
                    if L == 0:
                        pool.wait_ge(n1, t + 1)
                        P.tensor_tensor(hs(t), hs(t), x1[s], ALU.add).then_inc(hx, 1)
                        if exists(t + 2, NT):
                            root2(t + 2, s)
                    if exists(t + 3, NT):
                        root1(t + 3, 1 - s)
                over(pool, NT, body, head=2, tail=3)

            @part("scalar")
            def _(act):
                def lcopy(t, s):
                    act.wait_ge(lg, base + t + 1)
                    A.activation(logits[:, ds(t, 1), :].rearrange("p a e -> p (a e)"), lb[s][0:W, 0:E],
                                 ACT.Copy).then_inc(lge, 1)

                def body(t, s, k):
                    act.wait_ge(rows_ready, fbase + t + 1)
                    A.activation(scr[:, ds(t * SCR, D)], xg[s], ACT.Copy).then_inc(kept, 1)
                    act.wait_ge(td, base + t + 1)
                    if later(t, 2):
                        act.wait_ge(lg, base + t - 1)
                    A.activation(xT[s], tb[s][:, 0:2 * W], ACT.Copy).then_inc(te, 1)
                    if later(t, 1):
                        lcopy(t - 1, 1 - s)
                over(act, NT, body, head=2)
                lcopy(NT - 1, (NT - 1) % 2)

            @part("tensor")
            def _(pe):
                def prod(t, s):
                    pe.wait_ge(te, base + t + 1)
                    if later(t, 2):
                        pe.wait_ge(lge, base + t - 1)
                    for c in range(2):
                        mm = T.matmul(lb[s][0:W, 0:E], xT[s][:, c * W:(c + 1) * W], router_sb[:, c, L, :],
                                      start=c == 0, stop=c == 1)
                    mm.then_inc(lg, 1)

                def body(t, s, k):
                    pe.wait_ge(rows_ready, fbase + t + 1)
                    if later(t, 2):
                        pe.wait_ge(te, base + t - 1)
                    for c in range(2):
                        mm = T.transpose(tb[s][:, c * W:(c + 1) * W], xg[s][:, c * 128:(c + 1) * 128],
                                         ident_sb[0:W, 0:W])
                    mm.then_inc(td, 1)
                    if later(t, 1):
                        prod(t - 1, 1 - s)
                over(pe, NT, body, head=2)
                prod(NT - 1, (NT - 1) % 2)

            step = shared("choice_step")
            steps = choice_steps
            to_act, from_act = shared("choice_to_act"), shared("choice_from_act")
            take = area(4600)
            n3 = lambda a: a.rearrange("p (t e) -> p t e", e=E)
            p_, u_, oh, oh2, top, idf = (take(W, NT * E) for _ in range(6))
            idx = take(W, NT * E).bitcast(u32)
            r_ = take(W, NT)
            over_t = lambda a: a.unsqueeze(2).broadcast_to([W, NT, E])

            @part("scalar")
            def _(act):
                act.wait_ge(to_act, L + 1)
                A.activation(u_, p_ if L == 0 else logits[:, :, :].rearrange("p t e -> p (t e)"),
                             ACT.Exp if L == 0 else ACT.Sigmoid).then_inc(from_act, 1)

            def link(dve, ins):
                steps[0] += 1
                ins.then_inc(step, 1)
                dve.wait_ge(step, steps[0])

            @part("vector")
            def _(dve):
                dve.wait_ge(lge, base + NT)
                if L == 0:
                    lo = logits[:, :, :].rearrange("p t e -> p (t e)")
                    link(dve, V.tensor_scalar(p_, lo, 1e4, -1e4, ALU.min, ALU.max))
                    link(dve, V.tensor_reduce(r_, n3(p_), AX.X, ALU.max))
                    V.tensor_tensor(n3(p_), n3(p_), over_t(r_), ALU.subtract).then_inc(to_act, 1)
                    dve.wait_ge(from_act, L + 1)
                    link(dve, V.tensor_reduce(r_, n3(u_), AX.X, ALU.add))
                    link(dve, V.tensor_scalar(r_, r_, 1e-8, None, ALU.add))
                    link(dve, V.reciprocal(r_, r_))
                    link(dve, V.tensor_tensor(n3(p_), n3(u_), over_t(r_), ALU.mult))
                    link(dve, V.tensor_scalar(p_, p_, 1e-8, 1.0, ALU.max, ALU.min))
                else:
                    V.memset(r_, 0.0).then_inc(to_act, 1)
                    dve.wait_ge(from_act, L + 1)
                    link(dve, V.tensor_tensor(n3(p_), n3(u_), rbias_sb[:, :].unsqueeze(1).broadcast_to([W, NT, E]),
                                              ALU.add))
                for t in range(NT):
                    ins = V.max(n3(top)[:, t, :], n3(p_)[:, t, :])
                link(dve, ins)
                for t in range(NT):
                    ins = V.max_index(n3(idx)[:, t, :], n3(top)[:, t, :], n3(p_)[:, t, :])
                link(dve, ins)
                link(dve, V.tensor_copy(idf, idx))
                for c, o in ((0, oh), (1, oh2)):
                    ins = V.tensor_tensor(n3(o), iota_sb[0:W, 0:E].unsqueeze(1).broadcast_to([W, NT, E]),
                                          n3(idf)[:, :, c].unsqueeze(2).broadcast_to([W, NT, E]), ALU.is_equal)
                link(dve, ins)

            if L == 1:
                @part("vector")
                def _(dve):
                    link(dve, V.tensor_tensor(oh, oh, oh2, ALU.add))
                    link(dve, V.tensor_tensor(oh, oh, u_, ALU.mult))
                    link(dve, V.tensor_reduce(r_, n3(oh), AX.X, ALU.add))
                    link(dve, V.tensor_scalar(r_, r_, 1e-9, None, ALU.add))
                    link(dve, V.reciprocal(r_, r_))
                    link(dve, V.tensor_tensor(cw[:, :, :], n3(oh), over_t(r_), ALU.mult))
                    V.tensor_tensor(skipw[:, :], cw[:, :, E1], cw[:, :, E1 + 2], ALU.add).then_inc(n_over, 1)
                return

            ohs = take(W, NT * E)
            cnt, ntl, cum, start = (take(128, E) for _ in range(4))
            cmp_ = take(128, E * MAXT)
            cc = take(128, E * E)
            te_c = take(1, NS * E)
            te_f = take(1, NS)
            pf = take(W, NT)
            chosen, ranked = sem("chosen"), sem("ranked")
            rank_b, count_b = bank[0], bank[1]

            @part("tensor")
            def _(pe):
                pe.wait_ge(chosen, 1)
                T.matmul(rank_b[0:W, 0:NT * E], tri_sb[:, :], ohs, start=True, stop=False,
                         skip_group_check=True)
                for t in range(NT - 1):
                    m = NT - 1 - t
                    T.matmul(rank_b[0:W, (t + 1) * E:NT * E], ones[:, 0:W],
                             n3(ohs)[:, t, :].unsqueeze(1).broadcast_to([W, m, E]),
                             start=False, stop=t == NT - 2, skip_group_check=True)
                T.matmul(count_b[:, 0:NT * E], ones[:, :], ohs, start=True, stop=True).then_inc(ranked, 1)

            @part("vector")
            def _(dve):
                V.tensor_tensor(ohs, oh, oh2, ALU.add).then_inc(chosen, 1)
                dve.wait_ge(ranked, 1)
                link(dve, V.tensor_reduce(cnt, count_b[:, 0:NT * E].rearrange("p (t e) -> p e t", e=E),
                                          AX.X, ALU.add))
                c3 = cmp_.rearrange("p (e j) -> p e j", e=E)
                link(dve, V.tensor_tensor(c3, cnt.unsqueeze(2).broadcast_to([128, E, MAXT]),
                                          thr_sb[:, :].unsqueeze(1).broadcast_to([128, E, MAXT]), ALU.is_gt))
                link(dve, V.tensor_reduce(ntl, c3, AX.X, ALU.add))
                k3 = cc.rearrange("p (e j) -> p e j", e=E)
                link(dve, V.tensor_tensor(k3, ntl.unsqueeze(1).broadcast_to([128, E, E]),
                                          cumtri_sb[:, :].rearrange("p (e j) -> p e j", e=E), ALU.mult))
                link(dve, V.tensor_reduce(cum, k3, AX.X, ALU.add))
                link(dve, V.tensor_tensor(start, cum, ntl, ALU.subtract))
                link(dve, V.tensor_scalar(start, start, float(SLOT), None, ALU.mult))
                link(dve, V.tensor_tensor(n3(p_), n3(rank_b[0:W, 0:NT * E]),
                                          start[0:W, :].unsqueeze(1).broadcast_to([W, NT, E]), ALU.add))
                for c, o in ((0, oh), (1, oh2)):
                    link(dve, V.tensor_tensor(o, o, p_, ALU.mult))
                    link(dve, V.tensor_reduce(pf, n3(o), AX.X, ALU.add))
                    link(dve, V.tensor_copy(pos_u[c][:, :], pf))
                e3 = te_c.rearrange("p (i e) -> p i e", e=E)
                link(dve, V.tensor_tensor(e3, cum[0:1, :].unsqueeze(1).broadcast_to([1, NS, E]),
                                          iota_sb[0:1, :].unsqueeze(2).broadcast_to([1, NS, E]), ALU.is_le))
                link(dve, V.tensor_reduce(te_f, e3, AX.X, ALU.add))
                link(dve, V.tensor_scalar(te_f, te_f, float(E - 1), None, ALU.min))
                V.tensor_copy(tile_expert[:, :], te_f).then_inc(n_over, 1)

            @part("scalar")
            def _(act):
                act.wait_ge(n_over, 1)

                def gate0(t, s, k):
                    A.activation(scr[:, ds(t * SCR + D, D)], scr[:, ds(t * SCR, D)], ACT.Copy,
                                 scale=top[:, ds(t * E, 1)]).then_inc(gated[0], 1)
                over(act, NT, gate0, head=1)

            @part("vector")
            def _(dve):
                dve.wait_ge(n_over, 1)

                def gate1(t, s, k):
                    V.tensor_scalar(scr[:, ds(t * SCR + 2 * D, D)], scr[:, ds(t * SCR, D)],
                                    top[:, ds(t * E + 1, 1)], None, ALU.mult).then_inc(gated[1], 1)
                over(dve, NT, gate1, head=1)

            @part("gpsimd")
            def _(pool):
                pool.wait_ge(n_over, 1)
                for t in range(NT):
                    for c in range(2):
                        pool.wait_ge(gated[c], t + 1)
                        pool.indirect_dma_start(
                            xs_d[:, :], bass.IndirectOffsetOnAxis(pos_u[c][:, t:t + 1], 0),
                            scr[:, t * SCR + (1 + c) * D:t * SCR + (2 + c) * D], None).then_inc(scattered, 16)

        def experts(L, n, rows_, begin):
            S_ = lambda x: sem(f"{x}_{L}")
            R = rows_
            take = area(0)
            xin = [take(R, D) for _ in range(2)]
            xT = [take(128, 2 * R) for _ in range(2)]
            sg = take(R, FF)
            hid = take(R, FF)
            hT = take(128, 4 * R)
            yv = [take(R, D) for _ in range(2)]
            gd, ud, t2, td, m2, te, sd, he, hd, yd = (
                S_(x) for x in ("e_gate", "e_up", "e_hidT", "e_turned", "e_down", "e_xT", "e_silu",
                                "e_hidT_copied", "e_hid", "e_y"))
            xb, gb, ub, hb, yb = bank[0:2], bank[2], bank[3], bank[4], bank[5]
            if L == 0:
                xi = [S_(f"e_x{s}") for s in range(2)]
                ys = [S_(f"e_stored{s}") for s in range(2)]
            else:
                xf = S_("e_x")
                conv_acc = [take(128, 2 * W) for _ in range(2)]
                conv_tmp = take(128, 2 * W)
                rl = [take(W, D) for _ in range(2)]
                sk = [take(W, D) for _ in range(2)]
                cv0, cvs, cvd, rls, sks, sms = (
                    S_(x) for x in ("e_tap", "e_conv_step", "e_conv", "e_relu", "e_skip", "e_sum"))
                ys = [S_(f"e_stored{s}") for s in range(2)]

            @part("sync")
            def _(sp):
                if L == 0:
                    begin(sp)

                def load(i, s):
                    if later(i, 2):
                        sp.wait_ge(td, i - 1)
                    sp.dma_start(xin[s], xs_d[ds(i * R, R), :]).then_inc(xi[s], 16)

                def put(i, s):
                    sp.wait_ge(yd, i + 1)
                    dst = ys_d[ds(i * R, R), :] if L == 0 else out[ds(i * R, R), :]
                    sp.dma_start(dst, yv[s]).then_inc(ys[s], 16)
                if L == 0:
                    load(0, 0)
                    load(1, 1)

                    def body(i, s, k):
                        if exists(i + 2, n):
                            load(i + 2, s)
                        put(i, s)
                    over(sp, n, body, head=2, tail=2)
                else:
                    over(sp, n - 1, lambda i, s, k: put(i, s), head=2)
                    sp.wait_ge(yd, n)
                    r = B * Q - (n - 1) * W
                    sp.dma_start(out[(n - 1) * W:B * Q, :], yv[(n - 1) % 2][0:r, :]).then_inc(ys[(n - 1) % 2], 16)
                    for s in range(2):
                        sp.wait_ge(ys[s], 16 * ((n + 1 - s) // 2))

            @part("scalar")
            def _(act):
                begin(act)

                def fix(t, s):
                    if later(t, 2):
                        act.wait_ge(td, t - 1)
                    A.activation(xin[s], scr[:, ds(t * SCR, D)], ACT.Copy).then_inc(xf, 1)

                def turn(i, s):
                    act.wait_ge(td, i + 1)
                    if later(i, 2):
                        act.wait_ge(ud, i - 1)
                        if L == 1:
                            act.wait_ge(cvd, i - 1)
                    A.activation(xT[s], xb[s][:, 0:2 * R], ACT.Copy).then_inc(te, 1)

                def hid_turn(i):
                    act.wait_ge(t2, i + 1)
                    if later(i, 1):
                        act.wait_ge(m2, i)
                    A.activation(hT, hb[:, 0:4 * R], ACT.Copy).then_inc(he, 1)
                if L == 1:
                    fix(0, 0)
                    fix(1, 1)
                turn(0, 0)

                def body(i, s, k):
                    if L == 1:
                        if exists(i + 2, n):
                            fix(i + 2, s)
                        act.wait_ge(te, i + 1)
                        if later(i, 2):
                            act.wait_ge(m2, i - 1)
                        for c in range(2):
                            ins = A.activation(conv_acc[s][:, c * W:(c + 1) * W], xT[s][:, c * W:(c + 1) * W],
                                               ACT.Identity, bias=conv_sb[:, c, KC:KC + 1],
                                               scale=conv_sb[:, c, KC - 1:KC])
                        ins.then_inc(cv0, 1)
                    if later(i, 1):
                        hid_turn(i - 1)
                    act.wait_ge(gd, i + 1)
                    if later(i, 1):
                        act.wait_ge(hd, i)
                    A.activation(sg, gb[0:R, :], ACT.Silu).then_inc(sd, 1)
                    if exists(i + 1, n):
                        turn(i + 1, 1 - s)
                over(act, n, body, head=2, tail=2)
                hid_turn(n - 1)

            @part("vector")
            def _(dve):
                begin(dve)

                def result(i, s):
                    if L == 1:
                        dve.wait_ge(sms, i + 1)
                    dve.wait_ge(m2, i + 1)
                    if later(i, 2):
                        dve.wait_ge(ys[s], 16 * (i // 2) if isinstance(i, int) else (i - s) * 8)
                    if L == 0:
                        V.tensor_copy(yv[s], yb[0:R, 0:D]).then_inc(yd, 1)
                    else:
                        V.tensor_tensor(yv[s], sk[s], yb[0:R, 0:D], ALU.add).then_inc(yd, 1)

                def body(i, s, k):
                    if L == 1:
                        x = scr[:, ds(i * SCR, D)]
                        cwf = cw[:, :, :].rearrange("p t e -> p (t e)")
                        if later(i, 2):
                            dve.wait_ge(sms, i - 1)
                        V.tensor_scalar(rl[s], x, 0.0, cwf[:, ds(i * E + E1 + 3, 1)],
                                        ALU.max, ALU.mult).then_inc(rls, 1)
                        if later(i, 2):
                            dve.wait_ge(yd, i - 1)
                        V.scalar_tensor_tensor(sk[s], x, skipw[:, ds(i, 1)], hs(i),
                                               ALU.mult, ALU.add).then_inc(sks, 1)
                    dve.wait_ge(ud, i + 1)
                    dve.wait_ge(sd, i + 1)
                    if later(i, 1):
                        dve.wait_ge(t2, i)
                    if L == 0:
                        V.tensor_tensor(hid, sg, ub[0:R, :], ALU.mult).then_inc(hd, 1)
                    else:
                        for e in range(E1):
                            c_ = slice(e * I1, (e + 1) * I1)
                            ins = V.scalar_tensor_tensor(hid[:, c_], sg[:, c_], cwf[:, ds(i * E + e, 1)],
                                                         ub[0:R, c_], ALU.mult, ALU.mult)
                        ins.then_inc(hd, 1)
                    if later(i, 1):
                        result(i - 1, 1 - s)
                over(dve, n, body, head=2)
                result(n - 1, (n - 1) % 2)

            if L == 1:
                @part("gpsimd")
                def _(pool):
                    begin(pool)

                    def body(t, s, k):
                        x4 = xT[s].rearrange("p (c b q) -> p c b q", c=2, b=G)
                        a4 = conv_acc[s].rearrange("p (c b q) -> p c b q", c=2, b=G)
                        m4 = conv_tmp.rearrange("p (c b q) -> p c b q", c=2, b=G)
                        pool.wait_ge(cv0, t + 1)
                        for j in range(1, KC):
                            ins = None
                            for c in range(2):
                                ins = P.tensor_tensor(
                                    m4[:, c, :, 0:Q - j], x4[:, c, :, 0:Q - j],
                                    conv_sb[:, c, KC - 1 - j:KC - j].unsqueeze(2).broadcast_to([128, G, Q - j]),
                                    ALU.mult)
                            ins.then_inc(cvs, 1)
                            pool.wait_ge(cvs, (KC - 1) * 2 * t + 2 * j - 1)
                            for c in range(2):
                                ins = P.tensor_tensor(a4[:, c, :, j:Q], a4[:, c, :, j:Q], m4[:, c, :, 0:Q - j],
                                                      ALU.add)
                            if j < KC - 1:
                                ins.then_inc(cvs, 1)
                                pool.wait_ge(cvs, (KC - 1) * 2 * t + 2 * j)
                        ins.then_inc(cvd, 1)
                        pool.wait_ge(cvd, t + 1)
                        pool.sem_inc(cvs)
                        pool.wait_ge(rls, t + 1)
                        pool.wait_ge(sks, t + 1)
                        P.tensor_tensor(sk[s], sk[s], rl[s], ALU.add).then_inc(sms, 1)
                    over(pool, n, body, head=2)

            @part("tensor")
            def _(pe):
                begin(pe)

                def expert(i):
                    if L == 1:
                        return 0
                    return pe.value_load(tile_expert[0:1, ds(i, 1)], min_val=0, max_val=E - 1)
                gu = w_gu[:, :, :].rearrange("p e n -> p (e n)")
                dn = w_dn[:, :, :].rearrange("p e n -> p (e n)")

                def turn(i, s, k):
                    if L == 0:
                        pe.wait_ge(xi[s], 16 * k + 16)
                    else:
                        pe.wait_ge(xf, i + 1)
                    if later(i, 2):
                        pe.wait_ge(te, i - 1)
                    for c in range(2):
                        mm = T.transpose(xb[s][:, c * R:(c + 1) * R], xin[s][:, c * 128:(c + 1) * 128],
                                         ident_sb[0:R, 0:R])
                    mm.then_inc(td, 1)

                def wide(i, s, e, b_, o, done):
                    for c in range(2):
                        mm = T.matmul(b_[0:R, :], xT[s][:, c * R:(c + 1) * R],
                                      gu[:, ds(e * (4 * FF) + c * 2 * FF + o, FF)], start=c == 0, stop=c == 1)
                    mm.then_inc(done, 1)

                def hid_turn(i):
                    pe.wait_ge(hd, i + 1)
                    if later(i, 1):
                        pe.wait_ge(he, i)
                    for c in range(4):
                        mm = T.transpose(hb[:, c * R:(c + 1) * R], hid[:, c * 128:(c + 1) * 128],
                                         ident_sb[0:R, 0:R])
                    mm.then_inc(t2, 1)

                def down_(i, s, e):
                    pe.wait_ge(he, i + 1)
                    if later(i, 1):
                        pe.wait_ge(yd, i)
                    if L == 1:
                        pe.wait_ge(cvd, i + 1)
                    for c in range(4):
                        mm = T.matmul(yb[0:R, 0:D], hT[:, c * R:(c + 1) * R], dn[:, ds(e * (4 * D) + c * D, D)],
                                      start=c == 0, stop=L == 0 and c == 3, skip_group_check=L == 1)
                    if L == 1:
                        for c in range(2):
                            mm = T.matmul(yb[0:R, c * 128:(c + 1) * 128], conv_acc[s][:, c * W:(c + 1) * W],
                                          ident_sb[:, :], start=False, stop=c == 1, skip_group_check=True)
                    mm.then_inc(m2, 1)
                turn(0, 0, 0)

                def body(i, s, k):
                    e_last = expert(i - 1) if later(i, 1) else None
                    e = expert(i)
                    pe.wait_ge(te, i + 1)
                    if later(i, 1):
                        pe.wait_ge(sd, i)
                    wide(i, s, e, gb, 0, gd)
                    if later(i, 1):
                        hid_turn(i - 1)
                    wide(i, s, e, ub, FF, ud)
                    if exists(i + 1, n):
                        turn(i + 1, 1 - s, k + s)
                    if later(i, 1):
                        down_(i - 1, 1 - s, e_last)
                over(pe, n, body, head=2, tail=1)
                e_last = expert(n - 1)
                hid_turn(n - 1)
                down_(n - 1, (n - 1) % 2, e_last)
            return dict(m2=m2, ys=ys, yd=yd, ud=ud, te=te, he=he, sd=sd)

        gated = [sem(f"gated{c}") for c in range(2)]
        scattered = sem("scattered")
        routed0, routed1 = sem("routed0"), sem("routed1")
        choice_steps = [0]
        route(0, h_att0, routed0)

        def sorted_ready(eng):
            eng.wait_ge(routed0, 1)
            eng.wait_ge(scattered, 16 * 2 * NT)
            eng.wait_ge(both_layers["r_added"], NT)
            eng.wait_ge(experts_in, 16 * 12)
            eng.wait_ge(experts67_in, 16 * 4)

        @part("sync")
        def _(sp):
            sp.wait_ge(both_layers["d_proj"], NT)
            sp.dma_start(wqkv_sb[:, :, :], wqkv[1]).then_inc(attw_in[1], 16)
            sp.dma_start(wo_sb[:, :, :], wo[1]).then_inc(attw_in[1], 16)

        e0 = experts(0, NS, SLOT, sorted_ready)

        def outputs_stored(eng):
            for s in range(2):
                eng.wait_ge(e0["ys"][s], 16 * ((NS + 1 - s) // 2))

        @part("sync")
        def _(sp):
            sp.wait_ge(e0["m2"], NS)
            sp.dma_start(w_gu[:, 0, :], gate_up1).then_inc(ffn1_in, 16)
            sp.dma_start(w_dn[:, 0, :], down1).then_inc(ffn1_in, 16)

        take = area(4200)
        got = [[take(W, D) for _ in range(2)] for _ in range(3)]
        got_in = [sem(f"got_in{s}") for s in range(3)]
        summed, h_ffn0 = sem("summed"), sem("h_ffn0")

        @part("gpsimd")
        def _(pool):
            outputs_stored(pool)
            for t in range(NT):
                if t >= 3:
                    pool.wait_ge(h_ffn0, t - 2)
                for c in range(2):
                    pool.indirect_dma_start(
                        got[t % 3][c], None, ys_d[:, :],
                        bass.IndirectOffsetOnAxis(pos_u[c][:, t:t + 1], 0)).then_inc(got_in[t % 3], 16)

        @part("vector")
        def _(dve):
            def body(t, s, k):
                dve.wait_ge(got_in[s], 32 * k + 32)
                V.tensor_tensor(got[s][0], got[s][0], got[s][1], ALU.add).then_inc(summed, 1)
                dve.wait_ge(summed, t + 1)
                V.tensor_tensor(hs(t), hs(t), got[s][0], ALU.add).then_inc(h_ffn0, 1)
            over(dve, NT, body, unroll=3, head=3)
        if stop == "ffn0":
            store(h_ffn0)
            return finish()

        h_att1 = sem("h_att1")
        attention(1, h_ffn0, h_att1, outputs_stored)
        if stop == "attn1":
            store(h_att1)
            return finish()
        route(1, h_att1, routed1)

        def tokens_ready(eng):
            eng.wait_ge(routed1, 1)
            eng.wait_ge(ffn1_in, 32)
        experts(1, NT, W, tokens_ready)
        finish()



def host_arrays(i):
    import numpy as np
    f = np.float32
    a = {}
    x = np.asarray(i["x"]).reshape(B, CH, SIDE, PATCH, SIDE, PATCH).transpose(0, 2, 4, 1, 3, 5)
    x = x.reshape(B, SIDE * SIDE, NF * 128)
    full = np.zeros((NT * G, Q, NF * 128), f)
    full[:B, 1:] = x
    a["patches"] = full.reshape(NT, W, NF, 128).transpose(0, 3, 2, 1).reshape(NT, 128, NF * W)
    kmaj = lambda w, c: np.asarray(w).reshape(c, 128, -1).transpose(1, 0, 2)
    a["tok_w"] = kmaj(np.asarray(i["L0_tok_W"]).T, NF).reshape(128, NF * D)
    pos = np.asarray(i["L0_tok_pos_enc"])[0]
    add = np.concatenate([np.asarray(i["L0_tok_cls_token"])[0], np.tile(np.asarray(i["L0_tok_b"])[None], (Q - 1, 1))])
    row = lambda v: np.tile(np.asarray(v)[None], (W, 1))
    a["rows"] = np.stack([np.tile(pos, (G, 1)), np.tile(add, (G, 1)), row(i["L0_ffn_ln_gamma"]),
                          row(i["L0_ffn_ln_beta"]), row(i["L1_attn_bo"])], 1)
    a["ident"] = np.eye(128, dtype=f)
    ang = np.arange(Q, dtype=f)[:, None] * (1.0 / 10000.0 ** (np.arange(0, DK, 2, dtype=f) / DK)).astype(f)
    c, s = np.cos(ang), np.sin(ang)
    a["rope"] = np.tile(np.stack([np.concatenate([c, c], 1), np.concatenate([-s, s], 1)], 1), (G, 1, 1)).astype(f)
    a["headmask"] = (np.arange(128)[:, None] // DK == np.arange(HH)[None]).astype(f)
    a["imgmask"] = (np.arange(W)[:, None] // Q == np.arange(G)[None]).astype(f)
    a["causal"] = np.tile(np.where(np.arange(Q)[None] > np.arange(Q)[:, None], f(NEG), f(0)), (1, HH)).astype(f)
    a["selq"] = (np.arange(Q)[:, None] == np.arange(128)[None] % HALF).astype(f)
    a["tri"] = (np.arange(W)[:, None] < np.arange(W)[None]).astype(f)
    a["cumtri"] = np.tile((np.arange(E)[None] <= np.arange(E)[:, None]).astype(f).reshape(1, -1), (128, 1))
    a["thresholds"] = np.tile(SLOT * np.arange(MAXT, dtype=f)[None], (128, 1))
    a["iota"] = np.tile(np.arange(NS, dtype=f)[None], (128, 1))
    halves = np.concatenate([np.arange(0, DK, 2), np.arange(1, DK, 2)])
    perm = (np.arange(H)[:, None] * DK + halves[None]).reshape(-1)
    wq, wk = (np.asarray(i[f"L0_attn_{n}"])[perm] for n in ("Wq", "Wk"))
    l0 = np.concatenate([wq.T, wk.T, np.asarray(i["L0_attn_Wv"]).T], 1)
    l1 = np.concatenate([np.asarray(i[f"L1_attn_{n}"]).T for n in ("Wq", "Wk", "Wv")], 1)
    a["wqkv"] = np.stack([kmaj(l0, 2), kmaj(l1, 2)])
    a["wo"] = np.stack([kmaj(np.asarray(i[f"L{l}_attn_Wo"]).T, 2) for l in range(2)])
    a["router"] = np.stack([kmaj(np.asarray(i["L0_ffn_router_w"]).T, 2), kmaj(i["L1_ffn_Wr"], 2)], 2)
    a["router_bias"] = row(i["L1_ffn_router_bias"])
    a["gate_up"] = np.stack([kmaj(w.T, 2).reshape(128, -1) for w in np.asarray(i["L0_ffn_gate_up_w"])])
    a["down"] = np.stack([kmaj(w.T, 4).reshape(128, -1) for w in np.asarray(i["L0_ffn_down_w"])])
    wg, wu = (np.asarray(i[f"L1_ffn_{n}"]).transpose(1, 0, 2).reshape(D, E1 * I1) for n in ("Wg", "Wu"))
    a["gate_up1"] = kmaj(np.concatenate([wg, wu], 1), 2).reshape(128, -1)
    a["down1"] = kmaj(np.asarray(i["L1_ffn_Wd"]).reshape(E1 * I1, D), 4).reshape(128, -1)
    cv = np.concatenate([np.asarray(i["L1_ffn_conv_w"])[:, 0], np.asarray(i["L1_ffn_conv_b"])[None]])
    a["conv"] = cv.T.reshape(2, 128, KC + 1).transpose(1, 0, 2)
    return {k: np.ascontiguousarray(v) for k, v in a.items()}


STOP = "all"


def kernel(**inputs):
    import numpy as np
    import concourse.bacc as bacc
    from concourse import mybir as mb
    from concourse.bass_utils import run_bass_kernel_spmd as run

    nc = bacc.Bacc("TRN2", target_bir_lowering=False, num_devices=1)
    arrays = host_arrays(inputs)
    args = {k: nc.dram_tensor(k, v.shape, mb.dt.from_np(v.dtype), kind="ExternalInput").ap() for k, v in arrays.items()}
    out = nc.dram_tensor("out", (B * Q, D), mb.dt.float32, kind="ExternalOutput").ap()
    build(nc, **args, out=out, stop=STOP)
    r = run(nc, [arrays], core_ids=[0])
    return r.results[0]["out"].reshape(B, Q, D)
```

```python
import concourse.bass as bass
from concourse import mybir
from contextlib import ExitStack

B, IMG, CH, PATCH = 32, 96, 3, 16
SIDE = IMG // PATCH
Q = SIDE * SIDE + 1
D, H, DK = 256, 16, 16
G = 3
W = G * Q
NT = -(-B // G)
NF = CH * PATCH * PATCH // 128
E = 8
FF = 512
SLOT = 128
NS = (2 * B * Q + E * (SLOT - 1)) // SLOT
MAXT = -(-B * Q // SLOT)
WL = B * Q - (NT - 1) * W
NK = 2 * NT
E1, I1 = 4, 128
KC = 4
BANK = 512
HH = H // 2
VW = G * (DK + 1)
HALF = 64
SR = HALF + Q
SC = HH * W
SCR = max(SC, H * VW)
SCALE = DK ** -0.5
EPS = 1e-5
NEG = -3.0e38


def build(nc, patches, tok_w, rows, ident, rope, headmask, imgmask, causal, selq, tri, cumtri,
          thresholds, iota, pair_tile, padding, wqkv, wo, router, router_bias, gate_up, down, gate_up1, down1, conv,
          out, stop="all"):
    fp32, bf16 = mybir.dt.float32, mybir.dt.bfloat16
    u32, i32 = mybir.dt.uint32, mybir.dt.int32
    ALU, ACT, AX = mybir.AluOpType, mybir.ActivationFunctionType, mybir.AxisListType
    ds = bass.ds
    ctx = ExitStack()

    def sb(name, shape, dt=fp32):
        return ctx.enter_context(nc.sbuf_tensor(name, shape, dt))

    def sem(name):
        return ctx.enter_context(nc.semaphore(name))

    both_layers = {}

    def shared(name):
        if name not in both_layers:
            both_layers[name] = sem(name)
        return both_layers[name]

    def later(t, depth):
        return not isinstance(t, int) or t >= depth

    def carry(column=4):
        nc.vector.memset(spare[:, column:column + 1], 0.0)

    def exists(t, n):
        return not isinstance(t, int) or t < n

    def over(eng, n, body, unroll=2, head=2, tail=0):
        for t in range(head):
            body(t, t % unroll, t // unroll)
        trips = (n - tail - head) // unroll
        if trips > 0:
            with eng.Fori(0, trips) as i:
                for u in range(unroll):
                    body(i * unroll + (head + u), (head + u) % unroll, i + (head + u) // unroll)
        else:
            trips = 0
        for t in range(head + trips * unroll, n):
            body(t, t % unroll, t // unroll)

    with ctx:
        w_gu = sb("w_gu", [128, E, 2 * 2 * FF])
        w_dn = sb("w_dn", [128, E, 4 * D])
        tokw = w_gu[:, 6, 0:NF * D]
        patch = [w_gu[:, 7, s * NF * W:(s + 1) * NF * W] for s in range(3)]
        h = sb("h", [W, NT * D])
        scr = sb("scr", [W, NT * SCR])
        v_all = sb("v_all", [W, NT * D])
        wqkv_sb = sb("wqkv_sb", [128, 2, 3 * D])
        wo_sb = sb("wo_sb", [128, 2, D])
        router_sb = sb("router_sb", [128, 2, 2, E])
        rows_sb = sb("rows_sb", [W, 5, D])
        ident_sb = sb("ident_sb", [128, 128])
        rope_sb = sb("rope_sb", [W, 2, DK])
        headmask_sb = sb("headmask_sb", [128, HH])
        imgmask_sb = sb("imgmask_sb", [W, G + 2])
        causal_f = sb("causal_f", [Q, HH * Q])
        selq_f = sb("selq_f", [Q, 128])
        causal_sb = sb("causal_sb", [Q, HH * Q], bf16)
        selq_sb = sb("selq_sb", [Q, 128], bf16)
        tri_sb = sb("tri_sb", [W, W])
        cumtri_sb = sb("cumtri_sb", [128, E * E])
        thr_sb = sb("thr_sb", [128, MAXT])
        iota_sb = sb("iota_sb", [128, SLOT])
        pair_tile_sb = sb("pair_tile_sb", [W, NK])
        padding_sb = sb("padding_sb", [128, 2, NS])
        rbias_sb = sb("rbias_sb", [W, E])
        conv_sb = sb("conv_sb", [128, 2, KC + 1])
        ones = sb("ones", [W, H])
        ones_bf = sb("ones_bf", [W, 128], bf16)
        tri_bf = sb("tri_bf", [W, W], bf16)
        halfneg = sb("halfneg", [W, 1])
        epsv = sb("epsv", [W, 1])
        spare = sb("spare", [W, 5])
        stats = [sb(f"stats{s}", [W, 6]) for s in range(2)]
        mv = [sb(f"mv{s}", [W, 2]) for s in range(2)]
        veps = [sb(f"veps{s}", [W, 1]) for s in range(2)]
        rstd = [sb(f"rstd{s}", [W, 1]) for s in range(2)]
        stats2 = [sb(f"stats2{s}", [W, 6]) for s in range(2)]
        mv2 = [sb(f"mv2{s}", [W, 2]) for s in range(2)]
        veps2 = [sb(f"veps2{s}", [W, 1]) for s in range(2)]
        rstd2 = [sb(f"rstd2{s}", [W, 1]) for s in range(2)]
        logits = sb("logits", [W, NT, E])
        cw = sb("cw", [W, NT, E])
        skipw = sb("skipw", [W, NT])
        src_u = sb("src_u", [128, NS], u32)
        dst_u = sb("dst_u", [128, NS], u32)
        first = sb("first", [128, NS])
        tile_expert = sb("tile_expert", [1, NS], i32)
        work = sb("work", [128, 6500])

        def area(first=0):
            at = [first]

            def take(rows_, cols):
                a = work[0:rows_, at[0]:at[0] + cols]
                at[0] += cols
                assert at[0] <= 6500, at
                return a
            return take

        psum = ctx.enter_context(nc.psum_tensor("psum", [128, 8 * BANK], fp32))
        bank = [psum[:, i * BANK:(i + 1) * BANK] for i in range(8)]

        consts_in = sem("consts_in")
        patch_in = [sem(f"patch_in{s}") for s in range(3)]
        tokw_in = sem("tokw_in")
        attw_in = [sem(f"attw_in{n}") for n in range(2)]
        experts_in = sem("experts_in")
        experts67_in = sem("experts67_in")
        ffn1_in = sem("ffn1_in")
        tables = sem("tables")
        pool_tables = sem("pool_tables")
        tok_done = sem("tok_done")
        h_tok = sem("h_tok")
        out_sent = sem("out_sent")

        xn_d = nc.dram_tensor("expert_inputs", (NT * W, D + 2), fp32, kind="Internal").ap()
        ys_d = nc.dram_tensor("expert_outputs", (NK * W + NS * SLOT, D), fp32, kind="Internal").ap()

        block = ctx.enter_context(nc.Block())
        progs = {"sync": [], "gpsimd": [], "scalar": [], "vector": [], "tensor": []}

        def part(engine):
            def add(f):
                progs[engine].append(f)
            return add

        hs = lambda t: h[:, ds(t * D, D)]
        V, P, A, T = nc.vector, nc.gpsimd, nc.scalar, nc.tensor

        CONSTS = [(rows_sb[:, :, :], rows), (ident_sb[:, :], ident), (rope_sb[:, :, :], rope),
                  (headmask_sb[:, :], headmask), (imgmask_sb[:, :], imgmask), (causal_f[:, :], causal),
                  (selq_f[:, :], selq), (tri_sb[:, :], tri), (cumtri_sb[:, :], cumtri),
                  (thr_sb[:, :], thresholds), (iota_sb[:, :], iota), (pair_tile_sb[:, :], pair_tile),
                  (padding_sb[:, :, :], padding), (router_sb[:, :, :, :], router),
                  (rbias_sb[:, :], router_bias), (conv_sb[:, :, :], conv)]

        @part("sync")
        def _(sp):
            sp.dma_start(tokw, tok_w).then_inc(tokw_in, 16)

            def load(t, s, k):
                if later(t, 3):
                    sp.wait_ge(tok_done, t - 2)
                sp.dma_start(patch[s], patches[ds(t, 1), :, :].rearrange("a p n -> (a p) n")).then_inc(patch_in[s], 16)
            for t in range(3):
                load(t, t, 0)
            for dst, src in CONSTS:
                sp.dma_start(dst, src).then_inc(consts_in, 16)
            sp.dma_start(wqkv_sb[:, :, :], wqkv[0]).then_inc(attw_in[0], 16)
            sp.dma_start(wo_sb[:, :, :], wo[0]).then_inc(attw_in[0], 16)
            with sp.Fori(0, (NT - 3) // 3) as i:
                for u in range(3):
                    load(i * 3 + (3 + u), u, i + 1)
            for t in range(3 + (NT - 3) // 3 * 3, NT):
                load(t, t % 3, t // 3)
            for e in range(6):
                sp.dma_start(w_gu[:, e, :], gate_up[e]).then_inc(experts_in, 16)
                sp.dma_start(w_dn[:, e, :], down[e]).then_inc(experts_in, 16)
            sp.wait_ge(tok_done, NT)
            for e in range(6, E):
                sp.dma_start(w_gu[:, e, :], gate_up[e]).then_inc(experts67_in, 16)
                sp.dma_start(w_dn[:, e, :], down[e]).then_inc(experts67_in, 16)

        @part("gpsimd")
        def _(pool):
            P.memset(ones[:, :], 1.0).then_inc(pool_tables, 1)
            P.memset(halfneg[:, :], -0.5).then_inc(pool_tables, 1)
            P.memset(epsv[:, :], EPS).then_inc(pool_tables, 1)
            P.memset(ones_bf[:, :], 1.0).then_inc(pool_tables, 1)
            pool.wait_ge(pool_tables, 4)

        @part("vector")
        def _(dve):
            dve.wait_ge(consts_in, 16 * len(CONSTS))
            V.tensor_copy(causal_sb[:, :], causal_f[:, :]).then_inc(tables, 1)
            V.tensor_copy(selq_sb[:, :], selq_f[:, :]).then_inc(tables, 1)
            V.tensor_copy(tri_bf[:, :], tri_sb[:, :]).then_inc(tables, 1)
            V.tensor_tensor(rows_sb[:, 0, :], rows_sb[:, 0, :], rows_sb[:, 1, :], ALU.add).then_inc(tables, 1)
            dve.wait_ge(tables, 4)

            def add_pos(t, s, k):
                dve.wait_ge(tok_done, t + 1)
                V.tensor_tensor(hs(t), bank[s][0:W, 0:D], rows_sb[:, 0, :], ALU.add).then_inc(h_tok, 1)
            over(dve, NT, add_pos, unroll=3, head=3)

        @part("tensor")
        def _(pe):
            pe.wait_ge(tokw_in, 16)

            def product(t, s, k):
                pe.wait_ge(patch_in[s], 16 * k + 16)
                if later(t, 3):
                    pe.wait_ge(h_tok, t - 2)
                for c in range(NF):
                    mm = T.matmul(bank[s][0:W, 0:D], patch[s][:, c * W:(c + 1) * W],
                                  tokw[:, c * D:(c + 1) * D], start=c == 0, stop=c == NF - 1)
                mm.then_inc(tok_done, 1)
            over(pe, NT, product, unroll=3, head=3)

        def attention(L, h_in, h_out, free_before, make_h=None):
            base = L * NT
            take = area()
            xn = [take(W, D) for _ in range(2)]
            xnT = [take(128, 2 * W) for _ in range(2)]
            qkf = [take(W, 2 * D) for _ in range(2)]
            cosd = [take(W, 2 * D) for _ in range(2)]
            sind = [take(W, 2 * D) for _ in range(2)]
            st, ag, ve, rs, xd, td, xe_, qkd, vd, qke, vev, cosn, sinn, roped = (
                shared(x) for x in ("a_stats", "a_aggr", "a_veps", "a_rstd", "a_xn", "a_transposed",
                                "a_xnT", "a_qk", "a_v", "a_qk_copied", "a_v_copied", "a_cos",
                                "a_sin", "a_roped"))
            tb, qkb, vb = bank[0:2], bank[2:4], bank[4:6]
            scq = lambda t: scr[:, ds(t * SCR, 2 * D)]

            @part("vector")
            def _(dve):
                free_before(dve)

                def stat(t, s):
                    if make_h:
                        make_h(dve, t, s)
                    dve.wait_ge(h_in, t + 1)
                    if make_h:
                        carry()
                    V.bn_stats(stats[s][:, :], hs(t)).then_inc(st, 1)
                    if later(t, 2):
                        dve.wait_ge(rs, base + t - 1)
                    dve.wait_ge(st, base + t + 1)
                    carry()
                    V.bn_aggr(mv[s][:, :], stats[s][:, :]).then_inc(ag, 1)

                def norm(t, s):
                    dve.wait_ge(rs, base + t + 1)
                    dve.wait_ge(ag, base + t + 1)
                    if later(t, 2):
                        dve.wait_ge(td, base + t - 1)
                    V.tensor_scalar(xn[s], hs(t), mv[s][:, 0:1], rstd[s][:, :],
                                    ALU.subtract, ALU.mult).then_inc(xd, 1)

                def rotate(t, s):
                    dve.wait_ge(sinn, base + t + 1)
                    dve.wait_ge(cosn, base + t + 1)
                    V.tensor_tensor(scq(t), cosd[s], sind[s], ALU.add).then_inc(roped, 1)

                stat(0, 0)
                stat(1, 1)
                norm(0, 0)
                norm(1, 1)
                stat(2, 0)

                def body(t, s, k):
                    if exists(t + 2, NT):
                        norm(t + 2, s)
                    if exists(t + 3, NT):
                        stat(t + 3, 1 - s)
                    dve.wait_ge(qke, base + t + 1)
                    if later(t, 2):
                        dve.wait_ge(roped, base + t - 1)
                    V.tensor_tensor(cosd[s].rearrange("p (h d) -> p h d", d=DK),
                                    qkf[s].rearrange("p (h d) -> p h d", d=DK),
                                    rope_sb[:, 0, :].unsqueeze(1).broadcast_to([W, 2 * H, DK]),
                                    ALU.mult).then_inc(cosn, 1)
                    if later(t, 1):
                        rotate(t - 1, 1 - s)
                over(dve, NT, body, head=2, tail=3 + L)
                rotate(NT - 1, (NT - 1) % 2)

            @part("gpsimd")
            def _(pool):
                free_before(pool)

                def root(t, s):
                    pool.wait_ge(ag, base + t + 1)
                    P.tensor_tensor(veps[s][:, :], mv[s][:, 1:2], epsv[:, :], ALU.add).then_inc(ve, 1)
                    pool.wait_ge(ve, base + t + 1)
                    if later(t, 2):
                        pool.wait_ge(xd, base + t - 1)
                    P.tensor_tensor(rstd[s][:, :], veps[s][:, :], halfneg[:, :], ALU.pow).then_inc(rs, 1)
                root(0, 0)
                root(1, 1)
                root(2, 0)

                def body(t, s, k):
                    if exists(t + 3, NT):
                        root(t + 3, 1 - s)
                    pool.wait_ge(qke, base + t + 1)
                    if later(t, 2):
                        pool.wait_ge(roped, base + t - 1)
                    x = qkf[s].rearrange("p (h a d) -> p h a d", a=2, d=DK // 2)
                    o = sind[s].rearrange("p (h a d) -> p h a d", a=2, d=DK // 2)
                    sn = rope_sb[:, 1, :].rearrange("p (a d) -> p a d", a=2)
                    for a in range(2):
                        ins = P.tensor_tensor(o[:, :, a, :], x[:, :, 1 - a, :],
                                              sn[:, a, :].unsqueeze(1).broadcast_to([W, 2 * H, DK // 2]),
                                              ALU.mult)
                    ins.then_inc(sinn, 1)
                over(pool, NT, body, head=2, tail=3)

            @part("scalar")
            def _(act):
                free_before(act)

                def turn(t, s):
                    act.wait_ge(td, base + t + 1)
                    if later(t, 2):
                        act.wait_ge(vd, base + t - 1)
                    A.activation(xnT[s], tb[s][:, 0:2 * W], ACT.Copy).then_inc(xe_, 1)
                turn(0, 0)

                def body(t, s, k):
                    if exists(t + 1, NT):
                        turn(t + 1, 1 - s)
                    act.wait_ge(qkd, base + t + 1)
                    if later(t, 2):
                        act.wait_ge(cosn, base + t - 1)
                        act.wait_ge(sinn, base + t - 1)
                    A.activation(qkf[s], qkb[s][0:W, 0:2 * D], ACT.Copy).then_inc(qke, 1)
                    act.wait_ge(vd, base + t + 1)
                    A.activation(v_all[:, ds(t * D, D)], vb[s][0:W, 0:D], ACT.Copy).then_inc(vev, 1)
                over(act, NT, body, head=2, tail=1)

            @part("tensor")
            def _(pe):
                free_before(pe)
                pe.wait_ge(attw_in[L], 32)
                pe.wait_ge(tables, 4)

                def turn(t, s):
                    pe.wait_ge(xd, base + t + 1)
                    if later(t, 2):
                        pe.wait_ge(xe_, base + t - 1)
                    for c in range(2):
                        mm = T.transpose(tb[s][:, c * W:(c + 1) * W], xn[s][:, c * 128:(c + 1) * 128],
                                         ident_sb[0:W, 0:W])
                    mm.then_inc(td, 1)
                turn(0, 0)

                def body(t, s, k):
                    if exists(t + 1, NT):
                        turn(t + 1, 1 - s)
                    pe.wait_ge(xe_, base + t + 1)
                    if later(t, 2):
                        pe.wait_ge(qke, base + t - 1)
                        pe.wait_ge(vev, base + t - 1)
                    for o, b_, w_, sm in ((0, qkb, 2 * D, qkd), (2 * D, vb, D, vd)):
                        for c in range(2):
                            mm = T.matmul(b_[s][0:W, 0:w_], xnT[s][:, c * W:(c + 1) * W],
                                          wqkv_sb[:, c, o:o + w_], start=c == 0, stop=c == 1)
                        mm.then_inc(sm, 1)
                over(pe, NT, body, head=2, tail=1)

            take = area()
            qks = [take(W, 2 * D) for _ in range(2)]
            qkT = [take(128, 4 * W) for _ in range(2)]
            kblk = [take(128, 2 * HH * W) for _ in range(2)]
            mx = [take(SR, G * HH) for _ in range(2)]
            cp, tr, tre, bl0, bl1, scd, mxd, sbd = (
                shared(x) for x in ("b_qk", "b_transposed", "b_qkT", "b_block0", "b_block1",
                                    "b_scores", "b_max", "b_sub"))
            tbb = bank[0:2]
            sbank = lambda s, b: bank[2 + G * s + b]
            s4 = lambda s: psum[0:SR, (2 + G * s) * BANK:(2 + G * s + G) * BANK].rearrange(
                "p (b n) -> p b n", b=G)[:, :, 0:HH * Q].rearrange("p b (h k) -> p b h k", h=HH)

            def a_over(eng):
                eng.wait_ge(roped, base + NT)
                eng.wait_ge(vev, base + NT)

            @part("scalar")
            def _(act):
                a_over(act)

                def fix(t, s):
                    if later(t, 2):
                        act.wait_ge(tr, base + t - 1)
                    A.activation(qks[s], scq(t), ACT.Copy).then_inc(cp, 1)
                fix(0, 0)
                fix(1, 1)

                def turn(t, s):
                    act.wait_ge(tr, base + t + 1)
                    if later(t, 2):
                        act.wait_ge(scd, base + t - 1)
                    A.activation(qkT[s], tbb[s][:, 0:4 * W], ACT.Copy).then_inc(tre, 1)
                turn(0, 0)

                def body(t, s, k):
                    if exists(t + 2, NT):
                        fix(t + 2, s)
                    if exists(t + 1, NT):
                        turn(t + 1, 1 - s)
                over(act, NT, body, head=2, tail=2)

            def spread(eng, t, s, f, done):
                eng.wait_ge(tre, base + t + 1)
                if later(t, 2):
                    eng.wait_ge(scd, base + t - 1)
                b4 = kblk[s][:, f * HH * W:(f + 1) * HH * W].rearrange("p (b h q) -> p b h q", b=G, h=HH)
                k3 = qkT[s][:, (2 + f) * W:(3 + f) * W].rearrange("p (b q) -> p b q", b=G)
                for b in range(G):
                    ins = eng.tensor_tensor(
                        b4[:, b, :, :], k3[:, b, :].unsqueeze(1).broadcast_to([128, HH, Q]),
                        headmask_sb[:, :].unsqueeze(2).broadcast_to([128, HH, Q]), ALU.mult)
                ins.then_inc(done, 1)

            @part("gpsimd")
            def _(pool):
                a_over(pool)
                over(pool, NT, lambda t, s, k: spread(pool, t, s, 1, bl1), head=2)

            @part("vector")
            def _(dve):
                a_over(dve)
                spread(dve, 0, 0, 0, bl0)

                def body(t, s, k):
                    if exists(t + 1, NT):
                        spread(dve, t + 1, 1 - s, 0, bl0)
                    dve.wait_ge(scd, base + t + 1)
                    V.tensor_reduce(mx[s], s4(s), AX.X, ALU.max).then_inc(mxd, 1)
                    dve.wait_ge(mxd, base + t + 1)
                    m3 = mx[s].rearrange("p (b h) -> p b h", b=G)
                    o4 = scr[0:SR, ds(t * SCR, SC)].rearrange("p (h b k) -> p b h k", h=HH, b=G)
                    for b in range(G):
                        ins = V.tensor_tensor(o4[:, b, :, :], s4(s)[:, b, :, :],
                                              m3[:, b, :].unsqueeze(2).broadcast_to([SR, HH, Q]), ALU.subtract)
                    ins.then_inc(sbd, 1)
                over(dve, NT, body, head=2, tail=1)

            @part("tensor")
            def _(pe):
                a_over(pe)

                def turn(t, s):
                    pe.wait_ge(cp, base + t + 1)
                    if later(t, 2):
                        pe.wait_ge(tre, base + t - 1)
                    for c in range(4):
                        mm = T.transpose(tbb[s][:, c * W:(c + 1) * W], qks[s][:, c * 128:(c + 1) * 128],
                                         ident_sb[0:W, 0:W])
                    mm.then_inc(tr, 1)
                turn(0, 0)

                def body(t, s, k):
                    if exists(t + 1, NT):
                        turn(t + 1, 1 - s)
                    if later(t, 2):
                        pe.wait_ge(sbd, base + t - 1)
                    for b in range(G):
                        T.matmul(sbank(s, b)[:, 0:HH * Q], selq_sb[:, :], causal_sb[:, :],
                                 start=True, stop=False, skip_group_check=True)
                    for f, blocks in ((0, bl0), (1, bl1)):
                        pe.wait_ge(blocks, base + t + 1)
                        for b in range(G):
                            k0 = (f * G + b) * HH * Q
                            mm = T.matmul(sbank(s, b)[f * HALF:f * HALF + Q, 0:HH * Q],
                                          qkT[s][:, f * W + b * Q:f * W + (b + 1) * Q],
                                          kblk[s][:, k0:k0 + HH * Q],
                                          start=False, stop=f == 1, skip_group_check=True)
                    mm.then_inc(scd, 1)
                over(pe, NT, body, head=2, tail=1)

            take = area()
            pr = [take(SR, SC) for _ in range(2)]
            prT = [take(W, HH * 128) for _ in range(2)]
            vblk = [take(W, H * VW) for _ in range(2)]
            rc = [take(Q, HH * G) for _ in range(2)]
            ex, pt, pte0, pte1, vb_, pv0, pv1, rc0, rc1, oe0, oe1, vone = (
                shared(x) for x in ("c_exp", "c_transposed", "c_prT0", "c_prT1", "c_vblock", "c_out0",
                                "c_out1", "c_recip0", "c_recip1", "c_scaled0", "c_scaled1", "c_ones"))
            pte, pvd, rcd, oed = (pte0, pte1), (pv0, pv1), (rc0, rc1), (oe0, oe1)
            tpb = lambda s, f: bank[2 * s + f]
            ob = lambda s, f: bank[4 + 2 * s + f]

            def b_over(eng):
                eng.wait_ge(sbd, base + NT)

            def copy_prT(eng, fn, t, s, f):
                eng.wait_ge(pt, base + t + 1)
                if later(t, 2):
                    eng.wait_ge(pv1, base + t - 1)
                n3 = lambda a: a.rearrange("p (h q) -> p h q", q=128)[:, :, 0:SR]
                fn(n3(prT[s][:, f * 512:(f + 1) * 512]), n3(tpb(s, f)[0:W, :])).then_inc(pte[f], 1)

            def blocks(t, s, f):
                return ob(s, f)[0:Q, 0:HH * VW].rearrange("p (h b d) -> p h b d", h=HH, b=G)

            def recip(dve, t, s, f):
                dve.wait_ge(pvd[f], base + t + 1)
                if later(t, 1):
                    dve.wait_ge(oed[f], base + t)
                V.reciprocal(rc[f].rearrange("p (h b) -> p h b", h=HH),
                             blocks(t, s, f)[:, :, :, DK]).then_inc(rcd[f], 1)

            def scale(dve, t, s, f):
                dve.wait_ge(rcd[f], base + t + 1)
                o4 = scr[0:Q, ds(t * SCR, G * D)].rearrange("p (b h d) -> p h b d", b=G, d=DK)
                V.tensor_tensor(o4[:, f * HH:(f + 1) * HH, :, :], blocks(t, s, f)[:, :, :, 0:DK],
                                rc[f].rearrange("p (h b) -> p h b", h=HH).unsqueeze(3).broadcast_to([Q, HH, G, DK]),
                                ALU.mult).then_inc(oed[f], 1)

            act_copy = lambda o, i: A.activation(o, i, ACT.Copy)
            dve_copy = lambda o, i: V.tensor_copy(o, i)

            @part("scalar")
            def _(act):
                b_over(act)

                def expo(t, s):
                    if later(t, 2):
                        act.wait_ge(pt, base + t - 1)
                    A.activation(pr[s], scr[0:SR, ds(t * SCR, SC)], ACT.Exp, scale=SCALE).then_inc(ex, 1)
                expo(0, 0)
                expo(1, 1)
                copy_prT(act, act_copy, 0, 0, 0)

                def body(t, s, k):
                    if exists(t + 2, NT):
                        expo(t + 2, s)
                    if exists(t + 1, NT):
                        copy_prT(act, act_copy, t + 1, 1 - s, 0)
                over(act, NT, body, head=2, tail=2)

            @part("vector")
            def _(dve):
                b_over(dve)
                copy_prT(dve, dve_copy, 0, 0, 1)

                def body(t, s, k):
                    recip(dve, t, s, 0)
                    if exists(t + 1, NT):
                        copy_prT(dve, dve_copy, t + 1, 1 - s, 1)
                    dve.wait_ge(ex, base + t + 1)
                    scale(dve, t, s, 0)
                    recip(dve, t, s, 1)
                    scale(dve, t, s, 1)
                over(dve, NT, body, head=2, tail=1)

            @part("gpsimd")
            def _(pool):
                b_over(pool)
                v4 = lambda s: vblk[s].rearrange("p (h b d) -> p h b d", h=H, b=G)
                for s in range(2):
                    for b in range(G):
                        ins = P.tensor_scalar(v4(s)[:, :, b, DK], ones[:, 0:H], imgmask_sb[:, b:b + 1],
                                              None, ALU.mult)
                ins.then_inc(vone, 1)

                def body(t, s, k):
                    if later(t, 2):
                        pool.wait_ge(pv1, base + t - 1)
                    for b in range(G):
                        ins = P.tensor_tensor(v4(s)[:, :, b, 0:DK],
                                              v_all[:, ds(t * D, D)].rearrange("p (h d) -> p h d", d=DK),
                                              imgmask_sb[:, b:b + 1].unsqueeze(2).broadcast_to([W, H, DK]),
                                              ALU.mult)
                    ins.then_inc(vb_, 1)
                over(pool, NT, body, head=2)

            @part("tensor")
            def _(pe):
                b_over(pe)

                def turn(t, s):
                    pe.wait_ge(ex, base + t + 1)
                    if later(t, 2):
                        pe.wait_ge(pte0, base + t - 1)
                        pe.wait_ge(pte1, base + t - 1)
                    for j in range(HH):
                        mm = T.transpose(tpb(s, j // 4)[0:W, (j % 4) * 128:(j % 4) * 128 + SR],
                                         pr[s][:, j * W:(j + 1) * W], ident_sb[0:SR, 0:SR])
                    mm.then_inc(pt, 1)
                turn(0, 0)
                pe.wait_ge(vone, L + 1)

                def body(t, s, k):
                    if exists(t + 1, NT):
                        turn(t + 1, 1 - s)
                    pe.wait_ge(vb_, base + t + 1)
                    pe.wait_ge(pte0, base + t + 1)
                    pe.wait_ge(pte1, base + t + 1)
                    for f in range(2):
                        if later(t, 2):
                            pe.wait_ge(oed[f], base + t - 1)
                        for hd in range(HH):
                            p0 = hd * 128 + f * HALF
                            v0 = (f * HH + hd) * VW
                            mm = T.matmul(ob(s, f)[0:Q, hd * VW:(hd + 1) * VW], prT[s][:, p0:p0 + Q],
                                          vblk[s][:, v0:v0 + VW], start=True, stop=True)
                        mm.then_inc(pvd[f], 1)
                over(pe, NT, body, head=2, tail=1)

            take = area()
            on = [take(W, G * D) for _ in range(2)]
            oT = [take(128, 2 * W) for _ in range(2)]
            clr, ond, ot, ote, wod, bod = (
                shared(x) for x in ("d_clear", "d_out", "d_transposed", "d_outT", "d_proj", "d_bias"))
            otb, wob = bank[0:2], bank[2:4]

            def c_over(eng):
                eng.wait_ge(oe0, base + NT)
                eng.wait_ge(oe1, base + NT)

            @part("gpsimd")
            def _(pool):
                c_over(pool)
                if L == 1:
                    over(pool, NT, lambda t, s, k: P.tensor_tensor(
                        hs(t), hs(t), rows_sb[:, 4, :], ALU.add).then_inc(bod, 1), head=2)

            @part("vector")
            def _(dve):
                c_over(dve)
                for s in range(2):
                    V.memset(on[s], 0.0).then_inc(clr, 1)

                def body(t, s, k):
                    dve.wait_ge(wod, base + t + 1)
                    if L == 1:
                        dve.wait_ge(bod, t + 1)
                    V.tensor_tensor(hs(t), hs(t), wob[s][0:W, 0:D], ALU.add).then_inc(h_out, 1)
                over(dve, NT, body, head=2)

            @part("scalar")
            def _(act):
                c_over(act)
                act.wait_ge(clr, 2 * L + 2)

                def fix(t, s):
                    if later(t, 2):
                        act.wait_ge(ot, base + t - 1)
                    A.activation(on[s][0:Q, :], scr[0:Q, ds(t * SCR, G * D)], ACT.Copy).then_inc(ond, 1)
                fix(0, 0)
                fix(1, 1)

                def body(t, s, k):
                    act.wait_ge(ot, base + t + 1)
                    if later(t, 2):
                        act.wait_ge(wod, base + t - 1)
                    A.activation(oT[s], otb[s][:, 0:2 * W], ACT.Copy).then_inc(ote, 1)
                    if exists(t + 2, NT):
                        fix(t + 2, s)
                over(act, NT, body, head=2, tail=2)

            @part("tensor")
            def _(pe):
                c_over(pe)

                def turn(t, s):
                    pe.wait_ge(ond, base + t + 1)
                    if later(t, 2):
                        pe.wait_ge(ote, base + t - 1)
                    for f in range(2):
                        for b in range(G):
                            o = f * W + b * Q
                            mm = T.transpose(otb[s][:, o:o + W],
                                             on[s][:, b * D + f * 128:b * D + (f + 1) * 128],
                                             ident_sb[0:W, 0:W])
                    mm.then_inc(ot, 1)
                turn(0, 0)

                def body(t, s, k):
                    if exists(t + 1, NT):
                        turn(t + 1, 1 - s)
                    pe.wait_ge(ote, base + t + 1)
                    if later(t, 2):
                        pe.wait_ge(h_out, t - 1)
                    for f in range(2):
                        mm = T.matmul(wob[s][0:W, 0:D], oT[s][:, f * W:(f + 1) * W], wo_sb[:, f, :],
                                      start=f == 0, stop=f == 1)
                    mm.then_inc(wod, 1)
                over(pe, NT, body, head=2, tail=1)

        def store(ready):
            @part("sync")
            def _(sp):
                sp.wait_ge(ready, NT)
                sp.wait_ge(experts_in, 16 * 12)
                sp.wait_ge(experts67_in, 64)
                sp.wait_ge(attw_in[0], 32)
                if stop not in ("tok", "attn0"):
                    sp.wait_ge(attw_in[1], 32)
                    sp.wait_ge(ffn1_in, 32)
                for t in range(NT):
                    r = min(W, B * Q - t * W)
                    sp.dma_start(out[t * W:t * W + r, :], h[0:r, t * D:(t + 1) * D]).then_inc(out_sent, 16)
                sp.wait_ge(out_sent, 16 * NT)

        def finish():
            @block.sync
            def _(sp):
                for f in progs["sync"]:
                    f(sp)

            @block.gpsimd
            def _(pool):
                for f in progs["gpsimd"]:
                    f(pool)

            @block.scalar
            def _(act):
                for f in progs["scalar"]:
                    f(act)

            @block.vector
            def _(dve):
                for f in progs["vector"]:
                    f(dve)

            @block.tensor
            def _(pe):
                for f in progs["tensor"]:
                    f(pe)

        if stop == "tok":
            store(h_tok)
            return finish()

        def tok_over(eng):
            eng.wait_ge(tok_done, NT)
            eng.wait_ge(h_tok, NT)

        h_att0 = sem("h_att0")
        attention(0, h_tok, h_att0, tok_over)
        if stop == "attn0":
            store(h_att0)
            return finish()

        def route(L, h_in, n_over):
            base = L * NT
            take = area(2600)
            x1 = [take(W, D) for _ in range(2)]
            xg = [take(W, D) for _ in range(2)]
            tmp = take(W, D)
            xT = [take(128, 2 * W) for _ in range(2)]
            st, ag, ve, rs, n1, st2, ag2, ve2, rs2, f0, f1, hx, kept, td, te, lg, lge = (
                shared(x) for x in ("r_stats", "r_aggr", "r_veps", "r_rstd", "r_norm", "r_stats2",
                                    "r_aggr2", "r_veps2", "r_rstd2", "r_gamma", "r_rows", "r_added",
                                    "r_kept", "r_transposed", "r_rowsT", "r_logits",
                                    "r_logits_copied"))
            tb, lb = bank[4:6], bank[6:8]
            xo = xg if L == 1 else x1
            rows_ready = n1 if L == 1 else f1
            fbase = 0 if L == 0 else base

            @part("vector")
            def _(dve):
                def stat(t, s):
                    dve.wait_ge(h_in, t + 1)
                    if later(t, 2):
                        dve.wait_ge(ag, base + t - 1)
                    V.bn_stats(stats[s][:, :], hs(t)).then_inc(st, 1)

                def aggr(t, s):
                    if later(t, 2):
                        dve.wait_ge(rs, base + t - 1)
                        dve.wait_ge(n1, base + t - 1)
                    dve.wait_ge(st, base + t + 1)
                    carry(s)
                    V.bn_aggr(mv[s][:, :], stats[s][:, :]).then_inc(ag, 1)

                def norm(t, s):
                    dve.wait_ge(rs, base + t + 1)
                    if later(t, 2):
                        if L == 0:
                            dve.wait_ge(hx, t - 1)
                            dve.wait_ge(f0, t - 1)
                        else:
                            dve.wait_ge(td, base + t - 1)
                            dve.wait_ge(kept, base + t - 1)
                    V.tensor_scalar(xo[s], hs(t), mv[s][:, 0:1], rstd[s][:, :],
                                    ALU.subtract, ALU.mult).then_inc(n1, 1)

                def stat2(t, s):
                    dve.wait_ge(n1, t + 1)
                    V.bn_stats(stats2[s][:, :], x1[s]).then_inc(st2, 1)

                def aggr2(t, s):
                    if later(t, 2):
                        dve.wait_ge(rs2, t - 1)
                    dve.wait_ge(st2, t + 1)
                    carry(2 + s)
                    V.bn_aggr(mv2[s][:, :], stats2[s][:, :]).then_inc(ag2, 1)

                def affine0(t, s):
                    if later(t, 1):
                        dve.wait_ge(f1, t)
                    dve.wait_ge(rs2, t + 1)
                    V.scalar_tensor_tensor(tmp, x1[s], mv2[s][:, 0:1], rows_sb[:, 2, :],
                                           ALU.subtract, ALU.mult).then_inc(f0, 1)

                def affine1(t, s):
                    dve.wait_ge(f0, t + 1)
                    if later(t, 2):
                        dve.wait_ge(td, t - 1)
                        dve.wait_ge(kept, t - 1)
                    V.scalar_tensor_tensor(xg[s], tmp, rstd2[s][:, :], rows_sb[:, 3, :],
                                           ALU.mult, ALU.add).then_inc(f1, 1)
                stat(0, 0)
                stat(1, 1)
                aggr(0, 0)
                aggr(1, 1)
                stat(2, 0)
                stat(3, 1)
                norm(0, 0)
                norm(1, 1)
                aggr(2, 0)
                if L == 0:
                    stat2(0, 0)
                    stat2(1, 1)
                    aggr2(0, 0)
                    aggr2(1, 1)

                def body(t, s, k):
                    if L == 0:
                        affine0(t, s)
                    if exists(t + 3, NT):
                        aggr(t + 3, 1 - s)
                    if exists(t + 2, NT):
                        norm(t + 2, s)
                    if L == 0:
                        affine1(t, s)
                        if exists(t + 2, NT):
                            stat2(t + 2, s)
                    if exists(t + 4, NT):
                        stat(t + 4, s)
                    if L == 0 and exists(t + 2, NT):
                        aggr2(t + 2, s)
                over(dve, NT, body, head=2, tail=4)

            @part("gpsimd")
            def _(pool):
                def root(t, s):
                    pool.wait_ge(ag, base + t + 1)
                    P.tensor_tensor(veps[s][:, :], mv[s][:, 1:2], epsv[:, :], ALU.add).then_inc(ve, 1)
                    pool.wait_ge(ve, base + t + 1)
                    if later(t, 2):
                        pool.wait_ge(n1, base + t - 1)
                    P.tensor_tensor(rstd[s][:, :], veps[s][:, :], halfneg[:, :], ALU.pow).then_inc(rs, 1)

                def root2(t, s):
                    pool.wait_ge(ag2, t + 1)
                    P.tensor_tensor(veps2[s][:, :], mv2[s][:, 1:2], epsv[:, :], ALU.add).then_inc(ve2, 1)
                    pool.wait_ge(ve2, t + 1)
                    if later(t, 2):
                        pool.wait_ge(f1, t - 1)
                    P.tensor_tensor(rstd2[s][:, :], veps2[s][:, :], halfneg[:, :], ALU.pow).then_inc(rs2, 1)

                def add(t, s):
                    pool.wait_ge(n1, t + 1)
                    P.tensor_tensor(hs(t), hs(t), x1[s], ALU.add).then_inc(hx, 1)
                root(0, 0)
                root(1, 1)
                root(2, 0)
                if L == 0:
                    root2(0, 0)
                    root2(1, 1)
                    add(0, 0)

                def body(t, s, k):
                    if L == 0 and exists(t + 1, NT):
                        add(t + 1, 1 - s)
                    if exists(t + 3, NT):
                        root(t + 3, 1 - s)
                    if L == 0 and exists(t + 2, NT):
                        root2(t + 2, s)
                over(pool, NT, body, head=2, tail=3)

            @part("scalar")
            def _(act):
                def lcopy(t, s):
                    act.wait_ge(lg, base + t + 1)
                    A.activation(logits[:, ds(t, 1), :].rearrange("p a e -> p (a e)"), lb[s][0:W, 0:E],
                                 ACT.Copy).then_inc(lge, 1)

                def body(t, s, k):
                    act.wait_ge(rows_ready, fbase + t + 1)
                    A.activation(scr[:, ds(t * SCR, D)], xg[s], ACT.Copy).then_inc(kept, 1)
                    act.wait_ge(td, base + t + 1)
                    if later(t, 2):
                        act.wait_ge(lg, base + t - 1)
                    A.activation(xT[s], tb[s][:, 0:2 * W], ACT.Copy).then_inc(te, 1)
                    if later(t, 1):
                        lcopy(t - 1, 1 - s)
                over(act, NT, body, head=2)
                lcopy(NT - 1, (NT - 1) % 2)

            @part("tensor")
            def _(pe):
                def prod(t, s):
                    pe.wait_ge(te, base + t + 1)
                    if later(t, 2):
                        pe.wait_ge(lge, base + t - 1)
                    for c in range(2):
                        mm = T.matmul(lb[s][0:W, 0:E], xT[s][:, c * W:(c + 1) * W], router_sb[:, c, L, :],
                                      start=c == 0, stop=c == 1)
                    mm.then_inc(lg, 1)

                def body(t, s, k):
                    pe.wait_ge(rows_ready, fbase + t + 1)
                    if later(t, 2):
                        pe.wait_ge(te, base + t - 1)
                    for c in range(2):
                        mm = T.transpose(tb[s][:, c * W:(c + 1) * W], xg[s][:, c * 128:(c + 1) * 128],
                                         ident_sb[0:W, 0:W])
                    mm.then_inc(td, 1)
                    if later(t, 1):
                        prod(t - 1, 1 - s)
                over(pe, NT, body, head=2)
                prod(NT - 1, (NT - 1) % 2)

            step = shared("choice_step")
            steps = choice_steps
            to_act, from_act = shared("choice_to_act"), shared("choice_from_act")
            take = area(4600)
            n3 = lambda a: a.rearrange("p (t e) -> p t e", e=E)
            p_, u_, oh, oh2, top, idf = (take(W, NT * E) for _ in range(6))
            idx = take(W, NT * E).bitcast(u32)
            r_ = take(W, NT)
            over_t = lambda a: a.unsqueeze(2).broadcast_to([W, NT, E])

            @part("scalar")
            def _(act):
                act.wait_ge(to_act, L + 1)
                A.activation(u_, p_ if L == 0 else logits[:, :, :].rearrange("p t e -> p (t e)"),
                             ACT.Exp if L == 0 else ACT.Sigmoid).then_inc(from_act, 1)

            def link(dve, ins):
                steps[0] += 1
                ins.then_inc(step, 1)
                dve.wait_ge(step, steps[0])

            @part("vector")
            def _(dve):
                dve.wait_ge(lge, base + NT)
                if L == 0:
                    lo = logits[:, :, :].rearrange("p t e -> p (t e)")
                    link(dve, V.tensor_scalar(p_, lo, 1e4, -1e4, ALU.min, ALU.max))
                    link(dve, V.tensor_reduce(r_, n3(p_), AX.X, ALU.max))
                    V.tensor_tensor(n3(p_), n3(p_), over_t(r_), ALU.subtract).then_inc(to_act, 1)
                    dve.wait_ge(from_act, L + 1)
                    link(dve, V.tensor_reduce(r_, n3(u_), AX.X, ALU.add))
                    link(dve, V.tensor_scalar(r_, r_, 1e-8, None, ALU.add))
                    link(dve, V.reciprocal(r_, r_))
                    link(dve, V.tensor_tensor(n3(p_), n3(u_), over_t(r_), ALU.mult))
                    link(dve, V.tensor_scalar(p_, p_, 1e-8, 1.0, ALU.max, ALU.min))
                else:
                    V.memset(r_, 0.0).then_inc(to_act, 1)
                    dve.wait_ge(from_act, L + 1)
                    link(dve, V.tensor_tensor(n3(p_), n3(u_), rbias_sb[:, :].unsqueeze(1).broadcast_to([W, NT, E]),
                                              ALU.add))
                for t in range(NT):
                    ins = V.max(n3(top)[:, t, :], n3(p_)[:, t, :])
                link(dve, ins)
                for t in range(NT):
                    ins = V.max_index(n3(idx)[:, t, :], n3(top)[:, t, :], n3(p_)[:, t, :])
                link(dve, ins)
                link(dve, V.tensor_copy(idf, idx))
                for c, o in ((0, oh), (1, oh2)):
                    ins = V.tensor_tensor(n3(o), iota_sb[0:W, 0:E].unsqueeze(1).broadcast_to([W, NT, E]),
                                          n3(idf)[:, :, c].unsqueeze(2).broadcast_to([W, NT, E]), ALU.is_equal)
                link(dve, ins)

            if L == 1:
                @part("vector")
                def _(dve):
                    link(dve, V.tensor_tensor(oh, oh, oh2, ALU.add))
                    link(dve, V.tensor_tensor(oh, oh, u_, ALU.mult))
                    link(dve, V.tensor_reduce(r_, n3(oh), AX.X, ALU.add))
                    link(dve, V.tensor_scalar(r_, r_, 1e-9, None, ALU.add))
                    link(dve, V.reciprocal(r_, r_))
                    link(dve, V.tensor_tensor(cw[:, :, :], n3(oh), over_t(r_), ALU.mult))
                    V.tensor_tensor(skipw[:, :], cw[:, :, E1], cw[:, :, E1 + 2], ALU.add).then_inc(n_over, 1)
                return

            ohs = take(W, NT * E).bitcast(bf16)[:, 0:NT * E]
            cnt, ntl, cum, start = (take(128, E) for _ in range(4))
            cmp_ = take(128, E * MAXT)
            cc = take(128, E * E)
            te_c = take(1, NS * E)
            te_f = take(1, NS)
            pos = take(W, NK)
            pos_i = take(W, NK).bitcast(i32)
            part_i = take(W, 2 * NK).bitcast(i32)
            part_f = take(W, 2 * NK)
            take = area(0)
            slot_oh = take(W, NK * SLOT // 2).bitcast(bf16)
            tile_oh = take(W, NK * NS)
            marks = take(W, NK * 3 * NS // 2).bitcast(bf16)
            origin = take(128, 3 * NS)
            row1, row, moved, real = (take(128, NS) for _ in range(4))
            chosen, ranked, slots0, slots1, marked, pool_marked, found = (
                sem(x) for x in ("chosen", "ranked", "slots0", "slots1", "marked", "pool_marked", "found"))
            slots = (slots0, slots1)
            rank_b, count_b, origin_b = bank[0], bank[1], bank[2]

            @part("sync")
            def _(sp):
                def keep(t, s, k):
                    sp.wait_ge(kept, t + 1)
                    sp.dma_start(xn_d[ds(t * W, W), 0:D], scr[:, ds(t * SCR, D)]).then_inc(rows_out, 16)
                over(sp, NT, keep, head=2)
                sp.wait_ge(chosen, 1)
                sp.dma_start(xn_d[:, D:D + 2].rearrange("(t p) g -> p t g", p=W),
                             n3(top)[:, :, 0:2]).then_inc(rows_out, 16)

            @part("tensor")
            def _(pe):
                pe.wait_ge(chosen, 1)
                T.matmul(rank_b[0:W, 0:NT * E], tri_bf[:, :], ohs, start=True, stop=False,
                         skip_group_check=True)
                for t in range(NT - 1):
                    m = NT - 1 - t
                    T.matmul(rank_b[0:W, (t + 1) * E:NT * E], ones_bf[:, 0:W],
                             n3(ohs)[:, t, :].unsqueeze(1).broadcast_to([W, m, E]),
                             start=False, stop=t == NT - 2, skip_group_check=True)
                T.matmul(count_b[:, 0:NT * E], ones_bf[:, :], ohs, start=True, stop=True).then_inc(ranked, 1)
                pe.wait_ge(marked, 1)
                pe.wait_ge(pool_marked, 1)
                for k in range(NK):
                    if k % NT == 0:
                        pe.wait_ge(slots[k // NT], 1)
                    mm = T.matmul(origin_b[:, 0:3 * NS], slot_oh[:, k * SLOT:(k + 1) * SLOT],
                                  marks[:, k * 3 * NS:(k + 1) * 3 * NS], start=k == 0, stop=k == NK - 1)
                mm.then_inc(found, 1)

            def slot_marks(c):
                o3 = slot_oh.rearrange("p (k m) -> p k m", m=SLOT)[:, c * NT:(c + 1) * NT, :]
                V.tensor_tensor(
                    o3, iota_sb[0:W, :].unsqueeze(1).broadcast_to([W, NT, SLOT]),
                    part_f[:, NK + c * NT:NK + (c + 1) * NT].unsqueeze(2).broadcast_to([W, NT, SLOT]),
                    ALU.is_equal).then_inc(slots[c], 1)

            @part("gpsimd")
            def _(pool):
                m4 = marks.rearrange("p (k g i) -> p k g i", g=3, i=NS)
                t3 = tile_oh.rearrange("p (k i) -> p k i", i=NS)
                pool.wait_ge(chosen, 1)
                pool.wait_ge(hx, NT)
                P.memset(m4[:, NT:NK, 2, :], 0.0)
                pool.wait_ge(placed, 1)
                P.tensor_tensor(m4[:, :, 1, :], t3, pair_tile_sb[:, :].unsqueeze(2).broadcast_to([W, NK, NS]),
                                ALU.mult).then_inc(pool_marked, 1)

            @part("vector")
            def _(dve):
                for o in (oh, oh2):
                    ins = V.tensor_scalar(n3(o)[:, NT - 1, :], n3(o)[:, NT - 1, :], imgmask_sb[:, G:G + 1],
                                          None, ALU.mult)
                link(dve, ins)
                V.tensor_tensor(ohs, oh, oh2, ALU.add).then_inc(chosen, 1)
                dve.wait_ge(ranked, 1)
                dve.wait_ge(hx, NT)
                link(dve, V.tensor_reduce(cnt, count_b[:, 0:NT * E].rearrange("p (t e) -> p e t", e=E),
                                          AX.X, ALU.add))
                c3 = cmp_.rearrange("p (e j) -> p e j", e=E)
                link(dve, V.tensor_tensor(c3, cnt.unsqueeze(2).broadcast_to([128, E, MAXT]),
                                          thr_sb[:, :].unsqueeze(1).broadcast_to([128, E, MAXT]), ALU.is_gt))
                link(dve, V.tensor_reduce(ntl, c3, AX.X, ALU.add))
                k3 = cc.rearrange("p (e j) -> p e j", e=E)
                link(dve, V.tensor_tensor(k3, ntl.unsqueeze(1).broadcast_to([128, E, E]),
                                          cumtri_sb[:, :].rearrange("p (e j) -> p e j", e=E), ALU.mult))
                link(dve, V.tensor_reduce(cum, k3, AX.X, ALU.add))
                link(dve, V.tensor_tensor(start, cum, ntl, ALU.subtract))
                link(dve, V.tensor_scalar(start, start, float(SLOT), None, ALU.mult))
                link(dve, V.tensor_tensor(n3(p_), n3(rank_b[0:W, 0:NT * E]),
                                          start[0:W, :].unsqueeze(1).broadcast_to([W, NT, E]), ALU.add))
                for o in (oh, oh2):
                    ins = V.tensor_tensor(o, o, p_, ALU.mult)
                link(dve, ins)
                for c, o in ((0, oh), (1, oh2)):
                    ins = V.tensor_reduce(pos[:, c * NT:(c + 1) * NT], n3(o), AX.X, ALU.add)
                link(dve, ins)
                link(dve, V.tensor_copy(pos_i, pos))
                V.tensor_scalar(part_i[:, 0:NK], pos_i, SLOT.bit_length() - 1, None, ALU.logical_shift_right)
                link(dve, V.tensor_scalar(part_i[:, NK:2 * NK], pos_i, SLOT - 1, None, ALU.bitwise_and))
                link(dve, V.tensor_copy(part_f, part_i))
                t3 = tile_oh.rearrange("p (k i) -> p k i", i=NS)
                link(dve, V.tensor_tensor(t3, iota_sb[0:W, 0:NS].unsqueeze(1).broadcast_to([W, NK, NS]),
                                          part_f[:, 0:NK].unsqueeze(2).broadcast_to([W, NK, NS]), ALU.is_equal))
                for c in range(2):
                    o = t3[:, (c + 1) * NT - 1, :]
                    ins = V.tensor_scalar(o, o, imgmask_sb[:, G:G + 1], None, ALU.mult)
                ins.then_inc(placed, 1)
                dve.wait_ge(placed, 1)
                m4 = marks.rearrange("p (k g i) -> p k g i", g=3, i=NS)
                V.tensor_scalar(m4[:, :, 0, :], t3, imgmask_sb[:, G + 1:G + 2], None, ALU.mult)
                V.tensor_copy(m4[:, 0:NT, 2, :], t3[:, 0:NT, :]).then_inc(marked, 1)
                slot_marks(0)
                slot_marks(1)
                e3 = te_c.rearrange("p (i e) -> p i e", e=E)
                link(dve, V.tensor_tensor(e3, cum[0:1, :].unsqueeze(1).broadcast_to([1, NS, E]),
                                          iota_sb[0:1, 0:NS].unsqueeze(2).broadcast_to([1, NS, E]), ALU.is_le))
                link(dve, V.tensor_reduce(te_f, e3, AX.X, ALU.add))
                link(dve, V.tensor_scalar(te_f, te_f, float(E - 1), None, ALU.min))
                link(dve, V.tensor_copy(tile_expert[:, :], te_f))
                dve.wait_ge(found, 1)
                link(dve, V.tensor_copy(origin, origin_b[:, 0:3 * NS]))
                o1, ot_, of = (origin[:, g * NS:(g + 1) * NS] for g in range(3))
                link(dve, V.scalar_tensor_tensor(row1, ot_, float(W), o1, ALU.mult, ALU.add))
                link(dve, V.tensor_scalar(row, row1, -1.0, 0.0, ALU.add, ALU.max))
                V.tensor_copy(src_u[:, :], row).then_inc(indexed, 1)
                V.tensor_copy(first[:, :], of)
                V.tensor_scalar(real, o1, 1.0, None, ALU.min)
                link(dve, V.scalar_tensor_tensor(moved, of, -float(NT * W), row1, ALU.mult, ALU.add))
                link(dve, V.tensor_tensor(moved, moved, padding_sb[:, 0, :], ALU.add))
                link(dve, V.tensor_tensor(moved, moved, real, ALU.mult))
                link(dve, V.tensor_tensor(moved, moved, padding_sb[:, 1, :], ALU.add))
                V.tensor_copy(dst_u[:, :], moved).then_inc(n_over, 1)

        def experts(L, n, rows_, begin):
            S_ = lambda x: sem(f"{x}_{L}")
            R = rows_
            take = area(0)
            xin = [take(R, D + 2) for _ in range(2)]
            xT = [take(128, 2 * R) for _ in range(2)]
            sg = take(R, FF)
            hid = take(R, FF)
            hT = take(128, 4 * R)
            yv = [take(R, D) for _ in range(2)]
            gd, ud, t2, td, m2, te, sd, he, hd, yd = (
                S_(x) for x in ("e_gate", "e_up", "e_hidT", "e_turned", "e_down", "e_xT", "e_silu",
                                "e_hidT_copied", "e_hid", "e_y"))
            xb, gb, ub, hb, yb = bank[0:2], bank[2], bank[3], bank[4], bank[5]
            if L == 0:
                gate = [take(R, 1) for _ in range(2)]
                gated = S_("e_gated")
                xi = [S_(f"e_x{s}") for s in range(2)]
                ys = [S_(f"e_stored{s}") for s in range(2)]
            else:
                xf = S_("e_x")
                conv_acc = [take(128, 2 * W) for _ in range(2)]
                conv_tmp = take(128, 2 * W)
                rl = [take(W, D) for _ in range(2)]
                sk = [take(W, D) for _ in range(2)]
                cv0, cvs, cvd, rls, sks, sms = (
                    S_(x) for x in ("e_tap", "e_conv_step", "e_conv", "e_relu", "e_skip", "e_sum"))
                ys = [S_(f"e_stored{s}") for s in range(2)]

            def stored(eng, i, s):
                eng.wait_ge(ys[s], 16 * (i // 2) if isinstance(i, int) else (i - s) * 8)

            if L == 0:
                @part("gpsimd")
                def _(pool):
                    pool.wait_ge(indexed, 1)
                    pool.wait_ge(rows_out, 16 * (NT + 1))

                    def load(i, s):
                        if i >= 2:
                            pool.wait_ge(td, i - 1)
                            pool.wait_ge(gated, i - 1)
                        pool.indirect_dma_start(
                            xin[s], None, xn_d[:, :],
                            bass.IndirectOffsetOnAxis(src_u[:, i:i + 1], 0)).then_inc(xi[s], 16)

                    def put(i, s):
                        pool.wait_ge(yd, i + 1)
                        pool.indirect_dma_start(
                            ys_d[:, :], bass.IndirectOffsetOnAxis(dst_u[:, i:i + 1], 0),
                            yv[s], None).then_inc(ys[s], 16)
                    load(0, 0)
                    load(1, 1)
                    begin(pool)
                    for i in range(n):
                        if i + 2 < n:
                            load(i + 2, i % 2)
                        if i >= 1:
                            put(i - 1, (i - 1) % 2)
                    put(n - 1, (n - 1) % 2)
            else:
                @part("sync")
                def _(sp):
                    def put(i, s, k):
                        sp.wait_ge(yd, i + 1)
                        sp.dma_start(out[ds(i * R, R), :], yv[s]).then_inc(ys[s], 16)
                    over(sp, n - 1, put, head=2)
                    sp.wait_ge(yd, n)
                    sp.dma_start(out[(n - 1) * W:B * Q, :], yv[(n - 1) % 2][0:WL, :]).then_inc(ys[(n - 1) % 2], 16)
                    for s in range(2):
                        sp.wait_ge(ys[s], 16 * ((n + 1 - s) // 2))

            @part("scalar")
            def _(act):
                begin(act)

                def fix(t, s):
                    if later(t, 2):
                        act.wait_ge(td, t - 1)
                    A.activation(xin[s][:, 0:D], scr[:, ds(t * SCR, D)], ACT.Copy).then_inc(xf, 1)

                def turn(i, s):
                    act.wait_ge(td, i + 1)
                    if later(i, 2):
                        act.wait_ge(ud, i - 1)
                        if L == 1:
                            act.wait_ge(cvd, i - 1)
                    A.activation(xT[s], xb[s][:, 0:2 * R], ACT.Copy).then_inc(te, 1)

                def hid_turn(i):
                    act.wait_ge(t2, i + 1)
                    if later(i, 1):
                        act.wait_ge(m2, i)
                    A.activation(hT, hb[:, 0:4 * R], ACT.Copy).then_inc(he, 1)
                if L == 1:
                    fix(0, 0)
                    fix(1, 1)
                turn(0, 0)

                def body(i, s, k):
                    if L == 1:
                        if exists(i + 2, n):
                            fix(i + 2, s)
                        act.wait_ge(te, i + 1)
                        if later(i, 2):
                            act.wait_ge(m2, i - 1)
                        for c in range(2):
                            ins = A.activation(conv_acc[s][:, c * W:(c + 1) * W], xT[s][:, c * W:(c + 1) * W],
                                               ACT.Identity, bias=conv_sb[:, c, KC:KC + 1],
                                               scale=conv_sb[:, c, KC - 1:KC])
                        ins.then_inc(cv0, 1)
                    if later(i, 1):
                        hid_turn(i - 1)
                    act.wait_ge(gd, i + 1)
                    if later(i, 1):
                        act.wait_ge(hd, i)
                    if L == 0:
                        act.wait_ge(gated, i + 1)
                        A.activation(sg, gb[0:R, :], ACT.Silu, scale=gate[s]).then_inc(sd, 1)
                    else:
                        A.activation(sg, gb[0:R, :], ACT.Silu).then_inc(sd, 1)
                    if exists(i + 1, n):
                        turn(i + 1, 1 - s)
                over(act, n, body, head=2, tail=2)
                hid_turn(n - 1)

            @part("vector")
            def _(dve):
                begin(dve)

                def result(i, s):
                    if L == 1:
                        dve.wait_ge(sms, i + 1)
                    dve.wait_ge(m2, i + 1)
                    if later(i, 2):
                        stored(dve, i, s)
                    if L == 0:
                        V.tensor_copy(yv[s], yb[0:R, 0:D]).then_inc(yd, 1)
                    else:
                        V.tensor_tensor(yv[s], sk[s], yb[0:R, 0:D], ALU.add).then_inc(yd, 1)

                def body(i, s, k):
                    if L == 1:
                        x = scr[:, ds(i * SCR, D)]
                        cwf = cw[:, :, :].rearrange("p t e -> p (t e)")
                        if later(i, 2):
                            dve.wait_ge(sms, i - 1)
                        V.tensor_scalar(rl[s], x, 0.0, cwf[:, ds(i * E + E1 + 3, 1)],
                                        ALU.max, ALU.mult).then_inc(rls, 1)
                        if later(i, 2):
                            dve.wait_ge(yd, i - 1)
                        V.scalar_tensor_tensor(sk[s], x, skipw[:, ds(i, 1)], hs(i),
                                               ALU.mult, ALU.add).then_inc(sks, 1)
                    if L == 0:
                        dve.wait_ge(xi[s], (i - s) * 8 + 16)
                        if later(i, 2):
                            dve.wait_ge(sd, i - 1)
                            dve.wait_ge(hd, i - 1)
                        V.scalar_tensor_tensor(gate[s], xin[s][:, D:D + 1], first[:, ds(i, 1)],
                                               xin[s][:, D + 1:D + 2], ALU.mult, ALU.max).then_inc(gated, 1)
                        dve.wait_ge(gated, i + 1)
                    dve.wait_ge(ud, i + 1)
                    dve.wait_ge(sd, i + 1)
                    if later(i, 1):
                        dve.wait_ge(t2, i)
                    if L == 0:
                        V.scalar_tensor_tensor(hid, ub[0:R, :], gate[s], sg, ALU.mult, ALU.mult).then_inc(hd, 1)
                    else:
                        for e in range(E1):
                            c_ = slice(e * I1, (e + 1) * I1)
                            ins = V.scalar_tensor_tensor(hid[:, c_], sg[:, c_], cwf[:, ds(i * E + e, 1)],
                                                         ub[0:R, c_], ALU.mult, ALU.mult)
                        ins.then_inc(hd, 1)
                    if later(i, 1):
                        result(i - 1, 1 - s)
                over(dve, n, body, head=2)
                result(n - 1, (n - 1) % 2)

            if L == 1:
                @part("gpsimd")
                def _(pool):
                    begin(pool)

                    def body(t, s, k):
                        x4 = xT[s].rearrange("p (c b q) -> p c b q", c=2, b=G)
                        a4 = conv_acc[s].rearrange("p (c b q) -> p c b q", c=2, b=G)
                        m4 = conv_tmp.rearrange("p (c b q) -> p c b q", c=2, b=G)
                        pool.wait_ge(cv0, t + 1)
                        for j in range(1, KC):
                            ins = None
                            for c in range(2):
                                ins = P.tensor_tensor(
                                    m4[:, c, :, 0:Q - j], x4[:, c, :, 0:Q - j],
                                    conv_sb[:, c, KC - 1 - j:KC - j].unsqueeze(2).broadcast_to([128, G, Q - j]),
                                    ALU.mult)
                            ins.then_inc(cvs, 1)
                            pool.wait_ge(cvs, (KC - 1) * 2 * t + 2 * j - 1)
                            for c in range(2):
                                ins = P.tensor_tensor(a4[:, c, :, j:Q], a4[:, c, :, j:Q], m4[:, c, :, 0:Q - j],
                                                      ALU.add)
                            if j < KC - 1:
                                ins.then_inc(cvs, 1)
                                pool.wait_ge(cvs, (KC - 1) * 2 * t + 2 * j)
                        ins.then_inc(cvd, 1)
                        pool.wait_ge(cvd, t + 1)
                        pool.sem_inc(cvs)
                        pool.wait_ge(rls, t + 1)
                        pool.wait_ge(sks, t + 1)
                        P.tensor_tensor(sk[s], sk[s], rl[s], ALU.add).then_inc(sms, 1)
                    over(pool, n, body, head=2)

            @part("tensor")
            def _(pe):
                begin(pe)

                def expert(i):
                    if L == 1:
                        return 0
                    return pe.value_load(tile_expert[0:1, ds(i, 1)], min_val=0, max_val=E - 1)
                gu = w_gu[:, :, :].rearrange("p e n -> p (e n)")
                dn = w_dn[:, :, :].rearrange("p e n -> p (e n)")

                def turn(i, s):
                    if L == 0:
                        pe.wait_ge(xi[s], (i - s) * 8 + 16)
                    else:
                        pe.wait_ge(xf, i + 1)
                    if later(i, 2):
                        pe.wait_ge(te, i - 1)
                    for c in range(2):
                        mm = T.transpose(xb[s][:, c * R:(c + 1) * R], xin[s][:, c * 128:(c + 1) * 128],
                                         ident_sb[0:R, 0:R])
                    mm.then_inc(td, 1)

                def wide(i, s, e, b_, o, done):
                    for c in range(2):
                        mm = T.matmul(b_[0:R, :], xT[s][:, c * R:(c + 1) * R],
                                      gu[:, ds(e * (4 * FF) + c * 2 * FF + o, FF)], start=c == 0, stop=c == 1)
                    mm.then_inc(done, 1)

                def hid_turn(i):
                    pe.wait_ge(hd, i + 1)
                    if later(i, 1):
                        pe.wait_ge(he, i)
                    for c in range(4):
                        mm = T.transpose(hb[:, c * R:(c + 1) * R], hid[:, c * 128:(c + 1) * 128],
                                         ident_sb[0:R, 0:R])
                    mm.then_inc(t2, 1)

                def down_(i, s, e):
                    pe.wait_ge(he, i + 1)
                    if later(i, 1):
                        pe.wait_ge(yd, i)
                    if L == 1:
                        pe.wait_ge(cvd, i + 1)
                    for c in range(4):
                        mm = T.matmul(yb[0:R, 0:D], hT[:, c * R:(c + 1) * R], dn[:, ds(e * (4 * D) + c * D, D)],
                                      start=c == 0, stop=L == 0 and c == 3, skip_group_check=L == 1)
                    if L == 1:
                        for c in range(2):
                            mm = T.matmul(yb[0:R, c * 128:(c + 1) * 128], conv_acc[s][:, c * W:(c + 1) * W],
                                          ident_sb[:, :], start=False, stop=c == 1, skip_group_check=True)
                    mm.then_inc(m2, 1)
                turn(0, 0)

                def body(i, s, e_last, e):
                    pe.wait_ge(te, i + 1)
                    if later(i, 1):
                        pe.wait_ge(sd, i)
                    wide(i, s, e, gb, 0, gd)
                    if later(i, 1):
                        hid_turn(i - 1)
                    wide(i, s, e, ub, FF, ud)
                    if exists(i + 1, n):
                        turn(i + 1, 1 - s)
                    if later(i, 1):
                        down_(i - 1, 1 - s, e_last)
                e_last = None
                for i in range(2):
                    e = expert(i)
                    body(i, i, e_last, e)
                    e_last = e
                step_ = 4
                trips = (n - 3) // step_
                with pe.Fori(0, trips) as j:
                    e_last = expert(j * step_ + 1)
                    for u in range(step_):
                        e = expert(j * step_ + (2 + u))
                        body(j * step_ + (2 + u), u % 2, e_last, e)
                        e_last = e
                e_last = expert(2 + trips * step_ - 1)
                for i in range(2 + trips * step_, n):
                    e = expert(i)
                    body(i, i % 2, e_last, e)
                    e_last = e
                hid_turn(n - 1)
                down_(n - 1, (n - 1) % 2, e_last)
            return dict(m2=m2, ys=ys, yd=yd, ud=ud, te=te, he=he, sd=sd)

        indexed = sem("indexed")
        placed = sem("placed")
        rows_out = sem("rows_out")
        routed0, routed1 = sem("routed0"), sem("routed1")
        choice_steps = [0]
        route(0, h_att0, routed0)

        def sorted_ready(eng):
            eng.wait_ge(routed0, 1)
            eng.wait_ge(both_layers["r_added"], NT)
            eng.wait_ge(experts_in, 16 * 12)
            eng.wait_ge(experts67_in, 16 * 4)

        @part("sync")
        def _(sp):
            sp.wait_ge(both_layers["d_proj"], NT)
            sp.dma_start(wqkv_sb[:, :, :], wqkv[1]).then_inc(attw_in[1], 16)
            sp.dma_start(wo_sb[:, :, :], wo[1]).then_inc(attw_in[1], 16)

        e0 = experts(0, NS, SLOT, sorted_ready)

        def outputs_stored(eng):
            for s in range(2):
                eng.wait_ge(e0["ys"][s], 16 * ((NS + 1 - s) // 2))

        @part("sync")
        def _(sp):
            sp.wait_ge(e0["m2"], NS)
            sp.dma_start(w_gu[:, 0, :], gate_up1).then_inc(ffn1_in, 16)
            sp.dma_start(w_dn[:, 0, :], down1).then_inc(ffn1_in, 16)

        got_in = [sem(f"got_in{s}") for s in range(2)]
        summed, h_ffn0 = sem("summed"), sem("h_ffn0")

        @part("sync")
        def _(sp):
            outputs_stored(sp)
            y4 = ys_d[0:NK * W, :].rearrange("(c r) d -> r c d", c=2)

            def fetch(t, rows_, s):
                if later(t, 2):
                    sp.wait_ge(got_in[s], (t - s) * 8)
                sp.dma_start(scr[0:rows_, ds(t * SCR, 2 * D)].rearrange("p (c d) -> p c d", c=2),
                             y4[ds(t * W, rows_), :, :]).then_inc(got_in[s], 16)
            over(sp, NT - 1, lambda t, s, k: fetch(t, W, s), head=2)
            fetch(NT - 1, WL, (NT - 1) % 2)

        def combine(dve, t, s):
            r = WL if isinstance(t, int) and t == NT - 1 else W
            y = lambda c: scr[0:r, ds(t * SCR + c * D, D)]
            dve.wait_ge(got_in[s], (t - s) * 8 + 16)
            V.tensor_tensor(y(0), y(0), y(1), ALU.add).then_inc(summed, 1)
            dve.wait_ge(summed, t + 1)
            V.tensor_tensor(h[0:r, ds(t * D, D)], h[0:r, ds(t * D, D)], y(0), ALU.add).then_inc(h_ffn0, 1)
        if stop == "ffn0":
            @part("vector")
            def _(dve):
                for t in range(NT):
                    combine(dve, t, t % 2)
            store(h_ffn0)
            return finish()

        h_att1 = sem("h_att1")
        attention(1, h_ffn0, h_att1, outputs_stored, combine)
        if stop == "attn1":
            store(h_att1)
            return finish()
        route(1, h_att1, routed1)

        def tokens_ready(eng):
            eng.wait_ge(routed1, 1)
            eng.wait_ge(ffn1_in, 32)
        experts(1, NT, W, tokens_ready)
        finish()



def host_arrays(i):
    import numpy as np
    f = np.float32
    a = {}
    x = np.asarray(i["x"]).reshape(B, CH, SIDE, PATCH, SIDE, PATCH).transpose(0, 2, 4, 1, 3, 5)
    x = x.reshape(B, SIDE * SIDE, NF * 128)
    full = np.zeros((NT * G, Q, NF * 128), f)
    full[:B, 1:] = x
    a["patches"] = full.reshape(NT, W, NF, 128).transpose(0, 3, 2, 1).reshape(NT, 128, NF * W)
    kmaj = lambda w, c: np.asarray(w).reshape(c, 128, -1).transpose(1, 0, 2)
    a["tok_w"] = kmaj(np.asarray(i["L0_tok_W"]).T, NF).reshape(128, NF * D)
    pos = np.asarray(i["L0_tok_pos_enc"])[0]
    add = np.concatenate([np.asarray(i["L0_tok_cls_token"])[0], np.tile(np.asarray(i["L0_tok_b"])[None], (Q - 1, 1))])
    row = lambda v: np.tile(np.asarray(v)[None], (W, 1))
    a["rows"] = np.stack([np.tile(pos, (G, 1)), np.tile(add, (G, 1)), row(i["L0_ffn_ln_gamma"]),
                          row(i["L0_ffn_ln_beta"]), row(i["L1_attn_bo"])], 1)
    a["ident"] = np.eye(128, dtype=f)
    ang = np.arange(Q, dtype=f)[:, None] * (1.0 / 10000.0 ** (np.arange(0, DK, 2, dtype=f) / DK)).astype(f)
    c, s = np.cos(ang), np.sin(ang)
    a["rope"] = np.tile(np.stack([np.concatenate([c, c], 1), np.concatenate([-s, s], 1)], 1), (G, 1, 1)).astype(f)
    a["headmask"] = (np.arange(128)[:, None] // DK == np.arange(HH)[None]).astype(f)
    a["imgmask"] = np.concatenate([np.arange(W)[:, None] // Q == np.arange(G)[None],
                                   np.arange(W)[:, None] < WL, np.arange(W)[:, None] + 1], 1).astype(f)
    a["causal"] = np.tile(np.where(np.arange(Q)[None] > np.arange(Q)[:, None], f(NEG), f(0)), (1, HH)).astype(f)
    a["selq"] = (np.arange(Q)[:, None] == np.arange(128)[None] % HALF).astype(f)
    a["tri"] = (np.arange(W)[:, None] < np.arange(W)[None]).astype(f)
    a["cumtri"] = np.tile((np.arange(E)[None] <= np.arange(E)[:, None]).astype(f).reshape(1, -1), (128, 1))
    a["thresholds"] = np.tile(SLOT * np.arange(MAXT, dtype=f)[None], (128, 1))
    a["iota"] = np.tile(np.arange(SLOT, dtype=f)[None], (128, 1))
    a["pair_tile"] = np.tile(np.arange(NK, dtype=f)[None] % NT, (W, 1))
    own = NK * W + np.arange(NS)[None] * SLOT + np.arange(SLOT)[:, None]
    a["padding"] = np.stack([NT * W - 1 - own, own], 1).astype(f)
    halves = np.concatenate([np.arange(0, DK, 2), np.arange(1, DK, 2)])
    perm = (np.arange(H)[:, None] * DK + halves[None]).reshape(-1)
    wq, wk = (np.asarray(i[f"L0_attn_{n}"])[perm] for n in ("Wq", "Wk"))
    l0 = np.concatenate([wq.T, wk.T, np.asarray(i["L0_attn_Wv"]).T], 1)
    l1 = np.concatenate([np.asarray(i[f"L1_attn_{n}"]).T for n in ("Wq", "Wk", "Wv")], 1)
    a["wqkv"] = np.stack([kmaj(l0, 2), kmaj(l1, 2)])
    a["wo"] = np.stack([kmaj(np.asarray(i[f"L{l}_attn_Wo"]).T, 2) for l in range(2)])
    a["router"] = np.stack([kmaj(np.asarray(i["L0_ffn_router_w"]).T, 2), kmaj(i["L1_ffn_Wr"], 2)], 2)
    a["router_bias"] = row(i["L1_ffn_router_bias"])
    a["gate_up"] = np.stack([kmaj(w.T, 2).reshape(128, -1) for w in np.asarray(i["L0_ffn_gate_up_w"])])
    a["down"] = np.stack([kmaj(w.T, 4).reshape(128, -1) for w in np.asarray(i["L0_ffn_down_w"])])
    wg, wu = (np.asarray(i[f"L1_ffn_{n}"]).transpose(1, 0, 2).reshape(D, E1 * I1) for n in ("Wg", "Wu"))
    a["gate_up1"] = kmaj(np.concatenate([wg, wu], 1), 2).reshape(128, -1)
    a["down1"] = kmaj(np.asarray(i["L1_ffn_Wd"]).reshape(E1 * I1, D), 4).reshape(128, -1)
    cv = np.concatenate([np.asarray(i["L1_ffn_conv_w"])[:, 0], np.asarray(i["L1_ffn_conv_b"])[None]])
    a["conv"] = cv.T.reshape(2, 128, KC + 1).transpose(1, 0, 2)
    return {k: np.ascontiguousarray(v) for k, v in a.items()}


STOP = "all"


def kernel(**inputs):
    import numpy as np
    import concourse.bacc as bacc
    from concourse import mybir as mb
    from concourse.bass_utils import run_bass_kernel_spmd as run

    nc = bacc.Bacc("TRN2", target_bir_lowering=False, num_devices=1)
    arrays = host_arrays(inputs)
    args = {k: nc.dram_tensor(k, v.shape, mb.dt.from_np(v.dtype), kind="ExternalInput").ap() for k, v in arrays.items()}
    out = nc.dram_tensor("out", (B * Q, D), mb.dt.float32, kind="ExternalOutput").ap()
    build(nc, **args, out=out, stop=STOP)
    r = run(nc, [arrays], core_ids=[0])
    return r.results[0]["out"].reshape(B, Q, D)
```

```python
import concourse.bass as bass
from concourse import mybir
from contextlib import ExitStack

B, IMG, CH, PATCH = 32, 96, 3, 16
SIDE = IMG // PATCH
Q = SIDE * SIDE + 1
D, H, DK = 256, 16, 16
G = 3
W = G * Q
NT = -(-B // G)
NF = CH * PATCH * PATCH // 128
E = 8
FF = 512
SLOT = 128
NS = (2 * B * Q + E * (SLOT - 1)) // SLOT
MAXT = -(-B * Q // SLOT)
WL = B * Q - (NT - 1) * W
NK = 2 * NT
EARLY = E - 2
E1, I1 = 4, 128
KC = 4
BANK = 512
HH = H // 2
VW = G * (DK + 1)
HALF = 64
SR = HALF + Q
SC = HH * W
SCR = max(SC, H * VW)
SCALE = DK ** -0.5
EPS = 1e-5
ACT_HEADS = 4
A_COLS = 2 * D + 4 * W + 12 * D
C_COLS = 2 * HH * 128 + 2 * H * VW + 2 * HH * G
B_COLS = A_COLS + 4 * D + 8 * W
WORK = B_COLS + 2 * SC
CHOICE = 4700
NEG = -3.0e38


def build(nc, patches, tok_w, rows, ident, rope, headmask, imgmask, causal, selq, tri, cumtri,
          thresholds, iota, pair_tile, padding, wqkv, wo, router, router_bias, gate_up, down,
          gate_up1, down1, conv, out):
    fp32, bf16 = mybir.dt.float32, mybir.dt.bfloat16
    u32, i32 = mybir.dt.uint32, mybir.dt.int32
    ALU, ACT, AX = mybir.AluOpType, mybir.ActivationFunctionType, mybir.AxisListType
    ds = bass.ds
    ctx = ExitStack()

    def sb(name, shape, dt=fp32):
        return ctx.enter_context(nc.sbuf_tensor(name, shape, dt))

    def sem(name):
        return ctx.enter_context(nc.semaphore(name))

    both_layers = {}

    def shared(name):
        if name not in both_layers:
            both_layers[name] = sem(name)
        return both_layers[name]

    def later(t, depth):
        return not isinstance(t, int) or t >= depth

    def carry(column=4):
        nc.vector.memset(spare[:, column:column + 1], 0.0)

    def exists(t, n):
        return not isinstance(t, int) or 0 <= t < n

    def over(eng, n, body, unroll=2, head=2, tail=0):
        for t in range(head):
            body(t, t % unroll, t // unroll)
        trips = (n - tail - head) // unroll
        if trips > 0:
            with eng.Fori(0, trips) as i:
                for u in range(unroll):
                    body(i * unroll + (head + u), (head + u) % unroll, i + (head + u) // unroll)
        else:
            trips = 0
        for t in range(head + trips * unroll, n):
            body(t, t % unroll, t // unroll)

    def paired(eng, n, lag, first, second, early=0, ahead=0, swap=False):
        def step(t, s):
            if not swap and exists(t, n):
                first(t, s, None)
            if later(t, lag - early):
                second(t - lag, (s - lag) % 2, None)
            if swap and exists(t, n):
                first(t, s, None)
        head = lag + 2
        trips = (n - ahead - head) // 2
        for t in range(head):
            step(t, t % 2)
        if trips > 0:
            with eng.Fori(0, trips) as i:
                for u in range(2):
                    step(i * 2 + (head + u), (head + u) % 2)
        for t in range(head + max(trips, 0) * 2, n + lag):
            step(t, t % 2)

    with ctx:
        w_gu = sb("w_gu", [128, E, 2 * 2 * FF])
        w_dn = sb("w_dn", [128, E, 4 * D])
        tokw = w_gu[:, EARLY, 0:NF * D]
        patch = [w_gu[:, EARLY + 1, s * NF * W:(s + 1) * NF * W] for s in range(3)]
        h = sb("h", [W, NT * D])
        scr = sb("scr", [W, NT * SCR])
        v_all = sb("v_all", [W, NT * D])
        wqkv_sb = sb("wqkv_sb", [128, 2, 3 * D])
        wo_sb = sb("wo_sb", [128, 2, D])
        router_sb = sb("router_sb", [128, 2, 2, E])
        rows_sb = sb("rows_sb", [W, 5, D])
        ident_sb = sb("ident_sb", [128, 128])
        rope_sb = sb("rope_sb", [W, 2, DK])
        headmask_sb = sb("headmask_sb", [128, HH])
        imgmask_sb = sb("imgmask_sb", [W, G + 2])
        causal_f = sb("causal_f", [Q, HH * Q])
        selq_f = sb("selq_f", [Q, 128])
        causal_sb = sb("causal_sb", [Q, HH * Q], bf16)
        selq_sb = sb("selq_sb", [Q, 128], bf16)
        tri_sb = sb("tri_sb", [W, W])
        cumtri_sb = sb("cumtri_sb", [128, E * E])
        thr_sb = sb("thr_sb", [128, MAXT])
        iota_sb = sb("iota_sb", [128, SLOT])
        pair_tile_sb = sb("pair_tile_sb", [W, NK])
        padding_sb = sb("padding_sb", [128, 2, NS])
        rbias_sb = sb("rbias_sb", [W, E])
        conv_sb = sb("conv_sb", [128, 2, KC + 1])
        ones = sb("ones", [W, H])
        ones_bf = sb("ones_bf", [W, 128], bf16)
        tri_bf = sb("tri_bf", [W, W], bf16)
        halfneg = sb("halfneg", [W, 1])
        epsv = sb("epsv", [W, 1])
        spare = sb("spare", [W, 7])
        stats = [sb(f"stats{s}", [W, 6]) for s in range(2)]
        mv = [sb(f"mv{s}", [W, 2]) for s in range(2)]
        veps = [sb(f"veps{s}", [W, 1]) for s in range(2)]
        rstd = [sb(f"rstd{s}", [W, 1]) for s in range(2)]
        stats2 = [sb(f"stats2{s}", [W, 6]) for s in range(2)]
        mv2 = [sb(f"mv2{s}", [W, 2]) for s in range(2)]
        veps2 = [sb(f"veps2{s}", [W, 1]) for s in range(2)]
        rstd2 = [sb(f"rstd2{s}", [W, 1]) for s in range(2)]
        logits = sb("logits", [W, NT, E])
        cw = sb("cw", [W, NT, E])
        skipw = sb("skipw", [W, NT])
        src_u = sb("src_u", [128, NS], u32)
        dst_u = sb("dst_u", [128, NS], u32)
        first = sb("first", [128, NS])
        tile_expert = sb("tile_expert", [1, NS], i32)
        work = sb("work", [128, WORK])

        def area(first=0, end=WORK):
            at = [first]

            def take(rows_, cols):
                a = work[0:rows_, at[0]:at[0] + cols]
                at[0] += cols
                assert at[0] <= end, at
                return a
            return take

        psum = ctx.enter_context(nc.psum_tensor("psum", [128, 8 * BANK], fp32))
        bank = [psum[:, i * BANK:(i + 1) * BANK] for i in range(8)]

        consts_in = sem("consts_in")
        patch_in = [sem(f"patch_in{s}") for s in range(3)]
        tokw_in = [sem(f"tokw_in{n}") for n in range(2)]
        attw_in = [sem(f"attw_in{n}") for n in range(2)]
        experts_in = sem("experts_in")
        late_experts_in = sem("late_experts_in")
        ffn1_in = sem("ffn1_in")
        tables = sem("tables")
        pool_tables = sem("pool_tables")
        act_tables = sem("act_tables")
        tok_done = sem("tok_done")
        h_tok = sem("h_tok")

        xn_d = nc.dram_tensor("expert_inputs", (NT * W, D + 2), fp32, kind="Internal").ap()
        ys_d = nc.dram_tensor("expert_outputs", (NK * W + NS * SLOT, D), fp32, kind="Internal").ap()

        block = ctx.enter_context(nc.Block())
        progs = {"sync": [], "gpsimd": [], "scalar": [], "vector": [], "tensor": []}

        def part(engine):
            def add(f):
                progs[engine].append(f)
            return add

        hs = lambda t: h[:, ds(t * D, D)]
        norms_start = []
        first_rows = []
        project = {}
        V, P, A, T = nc.vector, nc.gpsimd, nc.scalar, nc.tensor

        CONSTS = [(rows_sb[:, :, :], rows), (ident_sb[:, :], ident), (rope_sb[:, :, :], rope),
                  (headmask_sb[:, :], headmask), (imgmask_sb[:, :], imgmask), (causal_f[:, :], causal),
                  (selq_f[:, :], selq), (tri_sb[:, :], tri), (cumtri_sb[:, :], cumtri),
                  (thr_sb[:, :], thresholds), (iota_sb[:, :], iota), (pair_tile_sb[:, :], pair_tile),
                  (padding_sb[:, :, :], padding), (router_sb[:, :, :, :], router),
                  (rbias_sb[:, :], router_bias), (conv_sb[:, :, :], conv)]

        @part("sync")
        def _(sp):
            half = NF // 2 * D
            sp.dma_start(tokw[:, 0:half], tok_w[:, 0:half]).then_inc(tokw_in[0], 16)

            def load(t, s, k):
                if later(t, 3):
                    sp.wait_ge(tok_done, t - 2)
                sp.dma_start(patch[s], patches[ds(t, 1), :, :].rearrange("a p n -> (a p) n")).then_inc(patch_in[s], 16)
            load(0, 0, 0)
            sp.dma_start(tokw[:, half:], tok_w[:, half:]).then_inc(tokw_in[1], 16)
            for t in range(1, 3):
                load(t, t, 0)
            for dst, src in CONSTS:
                sp.dma_start(dst, src).then_inc(consts_in, 16)
            with sp.Fori(0, (NT - 3) // 3) as i:
                for u in range(3):
                    load(i * 3 + (3 + u), u, i + 1)
            for t in range(3 + (NT - 3) // 3 * 3, NT):
                load(t, t % 3, t // 3)
            sp.dma_start(wqkv_sb[:, :, :], wqkv[0]).then_inc(attw_in[0], 16)
            sp.dma_start(wo_sb[:, :, :], wo[0]).then_inc(attw_in[0], 16)
            for e in range(EARLY):
                sp.dma_start(w_gu[:, e, :], gate_up[e]).then_inc(experts_in, 16)
                sp.dma_start(w_dn[:, e, :], down[e]).then_inc(experts_in, 16)
            sp.wait_ge(tok_done, NT)
            for e in range(EARLY, E):
                sp.dma_start(w_gu[:, e, :], gate_up[e]).then_inc(late_experts_in, 16)
                sp.dma_start(w_dn[:, e, :], down[e]).then_inc(late_experts_in, 16)

        @part("gpsimd")
        def _(pool):
            P.memset(ones[:, :], 1.0).then_inc(pool_tables, 1)
            P.memset(halfneg[:, :], -0.5).then_inc(pool_tables, 1)
            P.memset(epsv[:, :], EPS).then_inc(pool_tables, 1)
            P.memset(ones_bf[:, :], 1.0).then_inc(pool_tables, 1)
            pool.wait_ge(pool_tables, 4)

        @part("vector")
        def _(dve):
            dve.wait_ge(consts_in, 16 * len(CONSTS))
            V.tensor_copy(causal_sb[:, :], causal_f[:, :]).then_inc(tables, 1)
            V.tensor_copy(selq_sb[:, :], selq_f[:, :]).then_inc(tables, 1)
            V.tensor_tensor(rows_sb[:, 0, :], rows_sb[:, 0, :], rows_sb[:, 1, :], ALU.add).then_inc(tables, 1)
            dve.wait_ge(tables, 3)

            def add_pos(t, s, k):
                dve.wait_ge(tok_done, t + 1)
                V.tensor_tensor(hs(t), bank[s][0:W, 0:D], rows_sb[:, 0, :], ALU.add).then_inc(h_tok, 1)
            over(dve, NT - 3, add_pos, unroll=3, head=3)
            norms_start[0](dve)
            for t in range(NT - 3, NT):
                add_pos(t, t % 3, t // 3)

        @part("scalar")
        def _(act):
            act.wait_ge(consts_in, 16 * len(CONSTS))
            A.activation(tri_bf[:, :], tri_sb[:, :], ACT.Copy).then_inc(act_tables, 1)

        @part("tensor")
        def _(pe):
            pe.wait_ge(tokw_in[0], 16)

            def product(t, s, k):
                pe.wait_ge(patch_in[s], 16 * k + 16)
                if later(t, 3):
                    pe.wait_ge(h_tok, t - 2)
                for c in range(NF):
                    if isinstance(t, int) and t == 0 and c == NF // 2:
                        pe.wait_ge(tokw_in[1], 16)
                    mm = T.matmul(bank[s][0:W, 0:D], patch[s][:, c * W:(c + 1) * W],
                                  tokw[:, c * D:(c + 1) * D], start=c == 0, stop=c == NF - 1)
                mm.then_inc(tok_done, 1)
            over(pe, NT, product, unroll=3, head=3)

        def attention(L, h_in, h_out, free_before, make_h=None):
            base = L * NT
            take = area()
            xn = [take(W, D) for _ in range(2)]
            xnT = [take(128, 2 * W) for _ in range(2)]
            qkf = [take(W, 2 * D) for _ in range(2)]
            cosd = [take(W, 2 * D) for _ in range(2)]
            sind = [take(W, 2 * D) for _ in range(2)]
            st, ag, ve, rs, xd, td, xe_, qkd, vd, qke, vev, cosn, sinn, roped = (
                shared(x) for x in ("a_stats", "a_aggr", "a_veps", "a_rstd", "a_xn", "a_transposed",
                                "a_xnT", "a_qk", "a_v", "a_qk_copied", "a_v_copied", "a_cos",
                                "a_sin", "a_roped"))
            tb, qkb, vb = bank[0:2], bank[2:4], bank[4:6]
            scq = lambda t: scr[:, ds(t * SCR, 2 * D)]

            def norm_steps(dve):
                def stat(t, s):
                    if make_h:
                        make_h(dve, t, s)
                    dve.wait_ge(h_in, t + 1)
                    if make_h:
                        carry()
                    V.bn_stats(stats[s][:, :], hs(t)).then_inc(st, 1)
                    if later(t, 2):
                        dve.wait_ge(rs, base + t - 1)
                    dve.wait_ge(st, base + t + 1)
                    carry()
                    V.bn_aggr(mv[s][:, :], stats[s][:, :]).then_inc(ag, 1)

                def norm(t, s):
                    dve.wait_ge(rs, base + t + 1)
                    dve.wait_ge(ag, base + t + 1)
                    if later(t, 2):
                        dve.wait_ge(td, base + t - 1)
                    V.tensor_scalar(xn[s], hs(t), mv[s][:, 0:1], rstd[s][:, :],
                                    ALU.subtract, ALU.mult).then_inc(xd, 1)

                def start():
                    stat(0, 0)
                    stat(1, 1)
                    norm(0, 0)
                    norm(1, 1)
                    stat(2, 0)
                return stat, norm, start

            def start_norms(dve):
                norm_steps(dve)[2]()
            norms_start.append(start_norms)

            @part("vector")
            def _(dve):
                free_before(dve)
                stat, norm, _ = norm_steps(dve)
                if L == 1:
                    start_norms(dve)

                def rotate(t, s):
                    dve.wait_ge(sinn, base + t + 1)
                    dve.wait_ge(cosn, base + t + 1)
                    V.tensor_tensor(scq(t), cosd[s], sind[s], ALU.add).then_inc(roped, 1)

                def body(t, s, k):
                    if exists(t + 2, NT):
                        norm(t + 2, s)
                    if exists(t + 3, NT):
                        stat(t + 3, 1 - s)
                    dve.wait_ge(qke, base + t + 1)
                    if later(t, 2):
                        dve.wait_ge(roped, base + t - 1)
                    V.tensor_tensor(cosd[s].rearrange("p (h d) -> p h d", d=DK),
                                    qkf[s].rearrange("p (h d) -> p h d", d=DK),
                                    rope_sb[:, 0, :].unsqueeze(1).broadcast_to([W, 2 * H, DK]),
                                    ALU.mult).then_inc(cosn, 1)
                    if later(t, 1):
                        rotate(t - 1, 1 - s)
                over(dve, NT, body, head=2, tail=3 + L)
                rotate(NT - 1, (NT - 1) % 2)

            @part("gpsimd")
            def _(pool):
                def root(t, s):
                    pool.wait_ge(ag, base + t + 1)
                    P.tensor_tensor(veps[s][:, :], mv[s][:, 1:2], epsv[:, :], ALU.add).then_inc(ve, 1)
                    pool.wait_ge(ve, base + t + 1)
                    if later(t, 2):
                        pool.wait_ge(xd, base + t - 1)
                    P.tensor_tensor(rstd[s][:, :], veps[s][:, :], halfneg[:, :], ALU.pow).then_inc(rs, 1)
                for t in range(3):
                    root(t, t % 2)
                free_before(pool)

                def body(t, s, k):
                    if exists(t + 3, NT):
                        root(t + 3, 1 - s)
                    pool.wait_ge(qke, base + t + 1)
                    if later(t, 2):
                        pool.wait_ge(roped, base + t - 1)
                    x = qkf[s].rearrange("p (h a d) -> p h a d", a=2, d=DK // 2)
                    o = sind[s].rearrange("p (h a d) -> p h a d", a=2, d=DK // 2)
                    sn = rope_sb[:, 1, :].rearrange("p (a d) -> p a d", a=2)
                    for a in range(2):
                        ins = P.tensor_tensor(o[:, :, a, :], x[:, :, 1 - a, :],
                                              sn[:, a, :].unsqueeze(1).broadcast_to([W, 2 * H, DK // 2]),
                                              ALU.mult)
                    ins.then_inc(sinn, 1)
                over(pool, NT, body, head=2, tail=3)

            @part("scalar")
            def _(act):
                free_before(act)

                def turn(t, s):
                    act.wait_ge(td, base + t + 1)
                    if later(t, 2):
                        act.wait_ge(vd, base + t - 1)
                    A.activation(xnT[s], tb[s][:, 0:2 * W], ACT.Copy).then_inc(xe_, 1)
                turn(0, 0)

                def body(t, s, k):
                    if exists(t + 1, NT):
                        turn(t + 1, 1 - s)
                    act.wait_ge(qkd, base + t + 1)
                    if later(t, 2):
                        act.wait_ge(cosn, base + t - 1)
                        act.wait_ge(sinn, base + t - 1)
                    A.activation(qkf[s], qkb[s][0:W, 0:2 * D], ACT.Copy).then_inc(qke, 1)
                    act.wait_ge(vd, base + t + 1)
                    A.activation(v_all[:, ds(t * D, D)], vb[s][0:W, 0:D], ACT.Copy).then_inc(vev, 1)
                over(act, NT, body, head=2, tail=1)

            @part("tensor")
            def _(pe):
                free_before(pe)
                pe.wait_ge(attw_in[L], 32)
                pe.wait_ge(tables, 3)
                pe.wait_ge(act_tables, 1)

                def turn(t, s):
                    pe.wait_ge(xd, base + t + 1)
                    if later(t, 2):
                        pe.wait_ge(xe_, base + t - 1)
                    for c in range(2):
                        mm = T.transpose(tb[s][:, c * W:(c + 1) * W], xn[s][:, c * 128:(c + 1) * 128],
                                         ident_sb[0:W, 0:W])
                    mm.then_inc(td, 1)
                turn(0, 0)

                def body(t, s, k):
                    if exists(t + 1, NT):
                        turn(t + 1, 1 - s)
                    pe.wait_ge(xe_, base + t + 1)
                    if later(t, 2):
                        pe.wait_ge(qke, base + t - 1)
                        pe.wait_ge(vev, base + t - 1)
                    for o, b_, w_, sm in ((0, qkb, 2 * D, qkd), (2 * D, vb, D, vd)):
                        for c in range(2):
                            mm = T.matmul(b_[s][0:W, 0:w_], xnT[s][:, c * W:(c + 1) * W],
                                          wqkv_sb[:, c, o:o + w_], start=c == 0, stop=c == 1)
                        mm.then_inc(sm, 1)
                over(pe, NT, body, head=2, tail=1)

            take = area(A_COLS)
            qks = [take(W, 2 * D) for _ in range(2)]
            qkT = [take(128, 4 * W) for _ in range(2)]
            take = area()
            kblk = [take(128, 2 * HH * W) for _ in range(2)]
            take = area(C_COLS)
            mx = [take(SR, G * HH) for _ in range(2)]
            cp, tr, tre, bl0, bl1, bla, scd, mxd, sbd = (
                shared(x) for x in ("b_qk", "b_transposed", "b_qkT", "b_block0", "b_block1",
                                    "b_block_act", "b_scores", "b_max", "b_sub"))
            tbb = bank[0:2]
            sbank = lambda s, b: bank[2 + G * s + b]
            s4 = lambda s: psum[0:SR, (2 + G * s) * BANK:(2 + G * s + G) * BANK].rearrange(
                "p (b n) -> p b n", b=G)[:, :, 0:HH * Q].rearrange("p b (h k) -> p b h k", h=HH)

            def a_over(eng):
                eng.wait_ge(roped, base + NT)
                eng.wait_ge(vev, base + NT)

            @part("scalar")
            def _(act):
                def fix(t, s):
                    if later(t, 2):
                        act.wait_ge(tr, base + t - 1)
                    A.activation(qks[s], scq(t), ACT.Copy).then_inc(cp, 1)
                for t in range(2):
                    act.wait_ge(roped, base + t + 1)
                    fix(t, t)
                act.wait_ge(roped, base + NT)

                def turn(t, s):
                    act.wait_ge(tr, base + t + 1)
                    if later(t, 2):
                        act.wait_ge(scd, base + t - 1)
                    A.activation(qkT[s], tbb[s][:, 0:4 * W], ACT.Copy).then_inc(tre, 1)

                def spread_act(t, s):
                    act.wait_ge(tre, base + t + 1)
                    b4 = kblk[s][:, 0:HH * W].rearrange("p (b h q) -> p b h q", b=G, h=HH)
                    k3 = qkT[s][:, 2 * W:3 * W].rearrange("p (b q) -> p b q", b=G)
                    for hd in range(ACT_HEADS):
                        ins = A.activation(b4[:, :, hd, :], k3, ACT.Copy, scale=headmask_sb[:, hd:hd + 1])
                    ins.then_inc(bla, 1)
                turn(0, 0)
                spread_act(0, 0)

                def body(t, s, k):
                    if exists(t + 1, NT):
                        turn(t + 1, 1 - s)
                    if exists(t + 2, NT):
                        fix(t + 2, s)
                    if exists(t + 1, NT):
                        spread_act(t + 1, 1 - s)
                over(act, NT, body, head=2, tail=2)

            def spread(eng, t, s, f, first, done):
                eng.wait_ge(tre, base + t + 1)
                if later(t, 2):
                    eng.wait_ge(scd, base + t - 1)
                b4 = kblk[s][:, f * HH * W:(f + 1) * HH * W].rearrange("p (b h q) -> p b h q", b=G, h=HH)
                k3 = qkT[s][:, (2 + f) * W:(3 + f) * W].rearrange("p (b q) -> p b q", b=G)
                n_ = HH - first
                for b in range(G):
                    ins = eng.tensor_tensor(
                        b4[:, b, first:HH, :], k3[:, b, :].unsqueeze(1).broadcast_to([128, n_, Q]),
                        headmask_sb[:, first:HH].unsqueeze(2).broadcast_to([128, n_, Q]), ALU.mult)
                ins.then_inc(done, 1)

            @part("gpsimd")
            def _(pool):
                a_over(pool)
                over(pool, NT, lambda t, s, k: spread(pool, t, s, 1, 0, bl1), head=2)

            @part("vector")
            def _(dve):
                a_over(dve)
                spread(dve, 0, 0, 0, ACT_HEADS, bl0)

                def body(t, s, k):
                    if exists(t + 1, NT):
                        spread(dve, t + 1, 1 - s, 0, ACT_HEADS, bl0)
                    dve.wait_ge(scd, base + t + 1)
                    V.tensor_reduce(mx[s], s4(s), AX.X, ALU.max).then_inc(mxd, 1)
                    dve.wait_ge(mxd, base + t + 1)
                    m3 = mx[s].rearrange("p (b h) -> p b h", b=G)
                    o4 = scr[0:SR, ds(t * SCR, SC)].rearrange("p (h b k) -> p b h k", h=HH, b=G)
                    for b in range(G):
                        ins = V.tensor_tensor(o4[:, b, :, :], s4(s)[:, b, :, :],
                                              m3[:, b, :].unsqueeze(2).broadcast_to([SR, HH, Q]), ALU.subtract)
                    ins.then_inc(sbd, 1)
                over(dve, NT, body, head=2, tail=1)

            @part("tensor")
            def _(pe):
                def turn(t, s):
                    pe.wait_ge(cp, base + t + 1)
                    if later(t, 2):
                        pe.wait_ge(tre, base + t - 1)
                    for c in range(4):
                        mm = T.transpose(tbb[s][:, c * W:(c + 1) * W], qks[s][:, c * 128:(c + 1) * 128],
                                         ident_sb[0:W, 0:W])
                    mm.then_inc(tr, 1)
                turn(0, 0)
                a_over(pe)

                def body(t, s, k):
                    if exists(t + 1, NT):
                        turn(t + 1, 1 - s)
                    if later(t, 2):
                        pe.wait_ge(sbd, base + t - 1)
                    for b in range(G):
                        T.matmul(sbank(s, b)[:, 0:HH * Q], selq_sb[:, :], causal_sb[:, :],
                                 start=True, stop=False, skip_group_check=True)
                    pe.wait_ge(bla, base + t + 1)
                    for f, blocks in ((0, bl0), (1, bl1)):
                        pe.wait_ge(blocks, base + t + 1)
                        for b in range(G):
                            k0 = (f * G + b) * HH * Q
                            mm = T.matmul(sbank(s, b)[f * HALF:f * HALF + Q, 0:HH * Q],
                                          qkT[s][:, f * W + b * Q:f * W + (b + 1) * Q],
                                          kblk[s][:, k0:k0 + HH * Q],
                                          start=False, stop=f == 1, skip_group_check=True)
                    mm.then_inc(scd, 1)
                over(pe, NT, body, head=2, tail=1)

            take = area(B_COLS)
            pr = [take(SR, SC) for _ in range(2)]
            take = area()
            prT = [take(W, HH * 128) for _ in range(2)]
            vblk = [take(W, H * VW) for _ in range(2)]
            rc = [take(Q, HH * G) for _ in range(2)]
            ex, pt, pte0, pte1, vb_, pv0, pv1, rc0, rc1, oe0, oe1, vone = (
                shared(x) for x in ("c_exp", "c_transposed", "c_prT0", "c_prT1", "c_vblock", "c_out0",
                                "c_out1", "c_recip0", "c_recip1", "c_scaled0", "c_scaled1", "c_ones"))
            pte, pvd, rcd, oed = (pte0, pte1), (pv0, pv1), (rc0, rc1), (oe0, oe1)
            clr = shared("d_clear")
            take = area(C_COLS)
            on = [take(W, G * D) for _ in range(2)]
            tpb = lambda s, f: bank[2 * s + f]
            ob = lambda s, f: bank[4 + 2 * s + f]

            def b_over(eng):
                eng.wait_ge(scd, base + NT)

            def copy_prT(eng, fn, t, s, f):
                eng.wait_ge(pt, base + t + 1)
                if later(t, 2):
                    eng.wait_ge(pv1, base + t - 1)
                n3 = lambda a: a.rearrange("p (h q) -> p h q", q=128)[:, :, 0:SR]
                fn(n3(prT[s][:, f * 512:(f + 1) * 512]), n3(tpb(s, f)[0:W, :])).then_inc(pte[f], 1)

            def blocks(t, s, f):
                return ob(s, f)[0:Q, 0:HH * VW].rearrange("p (h b d) -> p h b d", h=HH, b=G)

            def recip(dve, t, s, f):
                dve.wait_ge(pvd[f], base + t + 1)
                if later(t, 1):
                    dve.wait_ge(oed[f], base + t)
                V.reciprocal(rc[f].rearrange("p (h b) -> p h b", h=HH),
                             blocks(t, s, f)[:, :, :, DK]).then_inc(rcd[f], 1)

            def scale(dve, t, s, f):
                dve.wait_ge(rcd[f], base + t + 1)
                o4 = scr[0:Q, ds(t * SCR, G * D)].rearrange("p (b h d) -> p h b d", b=G, d=DK)
                V.tensor_tensor(o4[:, f * HH:(f + 1) * HH, :, :], blocks(t, s, f)[:, :, :, 0:DK],
                                rc[f].rearrange("p (h b) -> p h b", h=HH).unsqueeze(3).broadcast_to([Q, HH, G, DK]),
                                ALU.mult).then_inc(oed[f], 1)

            act_copy = lambda o, i: A.activation(o, i, ACT.Copy)
            dve_copy = lambda o, i: V.tensor_copy(o, i)

            @part("scalar")
            def _(act):
                def expo(t, s):
                    if later(t, 2):
                        act.wait_ge(pt, base + t - 1)
                    A.activation(pr[s], scr[0:SR, ds(t * SCR, SC)], ACT.Exp, scale=SCALE).then_inc(ex, 1)
                for t in range(2):
                    act.wait_ge(sbd, base + t + 1)
                    expo(t, t)
                act.wait_ge(sbd, base + NT)
                b_over(act)
                copy_prT(act, act_copy, 0, 0, 0)

                def body(t, s, k):
                    if exists(t + 2, NT):
                        expo(t + 2, s)
                    if exists(t + 1, NT):
                        copy_prT(act, act_copy, t + 1, 1 - s, 0)
                over(act, NT, body, head=2, tail=2)

            @part("vector")
            def _(dve):
                b_over(dve)
                dve.wait_ge(sbd, base + NT)
                for s in range(2):
                    V.memset(on[s], 0.0).then_inc(clr, 1)
                copy_prT(dve, dve_copy, 0, 0, 1)

                def body(t, s, k):
                    recip(dve, t, s, 0)
                    if exists(t + 1, NT):
                        copy_prT(dve, dve_copy, t + 1, 1 - s, 1)
                    dve.wait_ge(ex, base + t + 1)
                    scale(dve, t, s, 0)
                    recip(dve, t, s, 1)
                    scale(dve, t, s, 1)
                over(dve, NT, body, head=2, tail=1)

            @part("gpsimd")
            def _(pool):
                b_over(pool)
                v4 = lambda s: vblk[s].rearrange("p (h b d) -> p h b d", h=H, b=G)
                for s in range(2):
                    for b in range(G):
                        ins = P.tensor_scalar(v4(s)[:, :, b, DK], ones[:, 0:H], imgmask_sb[:, b:b + 1],
                                              None, ALU.mult)
                ins.then_inc(vone, 1)

                def body(t, s, k):
                    if later(t, 2):
                        pool.wait_ge(pv1, base + t - 1)
                    for b in range(G):
                        ins = P.tensor_tensor(v4(s)[:, :, b, 0:DK],
                                              v_all[:, ds(t * D, D)].rearrange("p (h d) -> p h d", d=DK),
                                              imgmask_sb[:, b:b + 1].unsqueeze(2).broadcast_to([W, H, DK]),
                                              ALU.mult)
                    ins.then_inc(vb_, 1)
                over(pool, NT, body, head=2)

            @part("tensor")
            def _(pe):
                def turn(t, s):
                    pe.wait_ge(ex, base + t + 1)
                    if later(t, 2):
                        pe.wait_ge(pte0, base + t - 1)
                        pe.wait_ge(pte1, base + t - 1)
                    for j in range(HH):
                        mm = T.transpose(tpb(s, j // 4)[0:W, (j % 4) * 128:(j % 4) * 128 + SR],
                                         pr[s][:, j * W:(j + 1) * W], ident_sb[0:SR, 0:SR])
                    mm.then_inc(pt, 1)
                turn(0, 0)
                pe.wait_ge(vone, L + 1)
                pe.wait_ge(sbd, base + NT)

                def body(t, s, k):
                    if exists(t + 1, NT):
                        turn(t + 1, 1 - s)
                    pe.wait_ge(vb_, base + t + 1)
                    pe.wait_ge(pte0, base + t + 1)
                    pe.wait_ge(pte1, base + t + 1)
                    for f in range(2):
                        if later(t, 2):
                            pe.wait_ge(oed[f], base + t - 1)
                        for hd in range(HH):
                            p0 = hd * 128 + f * HALF
                            v0 = (f * HH + hd) * VW
                            mm = T.matmul(ob(s, f)[0:Q, hd * VW:(hd + 1) * VW], prT[s][:, p0:p0 + Q],
                                          vblk[s][:, v0:v0 + VW], start=True, stop=True)
                        mm.then_inc(pvd[f], 1)
                over(pe, NT, body, head=2, tail=1)

            take = area()
            oT = [take(128, 2 * W) for _ in range(2)]
            ond, ot, ote, wod, bod = (
                shared(x) for x in ("d_out", "d_transposed", "d_outT", "d_proj", "d_bias"))
            otb, wob = bank[0:2], bank[2:4]

            def c_over(eng):
                eng.wait_ge(oe0, base + NT)
                eng.wait_ge(oe1, base + NT)

            @part("gpsimd")
            def _(pool):
                c_over(pool)

                def body(t, s, k):
                    if L == 1:
                        P.tensor_tensor(hs(t), hs(t), rows_sb[:, 4, :], ALU.add).then_inc(bod, 1)
                project["gpsimd"] = body

            @part("vector")
            def _(dve):
                c_over(dve)

                def body(t, s, k):
                    dve.wait_ge(wod, base + t + 1)
                    if L == 1:
                        dve.wait_ge(bod, t + 1)
                    V.tensor_tensor(hs(t), hs(t), wob[s][0:W, 0:D], ALU.add).then_inc(h_out, 1)
                project["vector"] = body

            @part("scalar")
            def _(act):
                act.wait_ge(clr, 2 * L + 2)

                def fix(t, s):
                    if later(t, 2):
                        act.wait_ge(ot, base + t - 1)
                    A.activation(on[s][0:Q, :], scr[0:Q, ds(t * SCR, G * D)], ACT.Copy).then_inc(ond, 1)
                for t in range(2):
                    act.wait_ge(oe0, base + t + 1)
                    act.wait_ge(oe1, base + t + 1)
                    fix(t, t)
                c_over(act)

                def body(t, s, k):
                    act.wait_ge(ot, base + t + 1)
                    if later(t, 2):
                        act.wait_ge(wod, base + t - 1)
                    A.activation(oT[s], otb[s][:, 0:2 * W], ACT.Copy).then_inc(ote, 1)
                    if exists(t + 2, NT):
                        fix(t + 2, s)
                project["scalar"] = body

            @part("tensor")
            def _(pe):
                def turn(t, s):
                    pe.wait_ge(ond, base + t + 1)
                    if later(t, 2):
                        pe.wait_ge(ote, base + t - 1)
                    for f in range(2):
                        for b in range(G):
                            o = f * W + b * Q
                            mm = T.transpose(otb[s][:, o:o + W],
                                             on[s][:, b * D + f * 128:b * D + (f + 1) * 128],
                                             ident_sb[0:W, 0:W])
                    mm.then_inc(ot, 1)
                turn(0, 0)

                def body(t, s, k):
                    if exists(t + 1, NT):
                        turn(t + 1, 1 - s)
                    pe.wait_ge(ote, base + t + 1)
                    if later(t, 2):
                        pe.wait_ge(h_out, t - 1)
                    for f in range(2):
                        mm = T.matmul(wob[s][0:W, 0:D], oT[s][:, f * W:(f + 1) * W], wo_sb[:, f, :],
                                      start=f == 0, stop=f == 1)
                    mm.then_inc(wod, 1)
                project["tensor"] = body

        def finish():
            @block.sync
            def _(sp):
                for f in progs["sync"]:
                    f(sp)

            @block.gpsimd
            def _(pool):
                for f in progs["gpsimd"]:
                    f(pool)

            @block.scalar
            def _(act):
                for f in progs["scalar"]:
                    f(act)

            @block.vector
            def _(dve):
                for f in progs["vector"]:
                    f(dve)

            @block.tensor
            def _(pe):
                for f in progs["tensor"]:
                    f(pe)


        def tok_over(eng):
            eng.wait_ge(tok_done, NT)
            eng.wait_ge(h_tok, NT)

        h_att0 = sem("h_att0")
        attention(0, h_tok, h_att0, tok_over)

        def route(L, h_in, n_over):
            base = L * NT
            take = area(4 * W)
            x1 = [take(W, D) for _ in range(2)]
            xg = [take(W, D) for _ in range(2)]
            tmp = take(W, D)
            xT = [take(128, 2 * W) for _ in range(2)]
            st, ag, ve, rs, n1, st2, ag2, ve2, rs2, f0, f1, hx, kept, td, te, lg, lge = (
                shared(x) for x in ("r_stats", "r_aggr", "r_veps", "r_rstd", "r_norm", "r_stats2",
                                    "r_aggr2", "r_veps2", "r_rstd2", "r_gamma", "r_rows", "r_added",
                                    "r_kept", "r_transposed", "r_rowsT", "r_logits",
                                    "r_logits_copied"))
            tb, lb = bank[4:6], bank[6:8]
            xo = xg if L == 1 else x1
            rows_ready = n1 if L == 1 else f1
            fbase = 0 if L == 0 else base

            @part("vector")
            def _(dve):
                def stat(t, s):
                    dve.wait_ge(h_in, t + 1)
                    if later(t, 2):
                        dve.wait_ge(ag, base + t - 1)
                    carry(5 + s)
                    V.bn_stats(stats[s][:, :], hs(t)).then_inc(st, 1)

                def aggr(t, s):
                    if later(t, 2):
                        dve.wait_ge(rs, base + t - 1)
                        dve.wait_ge(n1, base + t - 1)
                    dve.wait_ge(st, base + t + 1)
                    carry(s)
                    V.bn_aggr(mv[s][:, :], stats[s][:, :]).then_inc(ag, 1)

                def norm(t, s):
                    dve.wait_ge(rs, base + t + 1)
                    if later(t, 2):
                        if L == 0:
                            dve.wait_ge(hx, t - 1)
                            dve.wait_ge(f0, t - 1)
                        else:
                            dve.wait_ge(td, base + t - 1)
                            dve.wait_ge(kept, base + t - 1)
                    V.tensor_scalar(xo[s], hs(t), mv[s][:, 0:1], rstd[s][:, :],
                                    ALU.subtract, ALU.mult).then_inc(n1, 1)

                def stat2(t, s):
                    dve.wait_ge(n1, t + 1)
                    V.bn_stats(stats2[s][:, :], x1[s]).then_inc(st2, 1)

                def aggr2(t, s):
                    if later(t, 2):
                        dve.wait_ge(rs2, t - 1)
                    dve.wait_ge(st2, t + 1)
                    carry(2 + s)
                    V.bn_aggr(mv2[s][:, :], stats2[s][:, :]).then_inc(ag2, 1)

                def affine0(t, s):
                    if later(t, 1):
                        dve.wait_ge(f1, t)
                    dve.wait_ge(rs2, t + 1)
                    V.scalar_tensor_tensor(tmp, x1[s], mv2[s][:, 0:1], rows_sb[:, 2, :],
                                           ALU.subtract, ALU.mult).then_inc(f0, 1)

                def affine1(t, s):
                    dve.wait_ge(f0, t + 1)
                    if later(t, 2):
                        dve.wait_ge(td, t - 1)
                        dve.wait_ge(kept, t - 1)
                    V.scalar_tensor_tensor(xg[s], tmp, rstd2[s][:, :], rows_sb[:, 3, :],
                                           ALU.mult, ALU.add).then_inc(f1, 1)

                def body(t, s, k):
                    if L == 0 and exists(t, NT):
                        affine0(t, s)
                    if exists(t + 3, NT):
                        aggr(t + 3, 1 - s)
                    if exists(t + 2, NT):
                        norm(t + 2, s)
                    if L == 0 and exists(t, NT):
                        affine1(t, s)
                    if L == 0 and exists(t + 2, NT):
                        stat2(t + 2, s)
                    if exists(t + 4, NT):
                        stat(t + 4, s)
                    if L == 0 and exists(t + 2, NT):
                        aggr2(t + 2, s)
                paired(dve, NT, 5, project["vector"], body, early=4, swap=True)

            @part("gpsimd")
            def _(pool):
                def root(t, s):
                    pool.wait_ge(ag, base + t + 1)
                    P.tensor_tensor(veps[s][:, :], mv[s][:, 1:2], epsv[:, :], ALU.add).then_inc(ve, 1)
                    pool.wait_ge(ve, base + t + 1)
                    if later(t, 2):
                        pool.wait_ge(n1, base + t - 1)
                    P.tensor_tensor(rstd[s][:, :], veps[s][:, :], halfneg[:, :], ALU.pow).then_inc(rs, 1)

                def root2(t, s):
                    pool.wait_ge(ag2, t + 1)
                    P.tensor_tensor(veps2[s][:, :], mv2[s][:, 1:2], epsv[:, :], ALU.add).then_inc(ve2, 1)
                    pool.wait_ge(ve2, t + 1)
                    if later(t, 2):
                        pool.wait_ge(f1, t - 1)
                    P.tensor_tensor(rstd2[s][:, :], veps2[s][:, :], halfneg[:, :], ALU.pow).then_inc(rs2, 1)

                def add(t, s):
                    pool.wait_ge(n1, t + 1)
                    P.tensor_tensor(hs(t), hs(t), x1[s], ALU.add).then_inc(hx, 1)

                def body(t, s, k):
                    if L == 0 and exists(t + 1, NT):
                        add(t + 1, 1 - s)
                    if exists(t + 3, NT):
                        root(t + 3, 1 - s)
                    if L == 0 and exists(t + 2, NT):
                        root2(t + 2, s)
                paired(pool, NT, 5, project["gpsimd"], body, early=3)

            @part("scalar")
            def _(act):
                def lcopy(t, s):
                    act.wait_ge(lg, base + t + 1)
                    A.activation(logits[:, ds(t, 1), :].rearrange("p a e -> p (a e)"), lb[s][0:W, 0:E],
                                 ACT.Copy).then_inc(lge, 1)

                def body(t, s, k):
                    act.wait_ge(rows_ready, fbase + t + 1)
                    A.activation(scr[:, ds(t * SCR, D)], xg[s], ACT.Copy).then_inc(kept, 1)
                    act.wait_ge(td, base + t + 1)
                    if later(t, 2):
                        act.wait_ge(lg, base + t - 1)
                    A.activation(xT[s], tb[s][:, 0:2 * W], ACT.Copy).then_inc(te, 1)
                    if later(t, 1):
                        lcopy(t - 1, 1 - s)
                paired(act, NT, 5, project["scalar"], body, ahead=2)
                lcopy(NT - 1, (NT - 1) % 2)

            @part("tensor")
            def _(pe):
                def prod(t, s):
                    pe.wait_ge(te, base + t + 1)
                    if later(t, 2):
                        pe.wait_ge(lge, base + t - 1)
                    for c in range(2):
                        mm = T.matmul(lb[s][0:W, 0:E], xT[s][:, c * W:(c + 1) * W], router_sb[:, c, L, :],
                                      start=c == 0, stop=c == 1)
                    mm.then_inc(lg, 1)

                def body(t, s, k):
                    pe.wait_ge(rows_ready, fbase + t + 1)
                    if later(t, 2):
                        pe.wait_ge(te, base + t - 1)
                    for c in range(2):
                        mm = T.transpose(tb[s][:, c * W:(c + 1) * W], xg[s][:, c * 128:(c + 1) * 128],
                                         ident_sb[0:W, 0:W])
                    mm.then_inc(td, 1)
                    if later(t, 1):
                        prod(t - 1, 1 - s)
                paired(pe, NT, 5, project["tensor"], body, ahead=1)
                prod(NT - 1, (NT - 1) % 2)

            step = shared("choice_step")
            steps = choice_steps
            to_act, from_act = shared("choice_to_act"), shared("choice_from_act")
            take = area(CHOICE)
            n3 = lambda a: a.rearrange("p (t e) -> p t e", e=E)
            p_, u_, oh, oh2, top, idf = (take(W, NT * E) for _ in range(6))
            idx = take(W, NT * E).bitcast(u32)
            r_ = take(W, NT)
            over_t = lambda a: a.unsqueeze(2).broadcast_to([W, NT, E])

            @part("scalar")
            def _(act):
                if L == 1:
                    first_rows[0](act)
                act.wait_ge(to_act, L + 1)
                A.activation(u_, p_ if L == 0 else logits[:, :, :].rearrange("p t e -> p (t e)"),
                             ACT.Exp if L == 0 else ACT.Sigmoid).then_inc(from_act, 1)

            def link(dve, ins):
                steps[0] += 1
                ins.then_inc(step, 1)
                dve.wait_ge(step, steps[0])

            @part("vector")
            def _(dve):
                dve.wait_ge(lge, base + NT)
                if L == 0:
                    lo = logits[:, :, :].rearrange("p t e -> p (t e)")
                    link(dve, V.tensor_scalar(p_, lo, 1e4, -1e4, ALU.min, ALU.max))
                    link(dve, V.tensor_reduce(r_, n3(p_), AX.X, ALU.max))
                    V.tensor_tensor(n3(p_), n3(p_), over_t(r_), ALU.subtract).then_inc(to_act, 1)
                    dve.wait_ge(from_act, L + 1)
                    link(dve, V.tensor_reduce(r_, n3(u_), AX.X, ALU.add))
                    link(dve, V.tensor_scalar(r_, r_, 1e-8, None, ALU.add))
                    link(dve, V.reciprocal(r_, r_))
                    link(dve, V.tensor_tensor(n3(p_), n3(u_), over_t(r_), ALU.mult))
                    link(dve, V.tensor_scalar(p_, p_, 1e-8, 1.0, ALU.max, ALU.min))
                else:
                    V.memset(r_, 0.0).then_inc(to_act, 1)
                    dve.wait_ge(from_act, L + 1)
                    link(dve, V.tensor_tensor(n3(p_), n3(u_), rbias_sb[:, :].unsqueeze(1).broadcast_to([W, NT, E]),
                                              ALU.add))
                for t in range(NT):
                    ins = V.max(n3(top)[:, t, :], n3(p_)[:, t, :])
                link(dve, ins)
                for t in range(NT):
                    ins = V.max_index(n3(idx)[:, t, :], n3(top)[:, t, :], n3(p_)[:, t, :])
                link(dve, ins)
                link(dve, V.tensor_copy(idf, idx))
                for c, o in ((0, oh), (1, oh2)):
                    ins = V.tensor_tensor(n3(o), iota_sb[0:W, 0:E].unsqueeze(1).broadcast_to([W, NT, E]),
                                          n3(idf)[:, :, c].unsqueeze(2).broadcast_to([W, NT, E]), ALU.is_equal)
                link(dve, ins)

            if L == 1:
                @part("vector")
                def _(dve):
                    link(dve, V.tensor_tensor(oh, oh, oh2, ALU.add))
                    link(dve, V.tensor_tensor(oh, oh, u_, ALU.mult))
                    link(dve, V.tensor_reduce(r_, n3(oh), AX.X, ALU.add))
                    link(dve, V.tensor_scalar(r_, r_, 1e-9, None, ALU.add))
                    link(dve, V.reciprocal(r_, r_))
                    link(dve, V.tensor_tensor(cw[:, :, :], n3(oh), over_t(r_), ALU.mult))
                    V.tensor_tensor(skipw[:, :], cw[:, :, E1], cw[:, :, E1 + 2], ALU.add).then_inc(n_over, 1)
                return

            ohs = take(W, NT * E).bitcast(bf16)[:, 0:NT * E]
            cnt, ntl, cum, start = (take(128, E) for _ in range(4))
            cmp_ = take(128, E * MAXT)
            cc = take(128, E * E)
            te_c = take(1, NS * E)
            te_f = take(1, NS)
            pos = take(W, NK)
            pos_i = take(W, NK).bitcast(i32)
            part_i = take(W, 2 * NK).bitcast(i32)
            part_f = take(W, 2 * NK)
            take = area(0)
            slot_oh = take(W, NK * SLOT // 2).bitcast(bf16)
            tile_oh = take(W, NK * NS)
            marks = take(W, NK * 3 * NS // 2).bitcast(bf16)
            origin = take(128, 3 * NS)
            row1, row, moved, real = (take(128, NS) for _ in range(4))
            chosen, ranked, slots0, slots1, marked, pool_marked, found = (
                sem(x) for x in ("chosen", "ranked", "slots0", "slots1", "marked", "pool_marked", "found"))
            slots = (slots0, slots1)
            rank_b, count_b, origin_b = bank[0], bank[1], bank[2]

            @part("sync")
            def _(sp):
                def keep(t, s, k):
                    sp.wait_ge(kept, t + 1)
                    sp.dma_start(xn_d[ds(t * W, W), 0:D], scr[:, ds(t * SCR, D)]).then_inc(rows_out, 16)
                over(sp, NT, keep, head=2)
                sp.wait_ge(chosen, 1)
                sp.dma_start(xn_d[:, D:D + 2].rearrange("(t p) g -> p t g", p=W),
                             n3(top)[:, :, 0:2]).then_inc(rows_out, 16)

            @part("tensor")
            def _(pe):
                pe.wait_ge(chosen, 1)
                T.matmul(rank_b[0:W, 0:NT * E], tri_bf[:, :], ohs, start=True, stop=False,
                         skip_group_check=True)
                for t in range(NT - 1):
                    m = NT - 1 - t
                    T.matmul(rank_b[0:W, (t + 1) * E:NT * E], ones_bf[:, 0:W],
                             n3(ohs)[:, t, :].unsqueeze(1).broadcast_to([W, m, E]),
                             start=False, stop=t == NT - 2, skip_group_check=True)
                T.matmul(count_b[:, 0:NT * E], ones_bf[:, :], ohs, start=True, stop=True).then_inc(ranked, 1)
                pe.wait_ge(marked, 1)
                pe.wait_ge(pool_marked, 1)
                for k in range(NK):
                    if k % NT == 0:
                        pe.wait_ge(slots[k // NT], 1)
                    mm = T.matmul(origin_b[:, 0:3 * NS], slot_oh[:, k * SLOT:(k + 1) * SLOT],
                                  marks[:, k * 3 * NS:(k + 1) * 3 * NS], start=k == 0, stop=k == NK - 1)
                mm.then_inc(found, 1)

            def slot_marks(c):
                o3 = slot_oh.rearrange("p (k m) -> p k m", m=SLOT)[:, c * NT:(c + 1) * NT, :]
                V.tensor_tensor(
                    o3, iota_sb[0:W, :].unsqueeze(1).broadcast_to([W, NT, SLOT]),
                    part_f[:, NK + c * NT:NK + (c + 1) * NT].unsqueeze(2).broadcast_to([W, NT, SLOT]),
                    ALU.is_equal).then_inc(slots[c], 1)

            @part("gpsimd")
            def _(pool):
                m4 = marks.rearrange("p (k g i) -> p k g i", g=3, i=NS)
                t3 = tile_oh.rearrange("p (k i) -> p k i", i=NS)
                pool.wait_ge(chosen, 1)
                pool.wait_ge(hx, NT)
                P.memset(m4[:, NT:NK, 2, :], 0.0)
                pool.wait_ge(placed, 1)
                P.tensor_tensor(m4[:, :, 1, :], t3, pair_tile_sb[:, :].unsqueeze(2).broadcast_to([W, NK, NS]),
                                ALU.mult).then_inc(pool_marked, 1)

            @part("vector")
            def _(dve):
                for o in (oh, oh2):
                    ins = V.tensor_scalar(n3(o)[:, NT - 1, :], n3(o)[:, NT - 1, :], imgmask_sb[:, G:G + 1],
                                          None, ALU.mult)
                link(dve, ins)
                V.tensor_tensor(ohs, oh, oh2, ALU.add).then_inc(chosen, 1)
                dve.wait_ge(ranked, 1)
                dve.wait_ge(hx, NT)
                link(dve, V.tensor_reduce(cnt, count_b[:, 0:NT * E].rearrange("p (t e) -> p e t", e=E),
                                          AX.X, ALU.add))
                c3 = cmp_.rearrange("p (e j) -> p e j", e=E)
                link(dve, V.tensor_tensor(c3, cnt.unsqueeze(2).broadcast_to([128, E, MAXT]),
                                          thr_sb[:, :].unsqueeze(1).broadcast_to([128, E, MAXT]), ALU.is_gt))
                link(dve, V.tensor_reduce(ntl, c3, AX.X, ALU.add))
                k3 = cc.rearrange("p (e j) -> p e j", e=E)
                link(dve, V.tensor_tensor(k3, ntl.unsqueeze(1).broadcast_to([128, E, E]),
                                          cumtri_sb[:, :].rearrange("p (e j) -> p e j", e=E), ALU.mult))
                link(dve, V.tensor_reduce(cum, k3, AX.X, ALU.add))
                link(dve, V.tensor_tensor(start, cum, ntl, ALU.subtract))
                link(dve, V.tensor_scalar(start, start, float(SLOT), None, ALU.mult))
                link(dve, V.tensor_tensor(n3(p_), n3(rank_b[0:W, 0:NT * E]),
                                          start[0:W, :].unsqueeze(1).broadcast_to([W, NT, E]), ALU.add))
                for o in (oh, oh2):
                    ins = V.tensor_tensor(o, o, p_, ALU.mult)
                link(dve, ins)
                for c, o in ((0, oh), (1, oh2)):
                    ins = V.tensor_reduce(pos[:, c * NT:(c + 1) * NT], n3(o), AX.X, ALU.add)
                link(dve, ins)
                link(dve, V.tensor_copy(pos_i, pos))
                V.tensor_scalar(part_i[:, 0:NK], pos_i, SLOT.bit_length() - 1, None, ALU.logical_shift_right)
                link(dve, V.tensor_scalar(part_i[:, NK:2 * NK], pos_i, SLOT - 1, None, ALU.bitwise_and))
                link(dve, V.tensor_copy(part_f, part_i))
                t3 = tile_oh.rearrange("p (k i) -> p k i", i=NS)
                link(dve, V.tensor_tensor(t3, iota_sb[0:W, 0:NS].unsqueeze(1).broadcast_to([W, NK, NS]),
                                          part_f[:, 0:NK].unsqueeze(2).broadcast_to([W, NK, NS]), ALU.is_equal))
                for c in range(2):
                    o = t3[:, (c + 1) * NT - 1, :]
                    ins = V.tensor_scalar(o, o, imgmask_sb[:, G:G + 1], None, ALU.mult)
                ins.then_inc(placed, 1)
                dve.wait_ge(placed, 1)
                m4 = marks.rearrange("p (k g i) -> p k g i", g=3, i=NS)
                V.tensor_scalar(m4[:, :, 0, :], t3, imgmask_sb[:, G + 1:G + 2], None, ALU.mult)
                V.tensor_copy(m4[:, 0:NT, 2, :], t3[:, 0:NT, :]).then_inc(marked, 1)
                slot_marks(0)
                slot_marks(1)
                e3 = te_c.rearrange("p (i e) -> p i e", e=E)
                link(dve, V.tensor_tensor(e3, cum[0:1, :].unsqueeze(1).broadcast_to([1, NS, E]),
                                          iota_sb[0:1, 0:NS].unsqueeze(2).broadcast_to([1, NS, E]), ALU.is_le))
                link(dve, V.tensor_reduce(te_f, e3, AX.X, ALU.add))
                link(dve, V.tensor_scalar(te_f, te_f, float(E - 1), None, ALU.min))
                link(dve, V.tensor_copy(tile_expert[:, :], te_f))
                dve.wait_ge(found, 1)
                link(dve, V.tensor_copy(origin, origin_b[:, 0:3 * NS]))
                o1, ot_, of = (origin[:, g * NS:(g + 1) * NS] for g in range(3))
                link(dve, V.scalar_tensor_tensor(row1, ot_, float(W), o1, ALU.mult, ALU.add))
                link(dve, V.tensor_scalar(row, row1, -1.0, 0.0, ALU.add, ALU.max))
                V.tensor_copy(src_u[:, :], row).then_inc(indexed, 1)
                V.tensor_copy(first[:, :], of)
                V.tensor_scalar(real, o1, 1.0, None, ALU.min)
                link(dve, V.scalar_tensor_tensor(moved, of, -float(NT * W), row1, ALU.mult, ALU.add))
                link(dve, V.tensor_tensor(moved, moved, padding_sb[:, 0, :], ALU.add))
                link(dve, V.tensor_tensor(moved, moved, real, ALU.mult))
                link(dve, V.tensor_tensor(moved, moved, padding_sb[:, 1, :], ALU.add))
                V.tensor_copy(dst_u[:, :], moved).then_inc(n_over, 1)

        def experts(L, n, rows_, begin):
            S_ = lambda x: sem(f"{x}_{L}")
            R = rows_
            take = area(0, CHOICE)
            xin = [take(R, D + 2) for _ in range(2)]
            xT = [take(128, 2 * R) for _ in range(2)]
            sg = take(R, FF)
            hid = take(R, FF)
            hT = take(128, 4 * R)
            yv = [take(R, D) for _ in range(2)]
            gd, ud, t2, td, m2, te, sd, he, hd, yd = (
                S_(x) for x in ("e_gate", "e_up", "e_hidT", "e_turned", "e_down", "e_xT", "e_silu",
                                "e_hidT_copied", "e_hid", "e_y"))
            xb, gb, ub, hb, yb, cb = bank[0:2], bank[2], bank[3], bank[4], bank[5], bank[6]
            if L == 0:
                gate = [take(R, 1) for _ in range(2)]
                gated = S_("e_gated")
                xi = [S_(f"e_x{s}") for s in range(2)]
                ys = [S_(f"e_stored{s}") for s in range(2)]
            else:
                xf = S_("e_x")
                conv_acc = [take(128, 2 * W) for _ in range(2)]
                conv_tmp = take(128, 2 * W)
                rl = [take(W, D) for _ in range(2)]
                sk = [take(W, D) for _ in range(2)]
                cv0, cvs, cvd, cvt, rls, sks, sms, yc = (
                    S_(x) for x in ("e_tap", "e_conv_step", "e_conv", "e_conv_turned", "e_relu", "e_skip",
                                    "e_sum", "e_conv_added"))
                ys = [S_(f"e_stored{s}") for s in range(2)]

            def stored(eng, i, s):
                eng.wait_ge(ys[s], 16 * (i // 2) if isinstance(i, int) else (i - s) * 8)

            if L == 0:
                @part("gpsimd")
                def _(pool):
                    pool.wait_ge(indexed, 1)
                    pool.wait_ge(rows_out, 16 * (NT + 1))

                    def load(i, s):
                        if i >= 2:
                            pool.wait_ge(td, i - 1)
                            pool.wait_ge(gated, i - 1)
                        pool.indirect_dma_start(
                            xin[s], None, xn_d[:, :],
                            bass.IndirectOffsetOnAxis(src_u[:, i:i + 1], 0)).then_inc(xi[s], 16)

                    def put(i, s):
                        pool.wait_ge(yd, i + 1)
                        pool.indirect_dma_start(
                            ys_d[:, :], bass.IndirectOffsetOnAxis(dst_u[:, i:i + 1], 0),
                            yv[s], None).then_inc(ys[s], 16)
                    load(0, 0)
                    load(1, 1)
                    begin(pool)
                    for i in range(n):
                        if i + 2 < n:
                            load(i + 2, i % 2)
                        if i >= 1:
                            put(i - 1, (i - 1) % 2)
                    put(n - 1, (n - 1) % 2)
            else:
                @part("sync")
                def _(sp):
                    def put(i, s, k):
                        sp.wait_ge(yd, i + 1)
                        sp.dma_start(out[ds(i * R, R), :], yv[s]).then_inc(ys[s], 16)
                    over(sp, n - 1, put, head=2)
                    sp.wait_ge(yd, n)
                    sp.dma_start(out[(n - 1) * W:B * Q, :], yv[(n - 1) % 2][0:WL, :]).then_inc(ys[(n - 1) % 2], 16)
                    for s in range(2):
                        sp.wait_ge(ys[s], 16 * ((n + 1 - s) // 2))

            def row_steps(act):
                def fix(t, s):
                    if later(t, 2):
                        act.wait_ge(td, t - 1)
                    A.activation(xin[s][:, 0:D], scr[:, ds(t * SCR, D)], ACT.Copy).then_inc(xf, 1)

                def turn(i, s):
                    act.wait_ge(td, i + 1)
                    if later(i, 2):
                        act.wait_ge(ud, i - 1)
                        if L == 1:
                            act.wait_ge(cvd, i - 1)
                    A.activation(xT[s], xb[s][:, 0:2 * R], ACT.Copy).then_inc(te, 1)

                return fix, turn

            if L == 1:
                @first_rows.append
                def _(act):
                    fix, turn = row_steps(act)
                    begin(act)
                    fix(0, 0)
                    fix(1, 1)
                    turn(0, 0)

            @part("scalar")
            def _(act):
                fix, turn = row_steps(act)
                if L == 0:
                    begin(act)
                    turn(0, 0)

                def hid_turn(i):
                    act.wait_ge(t2, i + 1)
                    if later(i, 1):
                        act.wait_ge(m2, i)
                    A.activation(hT, hb[:, 0:4 * R], ACT.Copy).then_inc(he, 1)
                def body(i, s, k):
                    if L == 1:
                        if exists(i + 2, n):
                            fix(i + 2, s)
                        act.wait_ge(te, i + 1)
                        if later(i, 2):
                            act.wait_ge(m2, i - 1)
                        for c in range(2):
                            ins = A.activation(conv_acc[s][:, c * W:(c + 1) * W], xT[s][:, c * W:(c + 1) * W],
                                               ACT.Identity, bias=conv_sb[:, c, KC:KC + 1],
                                               scale=conv_sb[:, c, KC - 1:KC])
                        ins.then_inc(cv0, 1)
                    if later(i, 1):
                        hid_turn(i - 1)
                    act.wait_ge(gd, i + 1)
                    if later(i, 1):
                        act.wait_ge(hd, i)
                    if L == 0:
                        act.wait_ge(gated, i + 1)
                        A.activation(sg, gb[0:R, :], ACT.Silu, scale=gate[s]).then_inc(sd, 1)
                    else:
                        A.activation(sg, gb[0:R, :], ACT.Silu).then_inc(sd, 1)
                    if exists(i + 1, n):
                        turn(i + 1, 1 - s)
                over(act, n, body, head=2, tail=2)
                hid_turn(n - 1)

            @part("vector")
            def _(dve):
                begin(dve)
                if L == 1:
                    dve.wait_ge(routed1, 1)

                def result(i, s):
                    if later(i, 2):
                        stored(dve, i, s)
                    if L == 1:
                        dve.wait_ge(sms, i + 1)
                        dve.wait_ge(cvt, i + 1)
                        V.tensor_tensor(yv[s], sk[s], cb[0:R, 0:D], ALU.add).then_inc(yc, 1)
                        dve.wait_ge(yc, i + 1)
                    dve.wait_ge(m2, i + 1)
                    if L == 0:
                        V.tensor_copy(yv[s], yb[0:R, 0:D]).then_inc(yd, 1)
                    else:
                        V.tensor_tensor(yv[s], yv[s], yb[0:R, 0:D], ALU.add).then_inc(yd, 1)

                def body(i, s, k):
                    if L == 1:
                        x = scr[:, ds(i * SCR, D)]
                        cwf = cw[:, :, :].rearrange("p t e -> p (t e)")
                        if later(i, 2):
                            dve.wait_ge(sms, i - 1)
                        V.tensor_scalar(rl[s], x, 0.0, cwf[:, ds(i * E + E1 + 3, 1)],
                                        ALU.max, ALU.mult).then_inc(rls, 1)
                        if later(i, 2):
                            dve.wait_ge(yd, i - 1)
                        V.scalar_tensor_tensor(sk[s], x, skipw[:, ds(i, 1)], hs(i),
                                               ALU.mult, ALU.add).then_inc(sks, 1)
                    if L == 0:
                        dve.wait_ge(xi[s], (i - s) * 8 + 16)
                        if later(i, 2):
                            dve.wait_ge(sd, i - 1)
                            dve.wait_ge(hd, i - 1)
                        V.scalar_tensor_tensor(gate[s], xin[s][:, D:D + 1], first[:, ds(i, 1)],
                                               xin[s][:, D + 1:D + 2], ALU.mult, ALU.max).then_inc(gated, 1)
                        dve.wait_ge(gated, i + 1)
                    dve.wait_ge(ud, i + 1)
                    dve.wait_ge(sd, i + 1)
                    if later(i, 1):
                        dve.wait_ge(t2, i)
                    if L == 0:
                        V.scalar_tensor_tensor(hid, ub[0:R, :], gate[s], sg, ALU.mult, ALU.mult).then_inc(hd, 1)
                    else:
                        for e in range(E1):
                            c_ = slice(e * I1, (e + 1) * I1)
                            ins = V.scalar_tensor_tensor(hid[:, c_], sg[:, c_], cwf[:, ds(i * E + e, 1)],
                                                         ub[0:R, c_], ALU.mult, ALU.mult)
                        ins.then_inc(hd, 1)
                    if later(i, 1):
                        result(i - 1, 1 - s)
                over(dve, n, body, head=2)
                result(n - 1, (n - 1) % 2)

            if L == 1:
                @part("gpsimd")
                def _(pool):
                    begin(pool)

                    def body(t, s, k):
                        x4 = xT[s].rearrange("p (c b q) -> p c b q", c=2, b=G)
                        a4 = conv_acc[s].rearrange("p (c b q) -> p c b q", c=2, b=G)
                        m4 = conv_tmp.rearrange("p (c b q) -> p c b q", c=2, b=G)
                        pool.wait_ge(cv0, t + 1)
                        for j in range(1, KC):
                            ins = None
                            for c in range(2):
                                ins = P.tensor_tensor(
                                    m4[:, c, :, 0:Q - j], x4[:, c, :, 0:Q - j],
                                    conv_sb[:, c, KC - 1 - j:KC - j].unsqueeze(2).broadcast_to([128, G, Q - j]),
                                    ALU.mult)
                            ins.then_inc(cvs, 1)
                            pool.wait_ge(cvs, (KC - 1) * 2 * t + 2 * j - 1)
                            for c in range(2):
                                ins = P.tensor_tensor(a4[:, c, :, j:Q], a4[:, c, :, j:Q], m4[:, c, :, 0:Q - j],
                                                      ALU.add)
                            if j < KC - 1:
                                ins.then_inc(cvs, 1)
                                pool.wait_ge(cvs, (KC - 1) * 2 * t + 2 * j)
                        ins.then_inc(cvd, 1)
                        pool.wait_ge(cvd, t + 1)
                        pool.sem_inc(cvs)
                        pool.wait_ge(rls, t + 1)
                        pool.wait_ge(sks, t + 1)
                        P.tensor_tensor(sk[s], sk[s], rl[s], ALU.add).then_inc(sms, 1)
                    over(pool, n, body, head=2)

            @part("tensor")
            def _(pe):
                begin(pe)

                def expert(i):
                    if L == 1:
                        return 0
                    return pe.value_load(tile_expert[0:1, ds(i, 1)], min_val=0, max_val=E - 1)
                gu = w_gu[:, :, :].rearrange("p e n -> p (e n)")
                dn = w_dn[:, :, :].rearrange("p e n -> p (e n)")

                def turn(i, s):
                    if L == 0:
                        pe.wait_ge(xi[s], (i - s) * 8 + 16)
                    else:
                        pe.wait_ge(xf, i + 1)
                    if later(i, 2):
                        pe.wait_ge(te, i - 1)
                    for c in range(2):
                        mm = T.transpose(xb[s][:, c * R:(c + 1) * R], xin[s][:, c * 128:(c + 1) * 128],
                                         ident_sb[0:R, 0:R])
                    mm.then_inc(td, 1)

                def wide(i, s, e, b_, o, done):
                    for c in range(2):
                        mm = T.matmul(b_[0:R, :], xT[s][:, c * R:(c + 1) * R],
                                      gu[:, ds(e * (4 * FF) + c * 2 * FF + o, FF)], start=c == 0, stop=c == 1)
                    mm.then_inc(done, 1)

                def hid_turn(i):
                    pe.wait_ge(hd, i + 1)
                    if later(i, 1):
                        pe.wait_ge(he, i)
                    for c in range(4):
                        mm = T.transpose(hb[:, c * R:(c + 1) * R], hid[:, c * 128:(c + 1) * 128],
                                         ident_sb[0:R, 0:R])
                    mm.then_inc(t2, 1)

                def down_(i, s, e):
                    pe.wait_ge(he, i + 1)
                    if later(i, 1):
                        pe.wait_ge(yd, i)
                    if L == 1:
                        pe.wait_ge(cvd, i + 1)
                        for c in range(2):
                            mm = T.transpose(cb[0:R, c * 128:(c + 1) * 128], conv_acc[s][:, c * W:(c + 1) * W],
                                             ident_sb[:, :])
                        mm.then_inc(cvt, 1)
                    for c in range(4):
                        mm = T.matmul(yb[0:R, 0:D], hT[:, c * R:(c + 1) * R], dn[:, ds(e * (4 * D) + c * D, D)],
                                      start=c == 0, stop=c == 3)
                    mm.then_inc(m2, 1)
                turn(0, 0)

                def body(i, s, e_last, e):
                    pe.wait_ge(te, i + 1)
                    if later(i, 1):
                        pe.wait_ge(sd, i)
                    wide(i, s, e, gb, 0, gd)
                    if later(i, 1):
                        hid_turn(i - 1)
                    wide(i, s, e, ub, FF, ud)
                    if exists(i + 1, n):
                        turn(i + 1, 1 - s)
                    if later(i, 1):
                        down_(i - 1, 1 - s, e_last)
                e_last = None
                for i in range(2):
                    e = expert(i)
                    body(i, i, e_last, e)
                    e_last = e
                step_ = 4
                trips = (n - 3) // step_
                with pe.Fori(0, trips) as j:
                    e_last = expert(j * step_ + 1)
                    for u in range(step_):
                        e = expert(j * step_ + (2 + u))
                        body(j * step_ + (2 + u), u % 2, e_last, e)
                        e_last = e
                e_last = expert(2 + trips * step_ - 1)
                for i in range(2 + trips * step_, n):
                    e = expert(i)
                    body(i, i % 2, e_last, e)
                    e_last = e
                hid_turn(n - 1)
                down_(n - 1, (n - 1) % 2, e_last)
            return m2, ys

        indexed = sem("indexed")
        placed = sem("placed")
        rows_out = sem("rows_out")
        routed0, routed1 = sem("routed0"), sem("routed1")
        choice_steps = [0]
        route(0, h_att0, routed0)

        def sorted_ready(eng):
            eng.wait_ge(routed0, 1)
            eng.wait_ge(both_layers["r_added"], NT)
            eng.wait_ge(experts_in, 16 * 2 * EARLY)
            eng.wait_ge(late_experts_in, 16 * 2 * (E - EARLY))

        @part("sync")
        def _(sp):
            sp.wait_ge(both_layers["d_proj"], NT)
            sp.dma_start(wqkv_sb[:, :, :], wqkv[1]).then_inc(attw_in[1], 16)
            sp.dma_start(wo_sb[:, :, :], wo[1]).then_inc(attw_in[1], 16)

        down_done0, stored0 = experts(0, NS, SLOT, sorted_ready)

        def outputs_stored(eng):
            for s in range(2):
                eng.wait_ge(stored0[s], 16 * ((NS + 1 - s) // 2))

        got_in = [sem(f"got_in{s}") for s in range(2)]
        summed, h_ffn0 = sem("summed"), sem("h_ffn0")

        @part("sync")
        def _(sp):
            outputs_stored(sp)
            y4 = ys_d[0:NK * W, :].rearrange("(c r) d -> r c d", c=2)

            def fetch(t, rows_, s):
                if later(t, 2):
                    sp.wait_ge(got_in[s], (t - s) * 8)
                sp.dma_start(scr[0:rows_, ds(t * SCR, 2 * D)].rearrange("p (c d) -> p c d", c=2),
                             y4[ds(t * W, rows_), :, :]).then_inc(got_in[s], 16)
            over(sp, NT - 1, lambda t, s, k: fetch(t, W, s), head=2)
            fetch(NT - 1, WL, (NT - 1) % 2)

        @part("sync")
        def _(sp):
            sp.wait_ge(down_done0, NS)
            sp.dma_start(w_gu[:, 0, :], gate_up1).then_inc(ffn1_in, 16)
            sp.dma_start(w_dn[:, 0, :], down1).then_inc(ffn1_in, 16)

        def combine(dve, t, s):
            r = WL if isinstance(t, int) and t == NT - 1 else W
            y = lambda c: scr[0:r, ds(t * SCR + c * D, D)]
            dve.wait_ge(got_in[s], (t - s) * 8 + 16)
            V.tensor_tensor(y(0), y(0), y(1), ALU.add).then_inc(summed, 1)
            dve.wait_ge(summed, t + 1)
            V.tensor_tensor(h[0:r, ds(t * D, D)], h[0:r, ds(t * D, D)], y(0), ALU.add).then_inc(h_ffn0, 1)

        h_att1 = sem("h_att1")
        attention(1, h_ffn0, h_att1, outputs_stored, combine)
        route(1, h_att1, routed1)

        def tokens_ready(eng):
            eng.wait_ge(both_layers["r_logits_copied"], 2 * NT)
            eng.wait_ge(both_layers["r_kept"], 2 * NT)
            eng.wait_ge(ffn1_in, 32)
        experts(1, NT, W, tokens_ready)
        finish()



def host_arrays(i):
    import numpy as np
    f = np.float32
    a = {}
    x = np.asarray(i["x"]).reshape(B, CH, SIDE, PATCH, SIDE, PATCH).transpose(0, 2, 4, 1, 3, 5)
    x = x.reshape(B, SIDE * SIDE, NF * 128)
    full = np.zeros((NT * G, Q, NF * 128), f)
    full[:B, 1:] = x
    a["patches"] = full.reshape(NT, W, NF, 128).transpose(0, 3, 2, 1).reshape(NT, 128, NF * W)
    kmaj = lambda w, c: np.asarray(w).reshape(c, 128, -1).transpose(1, 0, 2)
    a["tok_w"] = kmaj(np.asarray(i["L0_tok_W"]).T, NF).reshape(128, NF * D)
    pos = np.asarray(i["L0_tok_pos_enc"])[0]
    add = np.concatenate([np.asarray(i["L0_tok_cls_token"])[0], np.tile(np.asarray(i["L0_tok_b"])[None], (Q - 1, 1))])
    row = lambda v: np.tile(np.asarray(v)[None], (W, 1))
    a["rows"] = np.stack([np.tile(pos, (G, 1)), np.tile(add, (G, 1)), row(i["L0_ffn_ln_gamma"]),
                          row(i["L0_ffn_ln_beta"]), row(i["L1_attn_bo"])], 1)
    a["ident"] = np.eye(128, dtype=f)
    ang = np.arange(Q, dtype=f)[:, None] * (1.0 / 10000.0 ** (np.arange(0, DK, 2, dtype=f) / DK)).astype(f)
    c, s = np.cos(ang), np.sin(ang)
    a["rope"] = np.tile(np.stack([np.concatenate([c, c], 1), np.concatenate([-s, s], 1)], 1), (G, 1, 1)).astype(f)
    a["headmask"] = (np.arange(128)[:, None] // DK == np.arange(HH)[None]).astype(f)
    a["imgmask"] = np.concatenate([np.arange(W)[:, None] // Q == np.arange(G)[None],
                                   np.arange(W)[:, None] < WL, np.arange(W)[:, None] + 1], 1).astype(f)
    a["causal"] = np.tile(np.where(np.arange(Q)[None] > np.arange(Q)[:, None], f(NEG), f(0)), (1, HH)).astype(f)
    a["selq"] = (np.arange(Q)[:, None] == np.arange(128)[None] % HALF).astype(f)
    a["tri"] = (np.arange(W)[:, None] < np.arange(W)[None]).astype(f)
    a["cumtri"] = np.tile((np.arange(E)[None] <= np.arange(E)[:, None]).astype(f).reshape(1, -1), (128, 1))
    a["thresholds"] = np.tile(SLOT * np.arange(MAXT, dtype=f)[None], (128, 1))
    a["iota"] = np.tile(np.arange(SLOT, dtype=f)[None], (128, 1))
    a["pair_tile"] = np.tile(np.arange(NK, dtype=f)[None] % NT, (W, 1))
    own = NK * W + np.arange(NS)[None] * SLOT + np.arange(SLOT)[:, None]
    a["padding"] = np.stack([NT * W - 1 - own, own], 1).astype(f)
    halves = np.concatenate([np.arange(0, DK, 2), np.arange(1, DK, 2)])
    perm = (np.arange(H)[:, None] * DK + halves[None]).reshape(-1)
    wq, wk = (np.asarray(i[f"L0_attn_{n}"])[perm] for n in ("Wq", "Wk"))
    l0 = np.concatenate([wq.T, wk.T, np.asarray(i["L0_attn_Wv"]).T], 1)
    l1 = np.concatenate([np.asarray(i[f"L1_attn_{n}"]).T for n in ("Wq", "Wk", "Wv")], 1)
    a["wqkv"] = np.stack([kmaj(l0, 2), kmaj(l1, 2)])
    a["wo"] = np.stack([kmaj(np.asarray(i[f"L{l}_attn_Wo"]).T, 2) for l in range(2)])
    a["router"] = np.stack([kmaj(np.asarray(i["L0_ffn_router_w"]).T, 2), kmaj(i["L1_ffn_Wr"], 2)], 2)
    a["router_bias"] = row(i["L1_ffn_router_bias"])
    a["gate_up"] = np.stack([kmaj(w.T, 2).reshape(128, -1) for w in np.asarray(i["L0_ffn_gate_up_w"])])
    a["down"] = np.stack([kmaj(w.T, 4).reshape(128, -1) for w in np.asarray(i["L0_ffn_down_w"])])
    wg, wu = (np.asarray(i[f"L1_ffn_{n}"]).transpose(1, 0, 2).reshape(D, E1 * I1) for n in ("Wg", "Wu"))
    a["gate_up1"] = kmaj(np.concatenate([wg, wu], 1), 2).reshape(128, -1)
    a["down1"] = kmaj(np.asarray(i["L1_ffn_Wd"]).reshape(E1 * I1, D), 4).reshape(128, -1)
    cv = np.concatenate([np.asarray(i["L1_ffn_conv_w"])[:, 0], np.asarray(i["L1_ffn_conv_b"])[None]])
    a["conv"] = cv.T.reshape(2, 128, KC + 1).transpose(1, 0, 2)
    return {k: np.ascontiguousarray(v) for k, v in a.items()}


def kernel(**inputs):
    import numpy as np
    import concourse.bacc as bacc
    from concourse import mybir as mb
    from concourse.bass_utils import run_bass_kernel_spmd as run

    nc = bacc.Bacc("TRN2", target_bir_lowering=False, num_devices=1)
    arrays = host_arrays(inputs)
    args = {k: nc.dram_tensor(k, v.shape, mb.dt.from_np(v.dtype), kind="ExternalInput").ap() for k, v in arrays.items()}
    out = nc.dram_tensor("out", (B * Q, D), mb.dt.float32, kind="ExternalOutput").ap()
    build(nc, **args, out=out)
    r = run(nc, [arrays], core_ids=[0])
    return r.results[0]["out"].reshape(B, Q, D)
```
